# Optimizing a Trainium2 kernel written in Bass

```python
import numpy as np
import jax
import jax.numpy as jnp

def _softmax(x, axis=-1):
    return jax.nn.softmax(x, axis=axis)

def _gelu(x):
    return jax.nn.gelu(x, approximate=True)

def _silu(x):
    return jax.nn.silu(x)

def _sigmoid(x):
    return jax.nn.sigmoid(x)

def _layernorm(x, axis=-1, eps=1e-05):
    m = jnp.mean(x, axis=axis, keepdims=True)
    v = jnp.var(x, axis=axis, keepdims=True)
    return (x - m) / jnp.sqrt(v + eps)

def _scatter_add(tgt, idx, src, axis=0):
    return tgt.at[idx].add(src)

def _segment_sum(src, seg, n):
    return jax.ops.segment_sum(src, seg, n)
kernel_name = 'mk_flamingo_gated_d2_seqx_r4_778656'

def setup_inputs(seed: int=0):
    np.random.seed(seed)
    _w = jnp.asarray

    def _rec_inputs():
        import jax
        import jax.numpy as jnp
        _rk = jax.random.key(seed)
        x = 7.22e-05 + 1 * jax.random.normal(jax.random.fold_in(_rk, 1), (2, 1024, 256), jnp.float32)
        _lenS = 1024 - jax.random.randint(jax.random.fold_in(_rk, 7), (2,), 0, max(1, 1024 // 4) + 1, jnp.int32)
        _lenS2 = 77 - jax.random.randint(jax.random.fold_in(_rk, 8), (2,), 0, max(1, 77 // 4) + 1, jnp.int32)
        _ctx_1024P = jax.random.normal(jax.random.fold_in(_rk, 11), (2, 16, 256), jnp.float32)
        _ctx_1024c = jax.random.dirichlet(jax.random.fold_in(_rk, 511), 0.3 * jnp.ones((16,), jnp.float32), (2, 77))
        _ctx_1024t = jnp.einsum('bsk,bkd->bsd', _ctx_1024c, _ctx_1024P)
        _ctx_1024t = _ctx_1024t * jax.lax.rsqrt(jnp.mean(jnp.square(_ctx_1024t)) + 1e-12) * 0.953939
        ctx_1024 = 2.81802e-05 + 1.00001 * (_ctx_1024t + 0.3 * jax.random.normal(jax.random.fold_in(_rk, 611), (2, 77, 256), jnp.float32))
        _g = jax.random.normal(jax.random.fold_in(_rk, 9001), (2, 2), jnp.float32)
        _g = jnp.sign(_g) * jnp.maximum(jnp.abs(_g), 1.0) + (_g == 0) * 1.0
        g_xattn = _g[0]
        g_ffn = _g[1]
        return (x, ctx_1024, g_xattn, g_ffn)
    x, ctx_1024, g_xattn, g_ffn = _rec_inputs()

    def _L0_xattn_setup():
        import jax, jax.numpy as jnp
        import numpy as np
        B, NT, NM, C, H, FF = (8, 256, 512, 256, 8, 1024)

        def _ln(x, g, b):
            m = x.mean(-1, keepdims=True)
            v = jnp.mean((x - m) ** 2, axis=-1, keepdims=True)
            return (x - m) / jnp.sqrt(v + 1e-05) * g + b
        key = jax.random.key(seed)
        ks = jax.random.split(key, 8)
        w = lambda k, shape, s=0.02: jax.random.normal(k, shape, dtype=jnp.float32) * s
        return {'tgt': jax.random.normal(ks[0], (B, NT, C), dtype=jnp.float32), 'memory': jax.random.normal(ks[1], (B, NM, C), dtype=jnp.float32), 'qkv_w': w(ks[2], (3 * C, C)), 'qkv_b': jnp.zeros((3 * C,), jnp.float32), 'sa_out_w': w(ks[3], (C, C)), 'sa_out_b': jnp.zeros((C,), jnp.float32), 'in_proj_w': w(ks[4], (3 * C, C)), 'in_proj_b': jnp.zeros((3 * C,), jnp.float32), 'mha_out_w': w(ks[5], (C, C)), 'mha_out_b': jnp.zeros((C,), jnp.float32), 'lin1_w': w(ks[6], (FF, C)), 'lin1_b': jnp.zeros((FF,), jnp.float32), 'lin2_w': w(ks[7], (C, FF)), 'lin2_b': jnp.zeros((C,), jnp.float32), 'ln1_g': jnp.ones((C,), jnp.float32), 'ln1_b': jnp.zeros((C,), jnp.float32), 'ln2_g': jnp.ones((C,), jnp.float32), 'ln2_b': jnp.zeros((C,), jnp.float32), 'ln3_g': jnp.ones((C,), jnp.float32), 'ln3_b': jnp.zeros((C,), jnp.float32)}
    _L0_xattn_all = _L0_xattn_setup()
    _L0_xattn_in = {k: v for k, v in _L0_xattn_all.items() if k in ('qkv_w', 'qkv_b', 'sa_out_w', 'sa_out_b', 'in_proj_w', 'in_proj_b', 'mha_out_w', 'mha_out_b', 'lin1_w', 'lin1_b', 'lin2_w', 'lin2_b', 'ln1_g', 'ln1_b', 'ln2_g', 'ln2_b', 'ln3_g', 'ln3_b')}
    del _L0_xattn_all

    def _L0_ffn_setup():
        import jax, jax.numpy as jnp
        import numpy as np
        H = 256
        I = 128
        E = 8
        TOP_K = 2
        N_SHARED = 2
        SHARED_I = I * N_SHARED
        SCALE = 2.5
        NORM_TOPK = True
        B, S = (2, 256)

        def _swiglu(x, wg, wu, wd):
            g = x @ wg.T
            u = x @ wu.T
            return jax.nn.silu(g) * u @ wd.T
        key = jax.random.key(seed)
        ks = jax.random.split(key, 8)
        std = 0.02
        return {'hidden_states': jax.random.normal(ks[0], (B, S, H), jnp.float32), 'gate_weight': jax.random.normal(ks[1], (E, H), jnp.float32) * std, 'w_gate': jax.random.normal(ks[2], (E, I, H), jnp.float32) * std, 'w_up': jax.random.normal(ks[3], (E, I, H), jnp.float32) * std, 'w_down': jax.random.normal(ks[4], (E, H, I), jnp.float32) * std, 'ws_gate': jax.random.normal(ks[5], (SHARED_I, H), jnp.float32) * std, 'ws_up': jax.random.normal(ks[6], (SHARED_I, H), jnp.float32) * std, 'ws_down': jax.random.normal(ks[7], (H, SHARED_I), jnp.float32) * std}
    _L0_ffn_all = _L0_ffn_setup()
    _L0_ffn_in = {k: v for k, v in _L0_ffn_all.items() if k in ('gate_weight', 'w_gate', 'w_up', 'w_down', 'ws_gate', 'ws_up', 'ws_down')}
    del _L0_ffn_all

    def _L1_xattn_setup():
        import jax, jax.numpy as jnp
        import numpy as np
        B, N, M, D = (8, 512, 512, 256)
        key = jax.random.key(seed)
        k1, k2, k3, k4 = jax.random.split(key, 4)
        glorot = (2.0 / (D + D)) ** 0.5
        return {'text': jax.random.normal(k1, (B, N, D), dtype=jnp.float32), 'context': jax.random.normal(k2, (B, M, D), dtype=jnp.float32), 'We': jax.random.normal(k3, (D, D), dtype=jnp.float32) * glorot, 'W2': jax.random.normal(k4, (D, D), dtype=jnp.float32) * glorot}
    _L1_xattn_all = _L1_xattn_setup()
    _L1_xattn_in = {k: v for k, v in _L1_xattn_all.items() if k in ('We', 'W2')}
    del _L1_xattn_all

    def _L1_ffn_setup():
        import jax, jax.numpy as jnp
        import numpy as np
        DIM = 256

        def _reference_tuple_inner(x, W_r, W_k, W_v, mu_r, mu_k):
            B, T, C = x.shape
            x_prev = jnp.concatenate([jnp.zeros((B, 1, C), x.dtype), x[:, :-1, :]], axis=1)
            xr = mu_r * x + (1.0 - mu_r) * x_prev
            xk = mu_k * x + (1.0 - mu_k) * x_prev
            r = jax.nn.sigmoid(jnp.einsum('btc,dc->btd', xr, W_r))
            k = jnp.einsum('btc,dc->btd', xk, W_k)
            k_act = jnp.square(jax.nn.relu(k))
            out = r * jnp.einsum('btc,dc->btd', k_act, W_v)
            new_state = x[:, -1, :]
            return (out, new_state)
        key = jax.random.key(seed)
        ks = jax.random.split(key, 6)
        B, T, C = (8, 512, DIM)
        x = jax.random.normal(ks[0], (B, T, C), dtype=jnp.float32)
        s = 1.0 / np.sqrt(C)
        W_r = jax.random.uniform(ks[1], (C, C), jnp.float32, -s, s)
        W_k = jax.random.uniform(ks[2], (C, C), jnp.float32, -s, s)
        W_v = jax.random.uniform(ks[3], (C, C), jnp.float32, -s, s)
        mu_r = jax.random.uniform(ks[4], (C,), jnp.float32)
        mu_k = jax.random.uniform(ks[5], (C,), jnp.float32)
        return {'x': x, 'W_r': W_r, 'W_k': W_k, 'W_v': W_v, 'mu_r': mu_r, 'mu_k': mu_k}
    _L1_ffn_all = _L1_ffn_setup()
    _L1_ffn_in = {k: v for k, v in _L1_ffn_all.items() if k in ('W_r', 'W_k', 'W_v', 'mu_r', 'mu_k')}
    del _L1_ffn_all
    return {'x': x, 'ctx_1024': ctx_1024, 'g_xattn': g_xattn, 'g_ffn': g_ffn, 'L0_xattn_qkv_w': _L0_xattn_in['qkv_w'], 'L0_xattn_qkv_b': _L0_xattn_in['qkv_b'], 'L0_xattn_sa_out_w': _L0_xattn_in['sa_out_w'], 'L0_xattn_sa_out_b': _L0_xattn_in['sa_out_b'], 'L0_xattn_in_proj_w': _L0_xattn_in['in_proj_w'], 'L0_xattn_in_proj_b': _L0_xattn_in['in_proj_b'], 'L0_xattn_mha_out_w': _L0_xattn_in['mha_out_w'], 'L0_xattn_mha_out_b': _L0_xattn_in['mha_out_b'], 'L0_xattn_lin1_w': _L0_xattn_in['lin1_w'], 'L0_xattn_lin1_b': _L0_xattn_in['lin1_b'], 'L0_xattn_lin2_w': _L0_xattn_in['lin2_w'], 'L0_xattn_lin2_b': _L0_xattn_in['lin2_b'], 'L0_xattn_ln1_g': _L0_xattn_in['ln1_g'], 'L0_xattn_ln1_b': _L0_xattn_in['ln1_b'], 'L0_xattn_ln2_g': _L0_xattn_in['ln2_g'], 'L0_xattn_ln2_b': _L0_xattn_in['ln2_b'], 'L0_xattn_ln3_g': _L0_xattn_in['ln3_g'], 'L0_xattn_ln3_b': _L0_xattn_in['ln3_b'], 'L0_ffn_gate_weight': _L0_ffn_in['gate_weight'], 'L0_ffn_w_gate': _L0_ffn_in['w_gate'], 'L0_ffn_w_up': _L0_ffn_in['w_up'], 'L0_ffn_w_down': _L0_ffn_in['w_down'], 'L0_ffn_ws_gate': _L0_ffn_in['ws_gate'], 'L0_ffn_ws_up': _L0_ffn_in['ws_up'], 'L0_ffn_ws_down': _L0_ffn_in['ws_down'], 'L1_xattn_We': _L1_xattn_in['We'], 'L1_xattn_W2': _L1_xattn_in['W2'], 'L1_ffn_W_r': _L1_ffn_in['W_r'], 'L1_ffn_W_k': _L1_ffn_in['W_k'], 'L1_ffn_W_v': _L1_ffn_in['W_v'], 'L1_ffn_mu_r': _L1_ffn_in['mu_r'], 'L1_ffn_mu_k': _L1_ffn_in['mu_k']}

def reference(x, ctx_1024, g_xattn, g_ffn, L0_xattn_qkv_w, L0_xattn_qkv_b, L0_xattn_sa_out_w, L0_xattn_sa_out_b, L0_xattn_in_proj_w, L0_xattn_in_proj_b, L0_xattn_mha_out_w, L0_xattn_mha_out_b, L0_xattn_lin1_w, L0_xattn_lin1_b, L0_xattn_lin2_w, L0_xattn_lin2_b, L0_xattn_ln1_g, L0_xattn_ln1_b, L0_xattn_ln2_g, L0_xattn_ln2_b, L0_xattn_ln3_g, L0_xattn_ln3_b, L0_ffn_gate_weight, L0_ffn_w_gate, L0_ffn_w_up, L0_ffn_w_down, L0_ffn_ws_gate, L0_ffn_ws_up, L0_ffn_ws_down, L1_xattn_We, L1_xattn_W2, L1_ffn_W_r, L1_ffn_W_k, L1_ffn_W_v, L1_ffn_mu_r, L1_ffn_mu_k):
    import jax
    import jax.numpy as jnp

    def _L0_xattn_ref(tgt, memory, qkv_w, qkv_b, sa_out_w, sa_out_b, in_proj_w, in_proj_b, mha_out_w, mha_out_b, lin1_w, lin1_b, lin2_w, lin2_b, ln1_g, ln1_b, ln2_g, ln2_b, ln3_g, ln3_b):
        import jax, jax.numpy as jnp
        import numpy as np
        B, NT, NM, C, H, FF = (8, 256, 512, 256, 8, 1024)

        def _ln(x, g, b):
            m = x.mean(-1, keepdims=True)
            v = jnp.mean((x - m) ** 2, axis=-1, keepdims=True)
            return (x - m) / jnp.sqrt(v + 1e-05) * g + b
        Bx, N, Cx = tgt.shape
        qkv = tgt @ qkv_w.T + qkv_b
        q, k, v = jnp.split(qkv, 3, axis=-1)
        scores = jnp.einsum('bnc,bmc->bnm', q, k) * jnp.sqrt(jnp.float32(Cx))
        diag = jnp.eye(N, dtype=bool)
        scores = jnp.where(diag[None, :, :], scores, -jnp.inf)
        attn = jax.nn.softmax(scores, axis=-1)
        sa = jnp.einsum('bnm,bmc->bnc', attn, v) @ sa_out_w.T + sa_out_b
        x = _ln(tgt + sa, ln1_g, ln1_b)
        d = Cx // H
        wq, wk, wv = jnp.split(in_proj_w, 3, axis=0)
        bq, bk, bv = jnp.split(in_proj_b, 3, axis=0)
        qh = (x @ wq.T + bq).reshape(Bx, N, H, d).transpose(0, 2, 1, 3)
        kh = (memory @ wk.T + bk).reshape(Bx, -1, H, d).transpose(0, 2, 1, 3)
        vh = (memory @ wv.T + bv).reshape(Bx, -1, H, d).transpose(0, 2, 1, 3)
        a = jax.nn.softmax(jnp.einsum('bhnd,bhmd->bhnm', qh, kh) / jnp.sqrt(jnp.float32(d)), axis=-1)
        ca = jnp.einsum('bhnm,bhmd->bhnd', a, vh).transpose(0, 2, 1, 3).reshape(Bx, N, Cx)
        ca = ca @ mha_out_w.T + mha_out_b
        x = _ln(x + ca, ln2_g, ln2_b)
        ff = jax.nn.relu(x @ lin1_w.T + lin1_b) @ lin2_w.T + lin2_b
        return _ln(x + ff, ln3_g, ln3_b)

    def _L0_ffn_ref(hidden_states, gate_weight, w_gate, w_up, w_down, ws_gate, ws_up, ws_down):
        import jax, jax.numpy as jnp
        import numpy as np
        H = 256
        I = 128
        E = 8
        TOP_K = 2
        N_SHARED = 2
        SHARED_I = I * N_SHARED
        SCALE = 2.5
        NORM_TOPK = True
        B, S = (2, 256)

        def _swiglu(x, wg, wu, wd):
            g = x @ wg.T
            u = x @ wu.T
            return jax.nn.silu(g) * u @ wd.T
        b, s, h = hidden_states.shape
        x = hidden_states.reshape(-1, h)
        shared_out = _swiglu(x, ws_gate, ws_up, ws_down)
        logits = x.astype(jnp.float32) @ gate_weight.astype(jnp.float32).T
        scores = jax.nn.sigmoid(logits)
        topk_w, topk_idx = jax.lax.top_k(scores, TOP_K)
        if TOP_K > 1 and NORM_TOPK:
            topk_w = topk_w / (topk_w.sum(-1, keepdims=True) + 1e-20)
        topk_w = topk_w * SCALE
        onehot = jax.nn.one_hot(topk_idx, E, dtype=topk_w.dtype)
        combine = jnp.einsum('tk,tke->te', topk_w, onehot)
        g = jnp.einsum('th,eih->tei', x, w_gate)
        u = jnp.einsum('th,eih->tei', x, w_up)
        hmid = jax.nn.silu(g) * u
        y = jnp.einsum('tei,ehi->teh', hmid, w_down)
        routed_out = jnp.einsum('te,teh->th', combine, y)
        out = (routed_out + shared_out).reshape(b, s, h)
        return out

    def _L1_xattn_ref(text, context, We, W2):
        import jax, jax.numpy as jnp
        import numpy as np
        B, N, M, D = (8, 512, 512, 256)
        scores = jnp.einsum('bnd,bmd->bnm', text @ We, context)
        attn = jax.nn.softmax(scores, axis=1)
        res = jnp.einsum('bnm,bmd->bnd', attn, context)
        return res @ W2.T

    def _L1_ffn_ref(x, W_r, W_k, W_v, mu_r, mu_k):
        import jax, jax.numpy as jnp
        import numpy as np
        DIM = 256

        def _reference_tuple_inner(x, W_r, W_k, W_v, mu_r, mu_k):
            B, T, C = x.shape
            x_prev = jnp.concatenate([jnp.zeros((B, 1, C), x.dtype), x[:, :-1, :]], axis=1)
            xr = mu_r * x + (1.0 - mu_r) * x_prev
            xk = mu_k * x + (1.0 - mu_k) * x_prev
            r = jax.nn.sigmoid(jnp.einsum('btc,dc->btd', xr, W_r))
            k = jnp.einsum('btc,dc->btd', xk, W_k)
            k_act = jnp.square(jax.nn.relu(k))
            out = r * jnp.einsum('btc,dc->btd', k_act, W_v)
            new_state = x[:, -1, :]
            return (out, new_state)
        return _reference_tuple_inner(x, W_r, W_k, W_v, mu_r, mu_k)[0]
    x = x + jnp.tanh(g_xattn[0]) * _L0_xattn_ref(_layernorm(x, axis=-1), ctx_1024, L0_xattn_qkv_w, L0_xattn_qkv_b, L0_xattn_sa_out_w, L0_xattn_sa_out_b, L0_xattn_in_proj_w, L0_xattn_in_proj_b, L0_xattn_mha_out_w, L0_xattn_mha_out_b, L0_xattn_lin1_w, L0_xattn_lin1_b, L0_xattn_lin2_w, L0_xattn_lin2_b, L0_xattn_ln1_g, L0_xattn_ln1_b, L0_xattn_ln2_g, L0_xattn_ln2_b, L0_xattn_ln3_g, L0_xattn_ln3_b)
    x = x + jnp.tanh(g_ffn[0]) * _L0_ffn_ref(_layernorm(x, axis=-1), L0_ffn_gate_weight, L0_ffn_w_gate, L0_ffn_w_up, L0_ffn_w_down, L0_ffn_ws_gate, L0_ffn_ws_up, L0_ffn_ws_down)
    x = x + jnp.tanh(g_xattn[1]) * _L1_xattn_ref(_layernorm(x, axis=-1), ctx_1024, L1_xattn_We, L1_xattn_W2)
    x = x + jnp.tanh(g_ffn[1]) * _L1_ffn_ref(_layernorm(x, axis=-1), L1_ffn_W_r, L1_ffn_W_k, L1_ffn_W_v, L1_ffn_mu_r, L1_ffn_mu_k)
    return x

_drawn_inputs = setup_inputs


def setup_inputs(seed=0):
    import zlib

    import numpy as np

    out = dict(_drawn_inputs(seed))
    spreads = {'g_ffn': (-1.0, 0.6),
     'L0_xattn_qkv_b': (0.0, 0.603),
     'L0_xattn_sa_out_b': (0.0, 0.1),
     'L0_xattn_in_proj_b': (0.0, 0.521),
     'L0_xattn_mha_out_b': (0.0, 0.1),
     'L0_xattn_lin1_b': (0.0, 0.388),
     'L0_xattn_lin2_b': (0.0, 0.1),
     'L0_xattn_ln1_g': (1.0, 0.2),
     'L0_xattn_ln1_b': (0.0, 0.1),
     'L0_xattn_ln2_g': (1.0, 0.2),
     'L0_xattn_ln2_b': (0.0, 0.1),
     'L0_xattn_ln3_g': (1.0, 0.2),
     'L0_xattn_ln3_b': (0.0, 0.1)}
    factors = {'L0_ffn_gate_weight': 6.173,
     'L0_ffn_w_gate': 5.55,
     'L0_ffn_w_up': 5.457,
     'L0_ffn_w_down': 5.691,
     'L0_ffn_ws_gate': 6.693,
     'L0_ffn_ws_up': 6.694,
     'L0_ffn_ws_down': 6.794,
     'L1_ffn_W_r': 32.377,
     'L1_ffn_mu_r': 56.431,
     'L1_ffn_W_k': 3.73,
     'L1_ffn_W_v': 3.41,
     'L1_ffn_mu_k': 6.218}
    for name, (base, spread) in spreads.items():
        noise = np.random.default_rng([zlib.crc32(name.encode()), seed]).standard_normal(out[name].shape)
        drawn = base * np.exp(spread * noise) if base else spread * noise
        out[name] = jnp.asarray(drawn.astype(out[name].dtype))
    for name, factor in factors.items():
        out[name] = (out[name] * factor).astype(out[name].dtype)
    return out
```

```python
from contextlib import ExitStack

import concourse.bass as bass
from concourse import mybir

F32 = mybir.dt.float32
F32R = mybir.dt.float32r
U32 = mybir.dt.uint32
ALU = mybir.AluOpType
ACT = mybir.ActivationFunctionType
AX = mybir.AxisListType

P = 128
B, S, D = 2, 1024, 256
KC = D // P
NT = B * S // P
CH = 512
TPC = CH // P
NCH = B * S // CH
TPB = S // P
M = 77
H, DH = 8, 32
HH = H // 2
HM = HH * M
HP = 384
NQ = HP // P
FF, NF = 1024, 8
E, I = 8, 128
NU = E + 2
EPS = 1e-5
ROUTE_SCALE = 2.5

(W_V, W_SO, W_Q, W_K, W_VM, W_O, W_E, W_2) = range(8)
(C_BV, C_BK, C_BVM, C_BQ, C_G1, C_B1, C_G2, C_B2, C_MUR, C_MUK) = range(10)
NCOL = 10
(R_G1, R_G2, R_G3, R_B3) = range(4)
(BR_SO, BR_O, BR_F2, BR_B1, BR_B2) = range(5)


class Event:

    def __init__(self, sem, per=1, credit=0):
        self.sem, self.per, self.credit = sem, per, credit

    def wait(self, eng, t, k=0):
        value = self.per * t + k + 1 + self.credit
        if isinstance(value, int) and value <= self.credit:
            return
        eng.wait_ge(self.sem, value)


def build(nc, x, ctxT, gates, raw, cols, l1b, bcast, brow, w1, w2, gateT, gu, dn, rw, out):
    with ExitStack() as top:
        def sem(name):
            return top.enter_context(nc.semaphore(name))

        events = []

        def event(name, per=1, credit=0):
            events.append(Event(sem(name), per, credit))
            return events[-1]

        def sb(ctx, name, shape, dt=F32):
            return ctx.enter_context(nc.sbuf_tensor(name, shape, dt))

        def pair(ctx, name, shape):
            return sb(ctx, name + "_hi", shape, F32R), sb(ctx, name + "_lo", shape, F32R)

        with ExitStack() as setup:
            rawA = sb(setup, "rawA", [P, KC, 8 * D])
            w1raw = sb(setup, "w1raw", [P, KC, FF])
            w2raw = sb(setup, "w2raw", [P, NF, D])
        XT = pair(top, "XT", [P, KC, B * S])
        X = sb(top, "X", [P, NT, D])
        W1 = pair(top, "W1", [P, KC, FF])
        W2 = pair(top, "W2", [P, NF, D])
        hid = [pair(top, f"hid{k}", [P, CH]) for k in range(2)]
        work = [sb(top, f"work{k}", [P, CH]) for k in range(4)]
        ntile = sb(top, "ntile", [P, TPC, D])
        ztile = sb(top, "ztile", [P, TPC, D])
        bc = sb(top, "bc", [P, 4, D])
        gate_raw = sb(top, "gate_raw", [P, 4])
        tg = sb(top, "tg", [P, 4])
        col = sb(top, "col", [P, KC, NCOL])
        b1col = sb(top, "b1col", [P, NF])
        warm = sb(top, "warm", [P, 1])
        b2row = sb(top, "b2row", [33, D], F32R)
        ident = sb(top, "ident", [P, P])
        ones = sb(top, "ones", [33, P], F32R)
        ctx_sb = sb(top, "ctx_sb", [P, KC, B * M])
        Bctx = pair(top, "Bctx", [P, KC, B * M])
        C2 = sb(top, "C2", [M, B, D])
        gT_raw = sb(top, "gT_raw", [P, KC, E])
        gT = pair(top, "gT", [P, KC, P])
        cmb = sb(top, "cmb", [P, NT, E])
        moe_raw = sb(top, "moe_raw", [P, 3, D])
        stat = sb(top, "stat", [P, 8, 6])
        mv = sb(top, "mv", [P, 8, 2])
        var = sb(top, "var", [P, 8])
        rstd = sb(top, "rstd", [P, 8])
        half = sb(top, "half", [P, 8])
        iota = sb(top, "iota", [P, E])
        with ExitStack() as stage_a:
            Mt = pair(stage_a, "Mt", [P, KC, D])
            A = pair(stage_a, "A", [P, B, KC, 2, HM])
            VW = pair(stage_a, "VW", [P, B, 2 * NQ, D])
            araw = sb(stage_a, "araw", [P, KC, 2, HM])
            bias = sb(stage_a, "bias", [33, 2 * D], F32R)
            sbias = sb(stage_a, "sbias", [33, B, 2, HM], F32R)
            xt0 = pair(stage_a, "xt0", [P, KC, P])
            xt1 = pair(stage_a, "xt1", [P, KC, P])
            Pm = [sb(stage_a, f"Pm{k}", [P, 2, HP]) for k in range(2)]
            PT = pair(stage_a, "PT", [P, 2 * NQ, P])
            n0, n1, n2 = ntile[:, 0, :], (ntile[:, 1, :], ntile[:, 2, :]), (ntile[:, 3, :], ztile[:, 3, :])
            n1g, z2 = (ztile[:, 1, :], ztile[:, 2, :]), ztile[:, 0, :]
            nmr = sb(stage_a, "nmr", [P, 1])
            mx = sb(stage_a, "mx", [P, H])
            sm = sb(stage_a, "sm", [P, H])
            rc = sb(stage_a, "rc", [P, H])
        with ExitStack() as stage_c:
            GU = pair(stage_c, "GU", [P, KC, 2 * NU * I])
            DN = pair(stage_c, "DN", [P, NU, D])
            cT = pair(stage_c, "cT", [E, CH])
            cst = sb(stage_c, "cst", [P, TPC, E])
            lgT = sb(stage_c, "lgT", [P, CH])
            sel = sb(stage_c, "sel", [E, E, P], F32R)
            selraw = sb(stage_c, "selraw", [E, E, P])
            xr4 = sb(stage_c, "xr4", [P, TPC, D])
            ex = sb(stage_c, "ex", [P, TPC, E])
            sc = sb(stage_c, "sc", [P, TPC, E])
            top8 = sb(stage_c, "top8", [P, TPC, 8])
            idx8 = sb(stage_c, "idx8", [P, TPC, 8], U32)
            idxf = sb(stage_c, "idxf", [P, TPC, 8])
            tsum = sb(stage_c, "tsum", [P, TPC])
            tw = sb(stage_c, "tw", [P, TPC, 2])
            oh = sb(stage_c, "oh", [P, TPC, E])
        with ExitStack() as stage_e:
            XD = sb(stage_e, "XD", [P, KC, B * (S + 1)])
            Bst = pair(stage_e, "Bst", [P, KC, M])
            att = sb(stage_e, "att", [M, S])
            attp = pair(stage_e, "attp", [M, S])
            c2s = pair(stage_e, "c2s", [M, D])
            c2f = sb(stage_e, "c2f", [M, D])
            nmax = sb(stage_e, "nmax", [M, 1])
            asum = sb(stage_e, "asum", [M, 1])
            ascl = sb(stage_e, "ascl", [M, 1])
            dif = sb(stage_e, "dif", [P, KC, CH])
            xmix = [sb(stage_e, f"xmix{k}", [P, KC, CH]) for k in range(2)]
            xm = [pair(stage_e, f"xm{k}", [P, KC, CH]) for k in range(2)]
            ka = pair(stage_e, "ka", [P, KC, CH])
        PS = top.enter_context(nc.psum_tensor("PS", [P, 8, 512], F32))

        xv = x.rearrange("(i p) d -> p i d", p=P)
        ov = out.rearrange("(i p) d -> p i d", p=P)

        s_in = [sem(f"s_in{k}") for k in range(4)]
        s_x = sem("s_x")
        flags = {}

        def flag(name):
            if name not in flags:
                flags[name] = sem("f_" + name)
            return flags[name]

        def done(eng, name):
            eng.drain()
            eng.sem_inc(flag(name), 1)

        def need(eng, name):
            eng.wait_ge(flag(name), 1)

        block = top.enter_context(nc.Block())

        def mm3(pe, o, a, b, first, last, skip=False):
            pe.matmul(o, a[0], b[0], start=first, stop=False, skip_group_check=skip)
            pe.matmul(o, a[0], b[1], start=False, stop=False, skip_group_check=skip)
            return pe.matmul(o, a[1], b[0], start=False, stop=last, skip_group_check=skip)

        def sub(p2, *ix):
            return p2[0][ix], p2[1][ix]

        def f32(ap):
            return ap.bitcast(F32)

        a_ln0 = event("a_ln0"); a_t0 = event("a_t0"); a_h0 = event("a_h0"); a_l0 = event("a_l0")
        a_y = event("a_y"); a_v1 = event("a_v1"); a_r1 = event("a_r1"); a_n1 = event("a_n1")
        a_v0 = event("a_v0"); a_r0 = event("a_r0")
        a_t1 = event("a_t1"); a_h1 = event("a_h1"); a_l1 = event("a_l1"); a_g1 = event("a_g1")
        a_s = event("a_s"); a_mx = event("a_mx"); a_ex = event("a_ex"); a_rc = event("a_rc")
        a_p = event("a_p"); a_tp = event("a_tp"); a_hp = event("a_hp"); a_lp = event("a_lp")
        a_c = event("a_c"); a_v2 = event("a_v2"); a_r2 = event("a_r2"); a_n2 = event("a_n2")
        a_g2 = event("a_g2"); a_t2 = event("a_t2"); a_h2 = event("a_h2"); a_l2 = event("a_l2")
        a_z = event("a_z")

        def rsqrt(pool, k, n=1):
            return pool.tensor_tensor(rstd[:, k:k + n], var[:, k:k + n], half[:, 0:n], ALU.pow)

        def stats(dve, src, k, n=1):
            for j in range(n):
                dve.bn_stats(stat[:, k + j, :], src[j])
            dve.drain()
            for j in range(n):
                dve.bn_aggr(mv[:, k + j, :], stat[:, k + j, :])
            dve.drain()
            return dve.tensor_scalar(var[:, k:k + n], mv[:, k:k + n, 1], EPS, None, ALU.add)

        LAG = 4

        def a_step(pe, act, dve, pool, s, par, lo, hi):
            def on(off):
                return not isinstance(s, int) or lo <= s + off < hi

            def t(off):
                return s + off

            def q(off):
                return (par + off) % 2

            T1B, T0B, YB, SB, PB, CB = 0, 1, 2, 3, 5, 7

            def tbank(bank):
                return PS[:, bank, 0:D].rearrange("p (k t) -> p k t", k=KC)

            def x_tile(off):
                return X[:, s + off, :]

            def xt_tile(n, off):
                return XT[n][:, :, bass.ds((s + off) * P, P)]

            if pe:
                def transposes(src, bank):
                    for k in range(KC):
                        i_ = pe.transpose(PS[:, bank, k * P:(k + 1) * P], src[:, k * P:(k + 1) * P], ident[:, :])
                    return i_
                if on(-2):
                    a_n1.wait(pe, t(-2))
                    a_l2.wait(pe, t(-5))
                    transposes(n1[q(-2)], T1B).then_inc(a_t1.sem, 1)
                if on(-3):
                    a_p.wait(pe, t(-3))
                    a_lp.wait(pe, t(-4))
                    for r in range(2 * NQ):
                        j, k = r // NQ, r % NQ
                        i_ = pe.transpose(PS[:, PB + j, k * P:(k + 1) * P], Pm[q(-3)][:, j, k * P:(k + 1) * P],
                                          ident[:, :])
                    i_.then_inc(a_tp.sem, 1)
                if on(0):
                    a_ln0.wait(pe, t(0))
                    a_l0.wait(pe, t(-1))
                    transposes(n0, T0B).then_inc(a_t0.sem, 1)
                if on(-4):
                    a_n2.wait(pe, t(-4))
                    a_l1.wait(pe, t(-2) if on(-2) else NT - 1)
                    transposes(n2[q(-4)], T1B).then_inc(a_t2.sem, 1)
                if on(-1):
                    a_l0.wait(pe, t(-1))
                    a_n1.wait(pe, t(-2))
                    for k in range(KC):
                        mm3(pe, PS[:, YB, 0:D], sub(xt0, slice(None), k), sub(Mt, slice(None), k), k == 0, False)
                    pe.matmul(PS[:, YB, 0:D], ones[:, :], bias[:, 0:D], start=False, stop=True).then_inc(a_y.sem, 1)
                if on(-2):
                    a_l1.wait(pe, t(-2))
                    a_ex.wait(pe, t(-3))
                    for j in range(2):
                        for k in range(KC):
                            mm3(pe, PS[:, SB + j, 0:HM], sub(xt1, slice(None), k),
                                sub(A, slice(None), (s - 2) // TPB, k, j), k == 0, False)
                        i_ = pe.matmul(PS[:, SB + j, 0:HM], ones[:, :], sbias[:, (s - 2) // TPB, j, :], start=False, stop=True)
                    i_.then_inc(a_s.sem, 1)
                if on(-3):
                    a_lp.wait(pe, t(-3))
                    a_z.wait(pe, t(-4))
                    for r in range(2 * NQ):
                        mm3(pe, PS[:, CB, 0:D], sub(PT, slice(None), r), sub(VW, slice(None), (s - 3) // TPB, r), r == 0, False)
                    pe.matmul(PS[:, CB, 0:D], ones[:, :], bias[:, D:2 * D], start=False, stop=True).then_inc(a_c.sem, 1)
            if act:
                if on(-2):
                    a_t1.wait(act, t(-2))
                    a_s.wait(act, t(-3))
                    act.activation(xt1[0][:, :, :], tbank(T1B), ACT.Copy).then_inc(a_h1.sem, 1)
                if on(-3):
                    a_tp.wait(act, t(-3))
                    a_c.wait(act, t(-4))
                    act.activation(PT[0][:, :, :].rearrange("p (j c) t -> p j (c t)", j=2), PS[:, PB:PB + 2, 0:HP],
                                   ACT.Copy).then_inc(a_hp.sem, 1)
                if on(0):
                    a_t0.wait(act, t(0))
                    a_y.wait(act, t(-1))
                    act.activation(xt0[0][:, :, :], tbank(T0B), ACT.Copy).then_inc(a_h0.sem, 1)
                if on(-4):
                    a_t2.wait(act, t(-4))
                    act.activation(xt_tile(0, -4), tbank(T1B), ACT.Copy).then_inc(a_h2.sem, 1)
                if on(-1):
                    a_r1.wait(act, t(-1))
                    a_t1.wait(act, t(-3))
                    a_g1.wait(act, t(-3))
                    act.activation(n1[q(-1)], PS[:, YB, 0:D], ACT.Identity, bias=nmr[:, 0:1],
                                   scale=rstd[:, 1:2]).then_inc(a_n1.sem, 1)
                if on(-2):
                    a_mx.wait(act, t(-2))
                    a_tp.wait(act, t(-4))
                    a_rc.wait(act, t(-3))
                    for h in range(H):
                        j, g = h // HH, h % HH
                        i_ = act.activation(Pm[q(-2)][:, j, g * M:(g + 1) * M], PS[:, SB + j, g * M:(g + 1) * M],
                                            ACT.Exp, bias=mx[:, h:h + 1], accum_out=sm[:, h:h + 1])
                    act.drain()
                    act.sem_inc(a_ex.sem, 1)
            if dve:
                if on(-2):
                    a_h1.wait(dve, t(-2))
                    dve.tensor_tensor(xt1[1][:, :, :], tbank(T1B), f32(xt1[0][:, :, :]), ALU.subtract)\
                       .then_inc(a_l1.sem, 1)
                if on(1):
                    stats(dve, [x_tile(1)], 0).then_inc(a_v0.sem, 1)
                if on(0):
                    a_h0.wait(dve, t(0))
                    dve.tensor_tensor(xt0[1][:, :, :], tbank(T0B), f32(xt0[0][:, :, :]), ALU.subtract)\
                       .then_inc(a_l0.sem, 1)
                if on(-3):
                    a_hp.wait(dve, t(-3))
                    dve.tensor_tensor(PT[1][:, :, :].rearrange("p (j c) t -> p j (c t)", j=2), PS[:, PB:PB + 2, 0:HP],
                                      f32(PT[0][:, :, :].rearrange("p (j c) t -> p j (c t)", j=2)), ALU.subtract)\
                       .then_inc(a_lp.sem, 1)
                if on(-4):
                    a_h2.wait(dve, t(-4))
                    dve.tensor_tensor(xt_tile(1, -4), tbank(T1B), f32(xt_tile(0, -4)), ALU.subtract)\
                       .then_inc(a_l2.sem, 1)
                if on(-1):
                    a_y.wait(dve, t(-1))
                    a_n1.wait(dve, t(-2))
                    stats(dve, [PS[:, YB, 0:D]], 1).then_inc(a_v1.sem, 1)
                if on(1):
                    a_r0.wait(dve, t(1))
                    a_t0.wait(dve, t(0))
                    dve.tensor_scalar(n0, x_tile(1), mv[:, 0, 0:1], rstd[:, 0:1], ALU.subtract, ALU.mult)\
                       .then_inc(a_ln0.sem, 1)
                if on(-2):
                    a_s.wait(dve, t(-2))
                    a_ex.wait(dve, t(-3))
                    dve.tensor_reduce(mx[:, :].rearrange("p (j g) -> p j g", j=2),
                                      PS[:, SB:SB + 2, 0:HM].rearrange("p j (g m) -> p j g m", g=HH),
                                      AX.X, ALU.max, negate=True).then_inc(a_mx.sem, 1)
                if on(-3):
                    a_c.wait(dve, t(-3))
                    a_g1.wait(dve, t(-3))
                    dve.tensor_tensor(z2, PS[:, CB, 0:D], n1g[q(-3)], ALU.add)\
                       .then_inc(a_z.sem, 1)
                    dve.drain()
                    stats(dve, [z2], 2).then_inc(a_v2.sem, 1)
                if on(-2):
                    a_ex.wait(dve, t(-2))
                    a_p.wait(dve, t(-3))
                    dve.reciprocal(rc[:, :], sm[:, :]).then_inc(a_rc.sem, 1)
                if on(-3):
                    a_r2.wait(dve, t(-3))
                    a_t2.wait(dve, t(-5))
                    a_g2.wait(dve, t(-5))
                    dve.tensor_scalar(n2[q(-3)], z2, mv[:, 2, 0:1], rstd[:, 2:3],
                                      ALU.subtract, ALU.mult).then_inc(a_n2.sem, 1)
                    dve.drain()
            if pool:
                if on(1):
                    a_v0.wait(pool, t(1))
                    a_ln0.wait(pool, t(0))
                    rsqrt(pool, 0).then_inc(a_r0.sem, 1)
                if on(-1):
                    a_v1.wait(pool, t(-1))
                    a_n1.wait(pool, t(-2))
                    rsqrt(pool, 1)
                    pool.drain()
                    pool.tensor_scalar(nmr[:, :], mv[:, 1, 0:1], rstd[:, 1:2], -1.0, ALU.mult, ALU.mult)\
                        .then_inc(a_r1.sem, 1)
                if on(-2):
                    a_rc.wait(pool, t(-2))
                    pv = Pm[q(-2)][:, :, 0:HM].rearrange("p j (g m) -> p j g m", g=HH)
                    pool.tensor_tensor(pv, pv, rc[:, :].rearrange("p (j g) -> p j g", j=2).unsqueeze(3)
                                       .to_broadcast([P, 2, HH, M]), ALU.mult).then_inc(a_p.sem, 1)
                if on(-3):
                    a_v2.wait(pool, t(-3))
                    a_n2.wait(pool, t(-4))
                    rsqrt(pool, 2).then_inc(a_r2.sem, 1)
                if on(-1):
                    a_n1.wait(pool, t(-1))
                    a_z.wait(pool, t(-3))
                    pool.tensor_tensor(n1g[q(-1)], n1[q(-1)], bc[:, R_G1, :], ALU.mult)\
                        .then_inc(a_g1.sem, 1)
                if on(-3):
                    a_n2.wait(pool, t(-3))
                    pool.tensor_tensor(x_tile(-3), n2[q(-3)], bc[:, R_G2, :], ALU.mult)\
                        .then_inc(a_g2.sem, 1)

        def stage_a_tiles(pe, act, dve, pool, sp):
            if pe:
                need(pe, "setup")
            if act:
                need(act, "setup")
            if dve:
                dve.wait_ge(s_x, 16)
            if pool:
                need(pool, "setup")
            eng = pe or act or dve or pool
            if not eng:
                return
            for s in range(-1, LAG + 1):
                a_step(pe, act, dve, pool, s, s % 2, 0, NT)
            with eng.Fori(LAG + 1, NT - 2, 2) as s:
                a_step(pe, act, dve, pool, s, (LAG + 1) % 2, 0, NT)
                a_step(pe, act, dve, pool, s + 1, LAG % 2, 0, NT)
            for s in range(NT - 1, NT + LAG):
                a_step(pe, act, dve, pool, s, s % 2, 0, NT)

        def tiles4(buf, c):
            return buf[:, bass.ds(c * TPC, TPC), :]

        def norm4(dve, dst, src, k=0):
            for t in range(TPC):
                i_ = dve.tensor_scalar(dst[:, t, :], src(t), mv[:, k + t, 0:1], rstd[:, k + t:k + t + 1],
                                       ALU.subtract, ALU.mult)
            return i_

        def down(pe, u, hp, wd, bank0, n_units, first, brow_ap=None):
            for t in range(TPC):
                o = PS[:, bank0 + t // 2, (t % 2) * D:(t % 2 + 1) * D]
                st = first and t % 2 == 0
                if first and brow_ap is not None:
                    pe.matmul(o, ones[:, :], brow_ap, start=st, stop=False, skip_group_check=True)
                    st = False
                i_ = mm3(pe, o, sub(hp, slice(None), slice(t * P, (t + 1) * P)), wd, st, True, skip=True)
            return i_

        b_g = event("b_g", credit=1); b_a = event("b_a", credit=1); b_l = event("b_l", credit=1); b_d = event("b_d", credit=1)
        b_z = event("b_z", credit=1); b_v3 = event("b_v3", credit=1); b_r3 = event("b_r3", credit=1); b_n3 = event("b_n3", credit=1); b_m3 = event("b_m3", credit=1)
        b_x = event("b_x", credit=1); b_v4 = event("b_v4", credit=1); b_r4 = event("b_r4", credit=1); b_n4 = event("b_n4", credit=1)
        b_t4 = event("b_t4", credit=1); b_h4 = event("b_h4", credit=1); b_l4 = event("b_l4", credit=1)
        b_lg = event("b_lg", credit=1); b_lc = event("b_lc", credit=1); b_lt = event("b_lt", credit=1); b_ex = event("b_ex", credit=1); b_cm = event("b_cm", credit=1)
        s_xr = sem("s_xr"); s_moe = sem("s_moe"); g_moe = event("g_moe")
        s_rw = sem("s_rw"); g_rw = event("g_rw")
        GB, DB, TB, LB, RB = 0, 2, 4, 6, 7

        def b_tail(pe, act, dve, pool, p, f):
            def x_t(t):
                return X[:, p * TPC + t, :]

            ch = bass.ds(p * CH, CH)
            if f == 0:
                if dve:
                    b_d.wait(dve, NF * p + NF - 1)
                    for t in range(TPC):
                        i_ = dve.tensor_tensor(ztile[:, t, :], PS[:, DB + t // 2, (t % 2) * D:(t % 2 + 1) * D],
                                               x_t(t), ALU.add)
                    i_.then_inc(b_z.sem, 1)
                    dve.drain()
                    stats(dve, [ztile[:, t, :] for t in range(TPC)], 0, TPC).then_inc(b_v3.sem, 1)
                if pool:
                    pool.wait_ge(s_xr, 16 * (p + 1))
                    pool.tensor_tensor(xr4[:, :, :], xr4[:, :, :],
                                       bc[:, R_B3:R_B3 + 1, :].to_broadcast([P, TPC, D]), ALU.add)
                    b_v3.wait(pool, p)
                    rsqrt(pool, 0, TPC).then_inc(b_r3.sem, 1)
            if f == 1:
                if dve:
                    b_r3.wait(dve, p)
                    norm4(dve, ztile, lambda t: ztile[:, t, :]).then_inc(b_n3.sem, 1)
                if pool:
                    b_n3.wait(pool, p)
                    pool.tensor_tensor(ztile[:, :, :], ztile[:, :, :],
                                       bc[:, R_G3:R_G3 + 1, :].to_broadcast([P, TPC, D]), ALU.mult)\
                        .then_inc(b_m3.sem, 1)
            if f == 2:
                if dve:
                    b_m3.wait(dve, p)
                    dve.tensor_tensor(tiles4(X, p), ztile[:, :, :], xr4[:, :, :], ALU.add).then_inc(b_x.sem, 1)
                    dve.drain()
                    stats(dve, [x_t(t) for t in range(TPC)], 0, TPC).then_inc(b_v4.sem, 1)
                if pool:
                    b_v4.wait(pool, p)
                    rsqrt(pool, 0, TPC).then_inc(b_r4.sem, 1)
            if f == 3 and dve:
                b_r4.wait(dve, p)
                b_t4.wait(dve, p - 1)
                norm4(dve, ntile, x_t).then_inc(b_n4.sem, 1)
            if f == 4:
                if pe:
                    b_n4.wait(pe, p)
                    b_l4.wait(pe, p - 1)
                    for k in range(KC):
                        for t in range(TPC):
                            i_ = pe.transpose(PS[:, TB + k, t * P:(t + 1) * P], ntile[:, t, k * P:(k + 1) * P],
                                              ident[:, :])
                    i_.then_inc(b_t4.sem, 1)
                if act:
                    b_t4.wait(act, p)
                    for k in range(KC):
                        i_ = act.activation(XT[0][:, k, ch], PS[:, TB + k, :], ACT.Copy)
                    i_.then_inc(b_h4.sem, 1)
                if dve:
                    b_h4.wait(dve, p)
                    for k in range(KC):
                        i_ = dve.tensor_tensor(XT[1][:, k, ch], PS[:, TB + k, :], f32(XT[0][:, k, ch]), ALU.subtract)
                    i_.then_inc(b_l4.sem, 1)
            if f == 5:
                if pe:
                    b_l4.wait(pe, p)
                    b_lc.wait(pe, p - 1)
                    for k in range(KC):
                        i_ = mm3(pe, PS[:, LB, :], sub(gT, slice(None), k), sub(XT, slice(None), k, ch),
                                 k == 0, k == KC - 1)
                    i_.then_inc(b_lg.sem, 1)
                if act:
                    b_lg.wait(act, p)
                    b_lt.wait(act, p - 1)
                    act.activation(lgT[:, :], PS[:, LB, :], ACT.Copy).then_inc(b_lc.sem, 1)
            if f == 6:
                if pe:
                    b_lc.wait(pe, p)
                    b_ex.wait(pe, p - 1)
                    for t in range(TPC):
                        i_ = pe.transpose(PS[:, RB, t * P:(t + 1) * P], lgT[:, t * P:(t + 1) * P], ident[:, :])
                    i_.then_inc(b_lt.sem, 1)
                if act:
                    b_lt.wait(act, p)
                    b_cm.wait(act, p - 1)
                    act.activation(ex[:, :, :], PS[:, RB, :].rearrange("p (t e) -> p t e", t=TPC)[:, :, 0:E], ACT.Exp,
                                   scale=-1.0).then_inc(b_ex.sem, 1)
            if f == 7 and dve:
                b_ex.wait(dve, p)
                dve.tensor_scalar(sc[:, :, :], ex[:, :, :], 1.0, None, ALU.add)
                dve.drain()
                dve.reciprocal(sc[:, :, :], sc[:, :, :])
                dve.drain()
                for t in range(TPC):
                    dve.max(top8[:, t, :], sc[:, t, :])
                dve.drain()
                for t in range(TPC):
                    dve.max_index(idx8[:, t, :], top8[:, t, :], sc[:, t, :])
                dve.tensor_tensor(tsum[:, :], top8[:, :, 0], top8[:, :, 1], ALU.add)
                dve.drain()
                dve.tensor_copy(idxf[:, :, 0:2], idx8[:, :, 0:2])
                dve.tensor_scalar(tsum[:, :], tsum[:, :], 1e-20, None, ALU.add)
                dve.drain()
                dve.reciprocal(tsum[:, :], tsum[:, :])
                dve.drain()
                for n in range(2):
                    dve.scalar_tensor_tensor(tw[:, :, n], top8[:, :, n], ROUTE_SCALE, tsum[:, :], ALU.mult, ALU.mult)
                dve.drain()
                for t in range(TPC):
                    dve.tensor_scalar(oh[:, t, :], iota[:, :], idxf[:, t, 1:2], tw[:, t, 1:2], ALU.is_equal, ALU.mult)
                    dve.tensor_scalar(ex[:, t, :], iota[:, :], idxf[:, t, 0:1], tw[:, t, 0:1], ALU.is_equal, ALU.mult)
                dve.drain()
                dve.tensor_tensor(tiles4(cmb, p), oh[:, :, :], ex[:, :, :], ALU.add).then_inc(b_cm.sem, 1)

        def b_chunk(pe, act, dve, pool, c, tail):
            for f in range(NF):
                u = NF * c + f
                if pe:
                    b_a.wait(pe, u - 2)
                    for k in range(KC):
                        i_ = mm3(pe, PS[:, GB + f % 2, :], sub(W1, slice(None), k, slice(f * P, (f + 1) * P)),
                                 sub(XT, slice(None), k, bass.ds(c * CH, CH)), k == 0, k == KC - 1)
                    i_.then_inc(b_g.sem, 1)
                if act:
                    b_g.wait(act, u)
                    b_l.wait(act, u - 2)
                    act.activation(work[f % 2][:, :], PS[:, GB + f % 2, :], ACT.Relu, bias=b1col[:, f:f + 1])\
                        .then_inc(b_a.sem, 1)
                if dve:
                    b_a.wait(dve, u)
                    b_d.wait(dve, u - 2)
                    dve.tensor_copy(hid[f % 2][0][:, :], work[f % 2][:, :])
                    dve.drain()
                    dve.tensor_tensor(hid[f % 2][1][:, :], work[f % 2][:, :], f32(hid[f % 2][0][:, :]), ALU.subtract)\
                        .then_inc(b_l.sem, 1)
                if pe and (tail or f):
                    b_down(pe, c, f)
                if tail:
                    b_tail(pe, act, dve, pool, c - 1, f)

        def b_down(pe, c, f):
            g = (f - 1) % NF
            b_l.wait(pe, NF * c + f - 1)
            if g == 0:
                b_z.wait(pe, c - 1)
            down(pe, 0, hid[g % 2], sub(W2, slice(None), g), DB, NF, g == 0, b2row[:, :]).then_inc(b_d.sem, 1)

        def stage_b(pe, act, dve, pool, sp):
            if sp:
                a_g2.wait(sp, NT - 1); a_c.wait(sp, NT - 1); a_l2.wait(sp, NT - 1)
                sp.dma_start(xr4[:, :, :], xv[:, 0:TPC, :]).then_inc(s_xr, 16)
                for n in range(NU):
                    if n:
                        g_moe.wait(sp, n - 1)
                    sp.dma_start(moe_raw[:, 0:KC, :], gu.rearrange("(k p) (n c) -> n p k c", p=P, n=NU)[n])\
                        .then_inc(s_moe, 16)
                    sp.dma_start(moe_raw[:, KC, :], dn[n * P:(n + 1) * P, :]).then_inc(s_moe, 16)
                for n in range(1, NCH):
                    b_x.wait(sp, n - 1)
                    sp.dma_start(xr4[:, :, :], xv[:, n * TPC:(n + 1) * TPC, :]).then_inc(s_xr, 16)
            if pool:
                a_c.wait(pool, NT - 1); a_l2.wait(pool, NT - 1); a_t2.wait(pool, NT - 1)
                pool.memset(selraw[:, :, :], 0.0)
                pool.drain()
                pool.affine_select(out=selraw[:, :, :], in_=selraw[:, :, :], compare_op=ALU.not_equal, fill=1.0,
                                   base=0, pattern=[[-1, E], [0, P]], channel_multiplier=1)
                pool.drain()
                pool.tensor_copy(sel[:, :, :], selraw[:, :, :])
                for n in range(NU):
                    pool.wait_ge(s_moe, 32 * (n + 1))
                    cols_ = slice(n * 2 * I, (n + 1) * 2 * I)
                    pool.tensor_copy(GU[0][:, :, cols_], moe_raw[:, 0:KC, :])
                    pool.tensor_copy(DN[0][:, n, :], moe_raw[:, KC, :])
                    pool.drain()
                    pool.tensor_tensor(GU[1][:, :, cols_], moe_raw[:, 0:KC, :], f32(GU[0][:, :, cols_]), ALU.subtract)
                    pool.tensor_tensor(DN[1][:, n, :], moe_raw[:, KC, :], f32(DN[0][:, n, :]), ALU.subtract)
                    pool.drain()
                    pool.sem_inc(g_moe.sem, 1)
            if pe:
                a_l2.wait(pe, NT - 1)
            if dve:
                a_g2.wait(dve, NT - 1); a_t2.wait(dve, NT - 1)
            eng = pe or act or dve or pool
            if not eng:
                return
            b_chunk(pe, act, dve, pool, 0, False)
            with eng.Fori(1, NCH) as c:
                b_chunk(pe, act, dve, pool, c, True)
            if pe:
                b_down(pe, NCH, 0)
            for f in range(NF):
                b_tail(pe, act, dve, pool, NCH - 1, f)

        c_g = event("c_g", credit=1); c_s = event("c_s", credit=1); c_uo = event("c_uo", credit=1); c_m = event("c_m", credit=1); c_l = event("c_l", credit=1)
        c_d = event("c_d", credit=1); c_bc = event("c_bc", credit=1)
        c_cs = event("c_cs", credit=1); c_ct = event("c_ct", credit=1); c_ch = event("c_ch", credit=1); c_cl = event("c_cl", credit=1)
        c_x = event("c_x", credit=1); c_v = event("c_v", credit=1); c_r = event("c_r", credit=1); c_n = event("c_n", credit=1)
        c_t = event("c_t", credit=1); c_h = event("c_h", credit=1); c_lo = event("c_lo", credit=1)
        CG, CU, CD, CB, CT = 0, 2, 4, 6, 7
        NR = E

        def c_tail(pe, act, dve, pool, p, j):
            def x_t(t):
                return X[:, p * TPC + t, :]

            ch = bass.ds(p * CH, CH)
            if j == 0:
                if dve:
                    c_d.wait(dve, NU * p + NU - 1)
                    for t in range(TPC):
                        i_ = dve.scalar_tensor_tensor(x_t(t), PS[:, CD + t // 2, (t % 2) * D:(t % 2 + 1) * D],
                                                      tg[:, 2:3], x_t(t), ALU.mult, ALU.add)
                    i_.then_inc(c_x.sem, 1)
                    dve.drain()
                    stats(dve, [x_t(t) for t in range(TPC)], 0, TPC).then_inc(c_v.sem, 1)
                if pool:
                    c_v.wait(pool, p)
                    rsqrt(pool, 0, TPC).then_inc(c_r.sem, 1)
            if j == 1 and dve:
                c_r.wait(dve, p)
                c_t.wait(dve, 2 * p - 1)
                norm4(dve, ntile, x_t).then_inc(c_n.sem, 1)
            if j in (2, 3):
                k = j - 2
                if pe:
                    if k == 0:
                        c_n.wait(pe, p)
                        c_cl.wait(pe, NCH - 1 if isinstance(p, int) else p + 1)
                    else:
                        c_lo.wait(pe, 2 * p)
                    for t in range(TPC):
                        i_ = pe.transpose(PS[:, CT, t * P:(t + 1) * P], ntile[:, t, k * P:(k + 1) * P], ident[:, :])
                    i_.then_inc(c_t.sem, 1)
                if act:
                    c_t.wait(act, 2 * p + k)
                    act.activation(XT[0][:, k, ch], PS[:, CT, :], ACT.Copy).then_inc(c_h.sem, 1)
                if dve:
                    c_h.wait(dve, 2 * p + k)
                    dve.tensor_tensor(XT[1][:, k, ch], PS[:, CT, :], f32(XT[0][:, k, ch]), ALU.subtract)\
                        .then_inc(c_lo.sem, 1)

        def c_down(pe, c, j):
            g = (j - 1) % NU
            c_l.wait(pe, NU * c + j - 1)
            if g == 0:
                c_x.wait(pe, c - 1)
            down(pe, 0, hid[g % 2], sub(DN, slice(None), g), CD, NU, g == 0).then_inc(c_d.sem, 1)

        def c_chunk(pe, act, dve, pool, c, tail):
            if dve:
                c_ct.wait(dve, c - 1)
                dve.tensor_copy(cst[:, :, :], tiles4(cmb, c)).then_inc(c_cs.sem, 1)
            if pe:
                c_cs.wait(pe, c)
                c_lo.wait(pe, 2 * c - 3)
                for t in range(TPC):
                    i_ = pe.transpose(PS[0:E, CT, t * P:(t + 1) * P], cst[:, t, :], ident[:, :])
                i_.then_inc(c_ct.sem, 1)
            if act:
                c_ct.wait(act, c)
                c_bc.wait(act, NR * c - 1)
                act.activation(cT[0][:, :], PS[0:E, CT, :], ACT.Copy).then_inc(c_ch.sem, 1)
            if dve:
                c_ch.wait(dve, c)
                dve.tensor_tensor(cT[1][:, :], PS[0:E, CT, :], f32(cT[0][:, :]), ALU.subtract).then_inc(c_cl.sem, 1)
            ch = bass.ds(c * CH, CH)
            for j in range(NU):
                u = NU * c + j
                e = j - 2
                v = NR * c + e
                q = j % 2
                if pe:
                    c_s.wait(pe, u - 2)
                    c_l.wait(pe, u - 2)
                    for half_, bank in ((0, CG), (1, CU)):
                        w0 = (2 * j + half_) * I
                        for k in range(KC):
                            i_ = mm3(pe, PS[:, bank + q, :], sub(GU, slice(None), k, slice(w0, w0 + I)),
                                     sub(XT, slice(None), k, ch), k == 0, k == KC - 1)
                        i_.then_inc((c_g if half_ == 0 else c_uo).sem, 1)
                    if e >= 0:
                        c_cl.wait(pe, c)
                        c_m.wait(pe, v - 1)
                        pe.matmul(PS[:, CB, :], sel[:, e, :], cT[0][:, :], start=True, stop=False)
                        pe.matmul(PS[:, CB, :], sel[:, e, :], cT[1][:, :], start=False, stop=True)\
                            .then_inc(c_bc.sem, 1)
                if act:
                    c_g.wait(act, u)
                    c_l.wait(act, u - 2)
                    act.activation(work[q][:, :], PS[:, CG + q, :], ACT.Silu).then_inc(c_s.sem, 1)
                if dve:
                    c_s.wait(dve, u)
                    c_uo.wait(dve, u)
                    hv = work[2 + q]
                    dve.tensor_tensor(hv[:, :], PS[:, CU + q, :], work[q][:, :], ALU.mult)
                    dve.drain()
                    if e >= 0:
                        c_bc.wait(dve, v)
                        dve.tensor_tensor(hv[:, :], PS[:, CB, :], hv[:, :], ALU.mult).then_inc(c_m.sem, 1)
                        dve.drain()
                    c_d.wait(dve, u - 2)
                    dve.tensor_copy(hid[q][0][:, :], hv[:, :])
                    dve.drain()
                    dve.tensor_tensor(hid[q][1][:, :], hv[:, :], f32(hid[q][0][:, :]), ALU.subtract)\
                        .then_inc(c_l.sem, 1)
                if pe and (tail or j):
                    c_down(pe, c, j)
                if tail:
                    c_tail(pe, act, dve, pool, c - 1, j)

        def stage_c(pe, act, dve, pool, sp):
            if sp:
                for k in range(KC):
                    g_moe.wait(sp, NU - 1)
                    if k:
                        g_rw.wait(sp, k - 1)
                    sp.dma_start(moe_raw[:, :, :], rw[k * P:(k + 1) * P, :].rearrange("p (a d) -> p a d", a=3))\
                        .then_inc(s_rw, 16)
            if pool:
                b_g.wait(pool, NF * NCH - 1)
                for k in range(KC):
                    pool.wait_ge(s_rw, 16 * (k + 1))
                    hi, lo = (W1[n][:, k, 0:3 * D].rearrange("p (a d) -> p a d", a=3) for n in range(2))
                    pool.tensor_copy(hi, moe_raw[:, :, :])
                    pool.drain()
                    pool.tensor_tensor(lo, moe_raw[:, :, :], f32(hi), ALU.subtract)
                    pool.drain()
                    pool.sem_inc(g_rw.sem, 1)
            if pe:
                g_moe.wait(pe, NU - 1)
                b_l4.wait(pe, NCH - 1)
                b_cm.wait(pe, NCH - 1)
            if act:
                act.activation(warm[:, :], tg[:, 0:1], ACT.Silu)
            eng = pe or act or dve or pool
            if not eng:
                return
            c_chunk(pe, act, dve, pool, 0, False)
            with eng.Fori(1, NCH) as c:
                c_chunk(pe, act, dve, pool, c, True)
            if pe:
                c_down(pe, NCH, 0)
            for j in range(4):
                c_tail_last(pe, act, dve, pool, NCH - 1, j)

        def c_tail_last(pe, act, dve, pool, p, j):
            c_tail(pe, act, dve, pool, p, j)

        d_b = event("d_b", credit=1); d_s = event("d_s", credit=1); d_mx = event("d_mx", credit=1); d_ex = event("d_ex", credit=1); d_at = event("d_at", credit=1)
        d_o = event("d_o", credit=1); d_z = event("d_z", credit=2); d_v = event("d_v", credit=1); d_r = event("d_r", credit=1); d_n = event("d_n", credit=1)
        d_t = event("d_t", credit=2); d_xd = event("d_xd", credit=1)
        s_zero = event("s_zero")

        def d_batch(pe, act, dve, pool, b):
            if dve:
                d_s.wait(dve, b - 1)
                for n in range(2):
                    dve.tensor_copy(Bst[n][:, :, :], f32(Bctx[n][:, :, bass.ds(b * M, M)]))
                dve.drain()
                dve.sem_inc(d_b.sem, 1)
            if pe:
                d_b.wait(pe, b)
                d_ex.wait(pe, b - 1)
                for j in range(2):
                    for k in range(KC):
                        i_ = mm3(pe, PS[0:M, j, :], sub(Bst, slice(None), k),
                                 sub(XT, slice(None), k, bass.ds(b * S + j * CH, CH)), k == 0, k == KC - 1)
                i_.then_inc(d_s.sem, 1)
            if dve:
                d_s.wait(dve, b)
                d_ex.wait(dve, b - 1)
                dve.tensor_reduce(nmax[:, :], PS[0:M, 0:2, :], AX.XY, ALU.max, negate=True).then_inc(d_mx.sem, 1)
            if act:
                d_mx.wait(act, b)
                d_at.wait(act, b - 1)
                act.activation(att[:, :].rearrange("m (j t) -> m j t", j=2), PS[0:M, 0:2, :], ACT.Exp,
                               bias=nmax[:, 0:1], accum_out=asum[:, 0:1])
                act.drain()
                act.sem_inc(d_ex.sem, 1)
            if dve:
                d_ex.wait(dve, b)
                d_o.wait(dve, 2 * b - 1)
                dve.reciprocal(ascl[:, :], asum[:, :])
                dve.tensor_copy(attp[0][:, :], att[:, :])
                dve.drain()
                dve.tensor_tensor(ascl[:, :], ascl[:, :], tg[0:M, 1:2], ALU.mult)
                dve.tensor_tensor(attp[1][:, :], att[:, :], f32(attp[0][:, :]), ALU.subtract)
                dve.drain()
                dve.tensor_scalar(c2f[:, :], C2[:, b, :], ascl[:, 0:1], None, ALU.mult)
                dve.drain()
                dve.tensor_copy(c2s[0][:, :], c2f[:, :])
                dve.drain()
                dve.tensor_tensor(c2s[1][:, :], c2f[:, :], f32(c2s[0][:, :]), ALU.subtract)
                dve.drain()
                dve.sem_inc(d_at.sem, 1)
            for g in range(2):
                c = 2 * b + g
                bank = 2 if g == 0 else 6
                if pe:
                    d_at.wait(pe, b)
                    d_z.wait(pe, c - 2)
                    for t in range(TPC):
                        tok = slice((g * TPC + t) * P, (g * TPC + t + 1) * P)
                        i_ = mm3(pe, PS[:, bank + t // 2, (t % 2) * D:(t % 2 + 1) * D],
                                 sub(attp, slice(None), tok), sub(c2s, slice(None), slice(None)), True, True)
                    i_.then_inc(d_o.sem, 1)
            for g in range(2):
                c = 2 * b + g
                bank = 2 if g == 0 else 6
                if dve:
                    d_o.wait(dve, c)
                    for t in range(TPC):
                        xt_ = X[:, c * TPC + t, :]
                        i_ = dve.tensor_tensor(xt_, PS[:, bank + t // 2, (t % 2) * D:(t % 2 + 1) * D], xt_, ALU.add)
                    i_.then_inc(d_z.sem, 1)
                    dve.drain()
                    stats(dve, [X[:, c * TPC + t, :] for t in range(TPC)], TPC * g, TPC).then_inc(d_v.sem, 1)
                if pool:
                    d_v.wait(pool, c)
                    rsqrt2(pool, TPC * g).then_inc(d_r.sem, 1)
            for g in range(2):
                c = 2 * b + g
                nt_ = ntile if g == 0 else ztile
                if dve:
                    d_r.wait(dve, c)
                    d_t.wait(dve, c - 2)
                    norm4(dve, nt_, lambda t: X[:, c * TPC + t, :], TPC * g).then_inc(d_n.sem, 1)
                if pe:
                    d_n.wait(pe, c)
                    d_xd.wait(pe, c - 1)
                    for k in range(KC):
                        for t in range(TPC):
                            i_ = pe.transpose(PS[:, 4 + k, t * P:(t + 1) * P], nt_[:, t, k * P:(k + 1) * P],
                                              ident[:, :])
                    i_.then_inc(d_t.sem, 1)
                if act:
                    d_t.wait(act, c)
                    for k in range(KC):
                        i_ = act.activation(XD[:, k, bass.ds(b * (S + 1) + 1 + g * CH, CH)], PS[:, 4 + k, :], ACT.Copy)
                    i_.then_inc(d_xd.sem, 1)

        def rsqrt2(pool, k):
            return pool.tensor_tensor(rstd[:, k:k + TPC], var[:, k:k + TPC], half[:, 0:TPC], ALU.pow)

        def stage_d(pe, act, dve, pool, sp):
            if pe:
                c_lo.wait(pe, 2 * NCH - 1)
            if dve:
                c_d.wait(dve, NU * NCH - 1)
                for b in range(B):
                    i_ = dve.memset(XD[:, :, b * (S + 1):b * (S + 1) + 1], 0.0)
                i_.then_inc(s_zero.sem, 1)
            if act:
                c_d.wait(act, NU * NCH - 1)
                act.activation(warm[:, :], tg[:, 0:1], ACT.Exp)
            eng = pe or act or dve or pool
            if not eng:
                return
            with eng.Fori(0, B) as b:
                d_batch(pe, act, dve, pool, b)

        e_df = event("e_df", credit=1); e_mx = event("e_mx", credit=1); e_xh = event("e_xh", credit=1); e_xl = event("e_xl", credit=1)
        e_k = event("e_k", credit=1); e_s = event("e_s", credit=1); e_kl = event("e_kl", credit=1); e_r = event("e_r", credit=1); e_sg = event("e_sg", credit=1)
        e_vo = event("e_vo", credit=1); e_o = event("e_o", credit=1); e_st = [sem(f"e_st{g}") for g in range(2)]
        EK, ER, EV = 0, 2, 4

        def e_chunk(pe, act, dve, pool, sp, b, g):
            c = 2 * b + g
            off = b * (S + 1) + g * CH
            rs = work[2:4]
            if pool:
                e_mx.wait(pool, 2 * c - 1)
                pool.tensor_tensor(dif[:, :, :], XD[:, :, bass.ds(off + 1, CH)], XD[:, :, bass.ds(off, CH)],
                                   ALU.subtract).then_inc(e_df.sem, 1)
            for n, cc in ((1, C_MUK), (0, C_MUR)):
                m = 2 * c + 1 - n
                if dve:
                    e_df.wait(dve, c)
                    for k in range(KC):
                        i_ = dve.scalar_tensor_tensor(xmix[n][:, k, :], dif[:, k, :], col[:, k, cc:cc + 1],
                                                      XD[:, k, bass.ds(off, CH)], ALU.mult, ALU.add)
                    i_.then_inc(e_mx.sem, 1)
                if act:
                    e_mx.wait(act, m)
                    (e_k if n else e_r).wait(act, c - 1)
                    act.activation(xm[n][0][:, :, :], xmix[n][:, :, :], ACT.Copy).then_inc(e_xh.sem, 1)
                if dve:
                    e_xh.wait(dve, m)
                    dve.tensor_tensor(xm[n][1][:, :, :], xmix[n][:, :, :], f32(xm[n][0][:, :, :]), ALU.subtract)\
                        .then_inc(e_xl.sem, 1)
            if pe:
                e_xl.wait(pe, 2 * c)
                e_s.wait(pe, c - 1)
                for f in range(KC):
                    for k in range(KC):
                        i_ = mm3(pe, PS[:, EK + f, :], sub(W1, slice(None), k, slice(D + f * P, D + (f + 1) * P)),
                                 sub(xm[1], slice(None), k), k == 0, k == KC - 1)
                i_.then_inc(e_k.sem, 1)
                e_xl.wait(pe, 2 * c + 1)
                e_sg.wait(pe, c - 1)
                for t in range(TPC):
                    for k in range(KC):
                        i_ = mm3(pe, PS[:, ER + t // 2, (t % 2) * D:(t % 2 + 1) * D],
                                 sub(xm[0], slice(None), k, slice(t * P, (t + 1) * P)),
                                 sub(W1, slice(None), k, slice(0, D)), k == 0, k == KC - 1)
                i_.then_inc(e_r.sem, 1)
            if act:
                e_k.wait(act, c)
                e_kl.wait(act, c - 1)
                for f in range(KC):
                    i_ = act.activation(work[f][:, :], PS[:, EK + f, :], ACT.Relu)
                i_.then_inc(e_s.sem, 1)
                e_r.wait(act, c)
                e_o.wait(act, c - 1)
                for q in range(2):
                    i_ = act.activation(rs[q][:, :], PS[:, ER + q, :], ACT.Sigmoid)
                i_.then_inc(e_sg.sem, 1)
            if dve:
                e_s.wait(dve, c)
                e_vo.wait(dve, c - 1)
                for f in range(KC):
                    dve.tensor_tensor(work[f][:, :], work[f][:, :], work[f][:, :], ALU.mult)
                dve.drain()
                for f in range(KC):
                    dve.tensor_copy(ka[0][:, f, :], work[f][:, :])
                dve.drain()
                for f in range(KC):
                    i_ = dve.tensor_tensor(ka[1][:, f, :], work[f][:, :], f32(ka[0][:, f, :]), ALU.subtract)
                i_.then_inc(e_kl.sem, 1)
            if pe:
                e_kl.wait(pe, c)
                e_o.wait(pe, c - 1)
                for t in range(TPC):
                    for f in range(KC):
                        i_ = mm3(pe, PS[:, EV + t // 2, (t % 2) * D:(t % 2 + 1) * D],
                                 sub(ka, slice(None), f, slice(t * P, (t + 1) * P)),
                                 sub(W1, slice(None), f, slice(2 * D, 3 * D)), f == 0, f == KC - 1)
                i_.then_inc(e_vo.sem, 1)
            ot = ztile if g == 0 else ntile
            if dve:
                e_vo.wait(dve, c)
                e_sg.wait(dve, c)
                dve.wait_ge(e_st[g], 16 * b + 16)
                for q in range(2):
                    dve.tensor_tensor(rs[q][:, :], PS[:, EV + q, :], rs[q][:, :], ALU.mult)
                dve.drain()
                for q in range(2):
                    i_ = dve.scalar_tensor_tensor(ot[:, 2 * q:2 * q + 2, :],
                                                  rs[q][:, :].rearrange("p (a d) -> p a d", a=2), tg[:, 3:4],
                                                  X[:, bass.ds(c * TPC + 2 * q, 2), :], ALU.mult, ALU.add)
                i_.then_inc(e_o.sem, 1)
            if sp:
                e_o.wait(sp, c)
                sp.dma_start(ov[:, bass.ds(c * TPC, TPC), :], ot[:, :, :]).then_inc(e_st[g], 16)

        def stage_e(pe, act, dve, pool, sp):
            if pool:
                s_zero.wait(pool, 0)
                d_xd.wait(pool, NCH - 1)
            if pe:
                g_rw.wait(pe, KC - 1)
            if act:
                act.activation(warm[:, :], tg[:, 0:1], ACT.Sigmoid)
            if dve:
                d_t.wait(dve, NCH - 1)
                d_xd.wait(dve, NCH - 1)
            eng = pe or act or dve or pool or sp
            with eng.Fori(0, B) as b:
                for g in range(2):
                    e_chunk(pe, act, dve, pool, sp, b, g)
            if sp:
                for g in range(2):
                    sp.wait_ge(e_st[g], 16 * B + 16)


        def program(pe, act, dve, pool, sp):
            if sp:
                for ev in events:
                    if ev.credit:
                        sp.sem_inc(ev.sem, ev.credit)
                for g in range(2):
                    sp.sem_inc(e_st[g], 16)
                sp.dma_start(rawA[:, :, :], raw.rearrange("(k p) n -> p k n", p=P)).then_inc(s_in[0], 16)
                sp.dma_start(ctx_sb[:, :, :], ctxT.rearrange("(k p) n -> p k n", p=P)).then_inc(s_in[0], 16)
                sp.dma_start(col[:, :, :], cols.rearrange("(k p) n -> p k n", p=P)).then_inc(s_in[0], 16)
                sp.dma_start(ntile[0:1, :, :], brow[0:4, :].rearrange("(a n) d -> a n d", a=1)).then_inc(s_in[0], 16)
                sp.dma_start(ztile[0:1, 3, :], brow[4:5, :]).then_inc(s_in[0], 16)
                sp.dma_start(X[:, :, :], xv).then_inc(s_x, 16)
                sp.dma_start(w1raw[:, :, :], w1.rearrange("(k p) n -> p k n", p=P)).then_inc(s_in[1], 16)
                sp.dma_start(w2raw[:, :, :], w2.rearrange("p (f d) -> p f d", f=NF)).then_inc(s_in[1], 16)
                sp.dma_start(b1col[:, :], l1b).then_inc(s_in[1], 16)
                sp.dma_start(gT_raw[:, :, :], gateT.rearrange("(k p) n -> p k n", p=P)).then_inc(s_in[1], 16)
            if act:
                act.dma_start(bc[:, :, :], bcast.rearrange("(a n) d -> a n d", a=1).to_broadcast([P, 4, D])).then_inc(s_in[2], 16)
                act.dma_start(gate_raw[:, :], gates.rearrange("(a n) -> a n", a=1).to_broadcast([P, 4])).then_inc(s_in[2], 16)
            if pool:
                pool.memset(ident[:, :], 0.0)
                pool.memset(f32(ones[:, :]), 0.0)
                pool.memset(half[:, :], -0.5)
                for k in range(2):
                    pool.memset(Pm[k][:, :, :], 0.0)
                pool.memset(f32(bias[:, :]), 0.0)
                pool.memset(f32(sbias[:, :, :, :]), 0.0)
                pool.memset(f32(b2row[:, :]), 0.0)
                pool.iota(iota[:, :], [[1, E]], base=0, channel_multiplier=0, allow_small_or_imprecise_dtypes=True)
                pool.drain()
                pool.memset(f32(ones[0:1, :]), 1.0)
                pool.memset(f32(ones[32:33, :]), 1.0)
                pool.drain()
                pool.affine_select(out=ident[:, :], in_=ident[:, :], compare_op=ALU.not_equal, fill=1.0,
                                   base=0, pattern=[[-1, P]], channel_multiplier=1)
                done(pool, "const")

            def w(k, which, j):
                return rawA[:, k, which * D + j * P: which * D + (j + 1) * P]

            def wrow(k, which):
                return rawA[:, k, which * D:(which + 1) * D]

            brow_raw = [ntile[0:1, n, :] for n in range(4)] + [ztile[0:1, 3, :]]
            brow_sum = [work[2][0:1, 0:D], work[2][0:1, D:2 * D], work[3][0:1, 0:D]]
            kv = work
            scale = float(DH) ** -0.5
            if pe:
                pe.wait_ge(s_in[0], 80)
                need(pe, "const")
                for j in range(KC):
                    for which, c0 in ((W_K, 0), (W_VM, B * M)):
                        for k in range(KC):
                            pe.matmul(PS[:, j, c0:c0 + B * M], w(k, which, j), ctx_sb[:, k, :],
                                      start=(k == 0), stop=(k == KC - 1))
                done(pe, "kv_ps")
                for j in range(KC):
                    for k in range(KC):
                        pe.matmul(PS[:, 2, j * D:(j + 1) * D], w(k, W_V, j), wrow(k, W_SO),
                                  start=(k == 0), stop=(k == KC - 1))
                for k in range(KC):
                    pe.matmul(PS[0:1, 3, 0:D], col[:, k, C_BV:C_BV + 1], wrow(k, W_SO),
                              start=(k == 0), stop=(k == KC - 1))
                done(pe, "m_ps")
                for j in range(KC):
                    for k in range(KC):
                        pe.matmul(PS[:, 4, j * B * M:(j + 1) * B * M], w(k, W_E, j), ctx_sb[:, k, :],
                                  start=(k == 0), stop=(k == KC - 1))
                for b in range(B):
                    for k in range(KC):
                        pe.matmul(PS[0:M, 5, b * D:(b + 1) * D], ctx_sb[:, k, b * M:(b + 1) * M],
                                  wrow(k, W_2), start=(k == 0), stop=(k == KC - 1))
                pe.wait_ge(s_in[1], 64)
                for f in range(NF):
                    for k in range(KC):
                        pe.matmul(PS[:, 6, f:f + 1], w1raw[:, k, f * P:(f + 1) * P],
                                  col[:, k, C_B2:C_B2 + 1], start=(k == 0), stop=(k == KC - 1))
                done(pe, "l1_ps")
                need(pe, "m_sb")
                for b in range(B):
                    need(pe, f"lay{b}")
                    if b:
                        need(pe, "row0_sb")
                    for j in range(KC):
                        for k in range(2):
                            pe.matmul(PS[:, 2 * j + k, 0:HM], w(k, W_Q, j), Pm[0][:, k, 0:HM],
                                      start=True, stop=True)
                    done(pe, f"a{b}_ps")
                    need(pe, "vw0_sb" if b else "l1_sb")
                    for r in range(2 * NQ):
                        j, q = r // NQ, r % NQ
                        pe.matmul(PS[:, 4 + r // 2, (r % 2) * D:(r % 2 + 1) * D],
                                  Pm[1][:, j, q * P:(q + 1) * P], wrow(j, W_O), start=True, stop=True)
                    need(pe, f"a{b}_sb")
                    for k in range(2):
                        o = PS[0:1, 0 if k else 7, 0:HM]
                        pe.matmul(o, col[:, k, C_BQ:C_BQ + 1], Pm[0][:, k, 0:HM], start=True, stop=False)
                        for j in range(KC):
                            pe.matmul(o, col[:, j, C_B1:C_B1 + 1], araw[:, j, k, :],
                                      start=False, stop=(j == KC - 1))
                    done(pe, f"vwrow{b}_ps")
            if dve:
                dve.wait_ge(s_in[0], 80)
                need(dve, "const")
                for n in range(2):
                    dve.memset(f32(gT[n][:, :, E:P]), 0.0)
                need(dve, "kv_ps")
                for k in range(KC):
                    dve.tensor_scalar(kv[k][:, 0:B * M], PS[:, k, 0:B * M], col[:, k, C_BK:C_BK + 1],
                                      scale, ALU.add, ALU.mult)
                    dve.tensor_scalar(kv[k][:, B * M:2 * B * M], PS[:, k, B * M:2 * B * M],
                                      col[:, k, C_BVM:C_BVM + 1], None, ALU.add)
                dve.drain()

                def lay_out(b):
                    for k in range(KC):
                        for h in range(HH):
                            r = slice(h * DH, (h + 1) * DH)
                            for n in range(2):
                                dve.tensor_copy(Pm[n][r, k, h * M:(h + 1) * M],
                                                kv[k][r, (n * B + b) * M:(n * B + b + 1) * M])
                    done(dve, f"lay{b}")

                lay_out(0)
                need(dve, "m_ps")
                for j in range(KC):
                    for k in range(KC):
                        dst = ztile[:, j, k * P:(k + 1) * P]
                        src = PS[:, 2, j * D + k * P:j * D + (k + 1) * P]
                        if j == k:
                            dve.tensor_tensor(dst, src, ident[:, :], ALU.add)
                        else:
                            dve.tensor_copy(dst, src)
                dve.tensor_tensor(brow_sum[0], PS[0:1, 3, 0:D], brow_raw[BR_SO], ALU.add)
                dve.tensor_tensor(brow_sum[1], brow_raw[BR_O], brow_raw[BR_B1], ALU.add)
                dve.tensor_tensor(brow_sum[2], brow_raw[BR_F2], brow_raw[BR_B2], ALU.add)
                done(dve, "m_sb")
                dve.tensor_copy(Mt[0][:, :, :], ztile[:, 0:KC, :])
                rows = ((bias[:, 0:D], 0), (bias[:, D:2 * D], 1), (b2row[:, :], 2))
                for t_, n in rows:
                    dve.tensor_copy(t_[0:1, :], brow_sum[n])
                dve.drain()
                dve.tensor_tensor(Mt[1][:, :, :], ztile[:, 0:KC, :], f32(Mt[0][:, :, :]), ALU.subtract)
                for t_, n in rows:
                    dve.tensor_tensor(t_[32:33, :], brow_sum[n], f32(t_[0:1, :]), ALU.subtract)
                need(dve, "l1_ps")
                bk = PS[:, 4, 0:KC * B * M].rearrange("p (j c) -> p j c", j=KC)
                dve.tensor_copy(Bctx[0][:, :, :], bk)
                dve.tensor_copy(C2[:, :, :], PS[0:M, 5, :].rearrange("m (b d) -> m b d", b=B))
                dve.tensor_tensor(b1col[:, :], PS[:, 6, 0:NF], b1col[:, :], ALU.add)
                dve.drain()
                dve.tensor_tensor(Bctx[1][:, :, :], bk, f32(Bctx[0][:, :, :]), ALU.subtract)
                dve.tensor_copy(gT[0][:, :, 0:E], gT_raw[:, :, :])
                dve.drain()
                dve.tensor_tensor(gT[1][:, :, 0:E], gT_raw[:, :, :], f32(gT[0][:, :, 0:E]), ALU.subtract)
                done(dve, "l1_sb")
                for b in range(B):
                    need(dve, f"a{b}_sb")
                    for j in range(KC):
                        dve.tensor_scalar(A[0][:, b, j, :, :], araw[:, j, :, :], col[:, j, C_G1:C_G1 + 1],
                                          None, ALU.mult)
                    dve.drain()
                    for j in range(KC):
                        dve.scalar_tensor_tensor(A[1][:, b, j, :, :], araw[:, j, :, :], col[:, j, C_G1:C_G1 + 1],
                                                 f32(A[0][:, b, j, :, :]), ALU.mult, ALU.subtract)
                    need(dve, f"vwhi{b}")
                    for r in range(NQ):
                        dve.tensor_tensor(VW[1][:, b, 2 * r:2 * r + 2, :],
                                          PS[:, 4 + r, :].rearrange("p (a d) -> p a d", a=2),
                                          f32(VW[0][:, b, 2 * r:2 * r + 2, :]), ALU.subtract)
                    for k in range(2):
                        dve.tensor_tensor(sbias[32:33, b, k, :], PS[0:1, 0 if k else 7, 0:HM],
                                          f32(sbias[0:1, b, k, :]), ALU.subtract)
                    done(dve, f"vw{b}_sb")
                    done(dve, f"row{b}_sb")
                    if b == 0:
                        lay_out(1)
                need(dve, "wsplit")
                done(dve, "setup")
            if act:
                act.wait_ge(s_in[2], 32)
                act.activation(tg[:, :], gate_raw[:, :], ACT.Tanh)
                done(act, "tanh")
                for b in range(B):
                    need(act, f"a{b}_ps")
                    if b:
                        need(act, "row0_sb")
                    for j in range(KC):
                        for k in range(2):
                            act.activation(araw[:, j, k, :], PS[:, 2 * j + k, 0:HM], ACT.Copy)
                    done(act, f"a{b}_sb")
                    need(act, f"vwrow{b}_ps")
                    for r in range(NQ):
                        act.activation(VW[0][:, b, 2 * r:2 * r + 2, :],
                                       PS[:, 4 + r, :].rearrange("p (a d) -> p a d", a=2), ACT.Copy)
                    for k in range(2):
                        act.activation(sbias[0:1, b, k, :], PS[0:1, 0 if k else 7, 0:HM], ACT.Copy)
                    done(act, f"vwhi{b}")
            if pool:
                pool.wait_ge(s_in[0], 80)
                pool.wait_ge(s_in[1], 64)
                need(pool, "l1_ps")
                for k in range(KC):
                    pool.tensor_scalar(w1raw[:, k, :], w1raw[:, k, :], col[:, k, C_G2:C_G2 + 1], 0.0,
                                       ALU.mult, ALU.add)
                pool.tensor_copy(W2[0][:, :, :], w2raw[:, :, :])
                pool.drain()
                pool.tensor_copy(W1[0][:, :, :], w1raw[:, :, :])
                pool.tensor_tensor(W2[1][:, :, :], w2raw[:, :, :], f32(W2[0][:, :, :]), ALU.subtract)
                pool.drain()
                pool.tensor_tensor(W1[1][:, :, :], w1raw[:, :, :], f32(W1[0][:, :, :]), ALU.subtract)
                need(pool, "tanh")
                for r_ in (R_G3, R_B3):
                    pool.tensor_scalar(bc[:, r_, :], bc[:, r_, :], tg[:, 0:1], 0.0, ALU.mult, ALU.add)
                done(pool, "wsplit")

            stage_a_tiles(pe, act, dve, pool, sp)
            stage_b(pe, act, dve, pool, sp)
            stage_c(pe, act, dve, pool, sp)
            stage_d(pe, act, dve, pool, sp)
            stage_e(pe, act, dve, pool, sp)

        @block.sync
        def _(eng):
            program(None, None, None, None, eng)

        @block.tensor
        def _(eng):
            program(eng, None, None, None, None)

        @block.scalar
        def _(eng):
            program(None, eng, None, None, None)

        @block.vector
        def _(eng):
            program(None, None, eng, None, None)

        @block.gpsimd
        def _(eng):
            program(None, None, None, eng, None)




def kernel(**inputs):
    import numpy as np
    import concourse.bacc as bacc
    from concourse.bass_utils import run_bass_kernel_spmd

    f = {k: np.asarray(v) for k, v in inputs.items()}
    a = {k[9:]: v for k, v in f.items() if k.startswith("L0_xattn_")}
    m = {k[7:]: v for k, v in f.items() if k.startswith("L0_ffn_")}
    r = {k[7:]: v for k, v in f.items() if k.startswith("L1_ffn_")}
    c = np.concatenate
    raw = c([a["qkv_w"][2 * D:], a["sa_out_w"].T, a["in_proj_w"][:D], a["in_proj_w"][D:2 * D].T,
             a["in_proj_w"][2 * D:].T, a["mha_out_w"].T, f["L1_xattn_We"].T, f["L1_xattn_W2"].T], axis=1)
    cols = np.stack([a["qkv_b"][2 * D:], a["in_proj_b"][D:2 * D], a["in_proj_b"][2 * D:], a["in_proj_b"][:D],
                     a["ln1_g"], a["ln1_b"], a["ln2_g"], a["ln2_b"], r["mu_r"], r["mu_k"]], axis=1)
    bcast = np.stack([a["ln1_g"], a["ln2_g"], a["ln3_g"], a["ln3_b"]])
    brow = np.stack([a["sa_out_b"], a["mha_out_b"], a["lin2_b"], a["ln1_b"], a["ln2_b"]])
    wg = c([m["ws_gate"].reshape(2, I, D), m["w_gate"]])
    wu = c([m["ws_up"].reshape(2, I, D), m["w_up"]])
    gu = np.stack([wg, wu], axis=1).reshape(NU * 2 * I, D).T
    dn = c([m["ws_down"].T.reshape(2, I, D), m["w_down"].transpose(0, 2, 1)]).reshape(NU * I, D)
    arrays = {
        "x": f["x"].reshape(B * S, D), "ctxT": f["ctx_1024"].reshape(B * M, D).T,
        "gates": c([f["g_xattn"], f["g_ffn"]]), "raw": raw, "cols": cols, "l1b": a["lin1_b"].reshape(NF, P).T, "bcast": bcast,
        "brow": brow, "w1": a["lin1_w"].T, "w2": a["lin2_w"].T.reshape(NF, P, D).transpose(1, 0, 2).reshape(P, NF * D),
        "gateT": m["gate_weight"].T, "gu": gu, "dn": dn,
        "rw": c([r["W_r"].T, r["W_k"].T, r["W_v"].T], axis=1),
    }
    arrays = {k: np.ascontiguousarray(v) for k, v in arrays.items()}
    nc = bacc.Bacc("TRN2", target_bir_lowering=False, num_devices=1)
    aps = [nc.dram_tensor(k, v.shape, mybir.dt.from_np(v.dtype), kind="ExternalInput").ap() for k, v in arrays.items()]
    out = nc.dram_tensor("out", (B * S, D), F32, kind="ExternalOutput").ap()
    build(nc, *aps, out)
    res = run_bass_kernel_spmd(nc, [arrays], core_ids=[0])
    return res.results[0]["out"].reshape(B, S, D)
```

```python
from contextlib import ExitStack

import concourse.bass as bass
from concourse import mybir

F32 = mybir.dt.float32
F32R = mybir.dt.float32r
U32 = mybir.dt.uint32
ALU = mybir.AluOpType
ACT = mybir.ActivationFunctionType
AX = mybir.AxisListType

P = 128
B, S, D = 2, 1024, 256
KC = D // P
NT = B * S // P
CH = 512
TPC = CH // P
NCH = B * S // CH
TPB = S // P
M = 77
H, DH = 8, 32
HH = H // 2
HM = HH * M
HP = 384
NQ = HP // P
FF, NF = 1024, 8
E, I = 8, 128
NU = E + 2
EPS = 1e-5
ROUTE_SCALE = 2.5

(W_K, W_VM, W_V, W_SO, W_Q, W_O, W_E, W_2) = range(8)
(C_BV, C_BK, C_BVM, C_BQ, C_G1, C_B1, C_G2, C_B2, C_MUR, C_MUK) = range(10)
NCOL = 10
(R_G1, R_G2, R_G3, R_B3, R_B1) = range(5)
NBC = 5
(BR_SO, BR_O, BR_F2, BR_B1, BR_B2) = range(5)


class Event:

    def __init__(self, sem, per=1, credit=0):
        self.sem, self.per, self.credit = sem, per, credit

    def wait(self, eng, t, k=0):
        value = self.per * t + k + 1 + self.credit
        if isinstance(value, int) and value <= self.credit:
            return
        eng.wait_ge(self.sem, value)


def build(nc, x, ctxT, gates, raw, cols, l1b, bcast, brow, w1, w2, gateT, gu, dn, rw, out):
    with ExitStack() as top:
        def sem(name):
            return top.enter_context(nc.semaphore(name))

        events = []

        def event(name, per=1, credit=0):
            events.append(Event(sem(name), per, credit))
            return events[-1]

        def sb(ctx, name, shape, dt=F32):
            return ctx.enter_context(nc.sbuf_tensor(name, shape, dt))

        def pair(ctx, name, shape):
            return sb(ctx, name + "_hi", shape, F32R), sb(ctx, name + "_lo", shape, F32R)

        with ExitStack() as setup:
            rawA = sb(setup, "rawA", [P, KC, 8 * D])
            w1raw = sb(setup, "w1raw", [P, KC, FF])
            w2raw = sb(setup, "w2raw", [P, NF, D])
        XT = pair(top, "XT", [P, KC, B * S])
        X = sb(top, "X", [P, NT, D])
        W1 = pair(top, "W1", [P, KC, FF])
        W2 = pair(top, "W2", [P, NF, D])
        hid = [pair(top, f"hid{k}", [P, CH]) for k in range(2)]
        work = [sb(top, f"work{k}", [P, CH]) for k in range(4)]
        ntile = sb(top, "ntile", [P, TPC, D])
        ztile = sb(top, "ztile", [P, TPC, D])
        bc = sb(top, "bc", [P, NBC, D])
        gate_raw = sb(top, "gate_raw", [P, 4])
        tg = sb(top, "tg", [P, 4])
        col = sb(top, "col", [P, KC, NCOL])
        b1col = sb(top, "b1col", [P, NF])
        warm = sb(top, "warm", [P, 1])
        b2row = sb(top, "b2row", [33, D], F32R)
        ident = sb(top, "ident", [P, P])
        ones = sb(top, "ones", [33, P], F32R)
        ctx_sb = sb(top, "ctx_sb", [P, KC, B * M])
        Bctx = pair(top, "Bctx", [P, KC, B * M])
        C2 = sb(top, "C2", [M, B, D])
        gT_raw = sb(top, "gT_raw", [P, KC, E])
        gT = pair(top, "gT", [P, KC, P])
        cmb = sb(top, "cmb", [P, NT, E])
        moe_raw = [sb(top, f"moe_raw{k}", [P, 3, D]) for k in range(2)]
        stat = sb(top, "stat", [P, 8, 6])
        mv = sb(top, "mv", [P, 8, 2])
        var = sb(top, "var", [P, 8])
        rstd = sb(top, "rstd", [P, 8])
        half = sb(top, "half", [P, 8])
        iota = sb(top, "iota", [P, E])
        with ExitStack() as stage_a:
            Mt = pair(stage_a, "Mt", [P, KC, D])
            A = pair(stage_a, "A", [P, B, KC, 2, HM])
            VW = pair(stage_a, "VW", [P, B, 2 * NQ, D])
            bias = sb(stage_a, "bias", [33, 2 * D], F32R)
            sbias = sb(stage_a, "sbias", [33, B, 2, HM], F32R)
            xt01 = pair(stage_a, "xt01", [P, 2, KC, P])
            Pm = [sb(stage_a, f"Pm{k}", [P, 2, HP]) for k in range(2)]
            PT = pair(stage_a, "PT", [P, 2 * NQ, P])
            n0, n1, n2 = ntile[:, 0, :], (ntile[:, 1, :], ntile[:, 2, :]), (ntile[:, 3, :], ztile[:, 3, :])
            nmr = sb(stage_a, "nmr", [P, 1])
            ucol = sb(stage_a, "ucol", [P, KC])
            lay_v1 = sb(stage_a, "lay_v1", [P, KC, HP])
            stat0 = sb(stage_a, "stat0", [P, NT, 6])
            mv0 = sb(stage_a, "mv0", [P, NT, 2])
            var0 = sb(stage_a, "var0", [P, NT])
            rstd0 = sb(stage_a, "rstd0", [P, NT])
            nmr0 = sb(stage_a, "nmr0", [P, NT])
            mx = sb(stage_a, "mx", [P, H])
            sm = sb(stage_a, "sm", [P, H])
            rc = sb(stage_a, "rc", [P, H])
        with ExitStack() as stage_c:
            GU = pair(stage_c, "GU", [P, KC, 2 * NU * I])
            DN = pair(stage_c, "DN", [P, NU, D])
            cT = pair(stage_c, "cT", [E, CH])
            cst = sb(stage_c, "cst", [P, TPC, E])
            lgT = sb(stage_c, "lgT", [P, CH])
            sel = sb(stage_c, "sel", [E, E, P], F32R)
            selraw = sb(stage_c, "selraw", [E, E, P])
            xr4 = sb(stage_c, "xr4", [P, TPC, D])
            ex = sb(stage_c, "ex", [P, TPC, E])
            sc = sb(stage_c, "sc", [P, TPC, E])
            top8 = sb(stage_c, "top8", [P, TPC, 8])
            idx8 = sb(stage_c, "idx8", [P, TPC, 8], U32)
            idxf = sb(stage_c, "idxf", [P, TPC, 8])
            tsum = sb(stage_c, "tsum", [P, TPC])
            tw = sb(stage_c, "tw", [P, TPC, 2])
            oh = sb(stage_c, "oh", [P, TPC, E])
        with ExitStack() as stage_e:
            XD = sb(stage_e, "XD", [P, KC, B * (S + 1)])
            Bst = pair(stage_e, "Bst", [P, KC, M])
            att = sb(stage_e, "att", [M, S])
            attp = pair(stage_e, "attp", [M, S])
            c2s = pair(stage_e, "c2s", [M, D])
            c2f = sb(stage_e, "c2f", [M, D])
            nmax = sb(stage_e, "nmax", [M, 1])
            asum = sb(stage_e, "asum", [M, 1])
            ascl = sb(stage_e, "ascl", [M, 1])
            dif = sb(stage_e, "dif", [P, KC, CH])
            xmix = [sb(stage_e, f"xmix{k}", [P, KC, CH]) for k in range(2)]
            xm = [pair(stage_e, f"xm{k}", [P, KC, CH]) for k in range(2)]
            ka = pair(stage_e, "ka", [P, KC, CH])
        PS = top.enter_context(nc.psum_tensor("PS", [P, 8, 512], F32))

        xv = x.rearrange("(i p) d -> p i d", p=P)
        ov = out.rearrange("(i p) d -> p i d", p=P)

        N_LOADS = {"kv": 2, "m": 3, "q": 1, "x": 1, "e": 2, "w1": 2, "w2": 1, "col": 1, "bc": 2}
        s_ld = {name: sem("ld_" + name) for name in N_LOADS}

        def load(eng, name, dst, src):
            eng.dma_start(dst, src).then_inc(s_ld[name], 16)

        def loaded(eng, name):
            eng.wait_ge(s_ld[name], 16 * N_LOADS[name])

        flags = {}

        def flag(name):
            if name not in flags:
                flags[name] = sem("f_" + name)
            return flags[name]

        def done(eng, name):
            eng.drain()
            eng.sem_inc(flag(name), 1)

        def need(eng, name):
            eng.wait_ge(flag(name), 1)

        block = top.enter_context(nc.Block())

        lay_k = [[Pm[0][:, k, 0:HM] for k in range(KC)], [work[2 + k][:, 0:HM] for k in range(KC)]]
        lay_v = [[Pm[1][:, k, :] for k in range(KC)], [lay_v1[:, k, :] for k in range(KC)]]
        utmp = ztile[:, 0:KC, :]

        def mm3(pe, o, a, b, first, last, skip=False):
            pe.matmul(o, a[0], b[0], start=first, stop=False, skip_group_check=skip)
            pe.matmul(o, a[0], b[1], start=False, stop=False, skip_group_check=skip)
            return pe.matmul(o, a[1], b[0], start=False, stop=last, skip_group_check=skip)

        def sub(p2, *ix):
            return p2[0][ix], p2[1][ix]

        def f32(ap):
            return ap.bitcast(F32)

        a_n0 = event("a_n0"); a_t = event("a_t"); a_h = event("a_h"); a_l = event("a_l")
        a_y = event("a_y"); a_v1 = event("a_v1"); a_r1 = event("a_r1"); a_n1 = event("a_n1"); a_g1 = event("a_g1")
        a_s = event("a_s", per=2); a_mx = event("a_mx", per=2); a_ex = event("a_ex", per=2)
        a_rc = event("a_rc"); a_p = event("a_p"); a_tp = event("a_tp"); a_hp = event("a_hp"); a_lp = event("a_lp")
        a_c = event("a_c"); a_z = event("a_z"); a_v2 = event("a_v2"); a_r2 = event("a_r2"); a_n2 = event("a_n2")
        a_g2 = event("a_g2"); a_t2 = event("a_t2"); a_h2 = event("a_h2"); a_l2 = event("a_l2")

        def rsqrt(pool, k, n=1):
            return pool.tensor_tensor(rstd[:, k:k + n], var[:, k:k + n], half[:, 0:n], ALU.pow)

        def stats(dve, src, k, n=1):
            for j in range(n):
                dve.bn_stats(stat[:, k + j, :], src[j])
            dve.drain()
            for j in range(n):
                dve.bn_aggr(mv[:, k + j, :], stat[:, k + j, :])
            dve.drain()
            return dve.tensor_scalar(var[:, k:k + n], mv[:, k:k + n, 1], EPS, None, ALU.add)

        LAG = 5

        def a_step(pe, act, dve, pool, s, par):
            def on(off):
                return not isinstance(s, int) or 0 <= s + off < NT

            def q(off):
                return (par + off) % 2

            TB, YB, SB, PB, CB, T2B = 0, 1, 2, 4, 6, 7

            def x_tile(off):
                return X[:, s + off, :]

            def xt_tile(n, off):
                return XT[n][:, :, bass.ds((s + off) * P, P)]

            t01 = slice(0 if on(0) else 1, 2 if on(1) else 1)
            t01_ps = PS[:, TB, :].rearrange("p (a k t) -> p a k t", a=2, k=KC)[:, t01]
            xt = xt01
            pt_ps = PS[:, PB:PB + 2, 0:HP]
            pt = [PT[n][:, :, :].rearrange("p (j c) t -> p j (c t)", j=2) for n in range(2)]
            t2_ps = PS[:, T2B, 0:D].rearrange("p (k t) -> p k t", k=KC)
            b1 = (s - 1) // TPB
            b3 = (s - 3) // TPB

            if pe:
                if on(-3):
                    a_p.wait(pe, s - 3)
                    a_lp.wait(pe, s - 4)
                    for r in range(2 * NQ):
                        j, k = r // NQ, r % NQ
                        i_ = pe.transpose(PS[:, PB + j, k * P:(k + 1) * P], Pm[q(-3)][:, j, k * P:(k + 1) * P],
                                          ident[:, :])
                    i_.then_inc(a_tp.sem, 1)
                if on(-5):
                    a_n2.wait(pe, s - 5)
                    a_l2.wait(pe, s - 6)
                    for k in range(KC):
                        i_ = pe.transpose(PS[:, T2B, k * P:(k + 1) * P], n2[q(-5)][:, k * P:(k + 1) * P], ident[:, :])
                    i_.then_inc(a_t2.sem, 1)
                if on(0):
                    a_l.wait(pe, s)
                    a_n1.wait(pe, s - 1)
                    for k in range(KC):
                        mm3(pe, PS[:, YB, 0:D], sub(xt, slice(None), 1, k), sub(Mt, slice(None), k), k == 0, False)
                    pe.matmul(PS[:, YB, 0:D], ones[:, :], bias[:, 0:D], start=False, stop=True).then_inc(a_y.sem, 1)
                if on(-1):
                    a_l.wait(pe, s)
                    for j in range(2):
                        a_ex.wait(pe, s - 2, j)
                        for k in range(KC):
                            mm3(pe, PS[:, SB + j, 0:HM], sub(xt, slice(None), 0, k),
                                sub(A, slice(None), b1, k, j), k == 0, False)
                        pe.matmul(PS[:, SB + j, 0:HM], ones[:, :], sbias[:, b1, j, :], start=False, stop=True)\
                          .then_inc(a_s.sem, 1)
                def pv(blocks):
                    for r in blocks:
                        mm3(pe, PS[:, CB, 0:D], sub(PT, slice(None), r), sub(VW, slice(None), b3, r), r == 0, False)

                if on(-3):
                    a_lp.wait(pe, s - 3)
                    a_z.wait(pe, s - 4)
                    pv(range(NQ))
                if on(1) or on(0):
                    if on(0):
                        a_n1.wait(pe, s)
                    if on(1):
                        a_n0.wait(pe, s + 1)
                    a_l.wait(pe, s)
                    for a, src in enumerate((n1[q(0)], n0)):
                        if on(a):
                            for k in range(KC):
                                c0 = (a * KC + k) * P
                                i_ = pe.transpose(PS[:, TB, c0:c0 + P], src[:, k * P:(k + 1) * P], ident[:, :])
                    i_.then_inc(a_t.sem, 1)
                if on(-3):
                    pv(range(NQ, 2 * NQ))
                    pe.matmul(PS[:, CB, 0:D], ones[:, :], bias[:, D:2 * D], start=False, stop=True).then_inc(a_c.sem, 1)
            if act:
                def exps(off, j):
                    a_mx.wait(act, s + off, j)
                    if j == 0:
                        a_tp.wait(act, s + off - 2)
                        a_rc.wait(act, s + off - 1)
                    for g in range(HH):
                        h = j * HH + g
                        act.activation(Pm[q(off)][:, j, g * M:(g + 1) * M], PS[:, SB + j, g * M:(g + 1) * M],
                                       ACT.Exp, bias=mx[:, h:h + 1], accum_out=sm[:, h:h + 1])
                    act.drain()
                    act.sem_inc(a_ex.sem, 1)

                if on(-2):
                    exps(-2, 1)
                if on(-3):
                    a_tp.wait(act, s - 3)
                    a_c.wait(act, s - 4)
                    act.activation(pt[0], pt_ps, ACT.Copy).then_inc(a_hp.sem, 1)
                if on(-5):
                    a_t2.wait(act, s - 5)
                    act.activation(xt_tile(0, -5), t2_ps, ACT.Copy).then_inc(a_h2.sem, 1)
                if on(0):
                    a_r1.wait(act, s)
                    a_t.wait(act, s - 1)
                    a_g1.wait(act, s - 2)
                    act.activation(n1[q(0)], PS[:, YB, 0:D], ACT.Identity, bias=nmr[:, 0:1],
                                   scale=rstd[:, 1:2]).then_inc(a_n1.sem, 1)
                if on(-1):
                    exps(-1, 0)
                if on(1) or on(0):
                    a_t.wait(act, s + 1)
                    a_y.wait(act, s)
                    a_s.wait(act, s - 1, 1)
                    act.activation(xt[0][:, t01], t01_ps, ACT.Copy).then_inc(a_h.sem, 1)
                if on(2):
                    a_t.wait(act, s + 1)
                    act.activation(n0, x_tile(2), ACT.Identity, bias=nmr0[:, bass.ds(s + 2, 1)],
                                   scale=rstd0[:, bass.ds(s + 2, 1)]).then_inc(a_n0.sem, 1)
            if dve:
                if on(-4):
                    a_c.wait(dve, s - 4)
                    a_g1.wait(dve, s - 4)
                    dve.tensor_tensor(x_tile(-4), PS[:, CB, 0:D], x_tile(-4), ALU.add).then_inc(a_z.sem, 1)
                if on(-4):
                    dve.drain()
                    dve.bn_stats(stat[:, 2, :], x_tile(-4))
                if on(-4):
                    dve.drain()
                    dve.bn_aggr(mv[:, 2, :], stat[:, 2, :])
                    dve.drain()
                    dve.tensor_scalar(var[:, 2:3], mv[:, 2, 1:2], EPS, None, ALU.add).then_inc(a_v2.sem, 1)
                if on(0):
                    a_y.wait(dve, s)
                    a_n1.wait(dve, s - 1)
                    stats(dve, [PS[:, YB, 0:D]], 1).then_inc(a_v1.sem, 1)
                if on(-3):
                    a_hp.wait(dve, s - 3)
                    dve.tensor_tensor(pt[1], pt_ps, f32(pt[0]), ALU.subtract).then_inc(a_lp.sem, 1)
                if on(-2):
                    a_ex.wait(dve, s - 2, 1)
                    a_p.wait(dve, s - 3)
                    dve.reciprocal(rc[:, :], sm[:, :]).then_inc(a_rc.sem, 1)
                if on(-1):
                    for j in range(2):
                        a_s.wait(dve, s - 1, j)
                        a_ex.wait(dve, s - 2, j)
                        dve.tensor_reduce(mx[:, j * HH:(j + 1) * HH],
                                          PS[:, SB + j, 0:HM].rearrange("p (g m) -> p g m", g=HH),
                                          AX.X, ALU.max, negate=True).then_inc(a_mx.sem, 1)
                if on(-4):
                    a_r2.wait(dve, s - 4)
                    a_t2.wait(dve, s - 6)
                    a_g2.wait(dve, s - 6)
                    dve.tensor_scalar(n2[q(-4)], x_tile(-4), mv[:, 2, 0:1], rstd[:, 2:3],
                                      ALU.subtract, ALU.mult).then_inc(a_n2.sem, 1)
                if on(-5):
                    a_h2.wait(dve, s - 5)
                    dve.tensor_tensor(xt_tile(1, -5), t2_ps, f32(xt_tile(0, -5)), ALU.subtract)\
                       .then_inc(a_l2.sem, 1)
                if on(1) or on(0):
                    a_h.wait(dve, s + 1)
                    dve.tensor_tensor(xt[1][:, t01], t01_ps, f32(xt[0][:, t01]), ALU.subtract).then_inc(a_l.sem, 1)
            if pool:
                if on(-1):
                    a_n1.wait(pool, s - 1)
                    a_n0.wait(pool, s - 1)
                    pool.tensor_tensor(x_tile(-1), n1[q(-1)], bc[:, R_G1, :], ALU.mult).then_inc(a_g1.sem, 1)
                if on(-4):
                    a_v2.wait(pool, s - 4)
                    a_n2.wait(pool, s - 5)
                    rsqrt(pool, 2).then_inc(a_r2.sem, 1)
                if on(0):
                    a_v1.wait(pool, s)
                    a_n1.wait(pool, s - 1)
                    rsqrt(pool, 1)
                    pool.drain()
                    pool.tensor_scalar(nmr[:, :], mv[:, 1, 0:1], rstd[:, 1:2], -1.0, ALU.mult, ALU.mult)\
                        .then_inc(a_r1.sem, 1)
                if on(-2):
                    a_rc.wait(pool, s - 2)
                    pv = Pm[q(-2)][:, :, 0:HM].rearrange("p j (g m) -> p j g m", g=HH)
                    pool.tensor_tensor(pv, pv, rc[:, :].rearrange("p (j g) -> p j g", j=2).unsqueeze(3)
                                       .to_broadcast([P, 2, HH, M]), ALU.mult).then_inc(a_p.sem, 1)
                if on(-5):
                    a_n2.wait(pool, s - 5)
                    pool.tensor_tensor(x_tile(-5), n2[q(-5)], bc[:, R_G2, :], ALU.mult)\
                        .then_inc(a_g2.sem, 1)

        NPART = 4

        def ffn_weights(act, dve, pool, n):
            k, c1 = n // 2, slice((n % 2) * FF // 2, (n % 2 + 1) * FF // 2)
            f2 = slice(n * NF // NPART, (n + 1) * NF // NPART)
            g2 = col[:, k, C_G2:C_G2 + 1]
            if act:
                loaded(act, "w1")
                loaded(act, "w2")
                act.activation(W1[0][:, k, c1], w1raw[:, k, c1], ACT.Identity, scale=g2)
                act.activation(W2[0][:, f2, :], w2raw[:, f2, :], ACT.Copy)
                done(act, f"whi{n}")
            if dve:
                need(dve, f"whi{n}")
                dve.scalar_tensor_tensor(W1[1][:, k, c1], w1raw[:, k, c1], g2, f32(W1[0][:, k, c1]),
                                         ALU.mult, ALU.subtract)
            if pool:
                need(pool, f"whi{n}")
                pool.tensor_tensor(W2[1][:, f2, :], w2raw[:, f2, :], f32(W2[0][:, f2, :]), ALU.subtract)
                done(pool, f"w2lo{n}")

        def stage_a_tiles(pe, act, dve, pool, sp):
            if pe:
                need(pe, "setup")
            if act:
                need(act, "setup")
                need(act, "ln0")
            if pool:
                need(pool, "setup")
            eng = pe or act or dve or pool
            if not eng:
                return
            if act:
                act.activation(n0, X[:, 0, :], ACT.Identity, bias=nmr0[:, 0:1], scale=rstd0[:, 0:1])\
                   .then_inc(a_n0.sem, 1)
            for s in range(-1, LAG + 1):
                if s == LAG and dve:
                    need(dve, f"w2lo{NPART - 1}")
                a_step(pe, act, dve, pool, s, s % 2)
                if 0 <= s < NPART:
                    ffn_weights(act, dve, pool, s)
            with eng.Fori(LAG + 1, NT - 3, 2) as s:
                a_step(pe, act, dve, pool, s, (LAG + 1) % 2)
                a_step(pe, act, dve, pool, s + 1, LAG % 2)
            for s in range(NT - 2, NT + LAG):
                a_step(pe, act, dve, pool, s, s % 2)

        def tiles4(buf, c):
            return buf[:, bass.ds(c * TPC, TPC), :]

        def norm4(dve, dst, src, k=0):
            for t in range(TPC):
                i_ = dve.tensor_scalar(dst[:, t, :], src(t), mv[:, k + t, 0:1], rstd[:, k + t:k + t + 1],
                                       ALU.subtract, ALU.mult)
            return i_

        def down(pe, u, hp, wd, bank0, n_units, first, brow_ap=None):
            for t in range(TPC):
                o = PS[:, bank0 + t // 2, (t % 2) * D:(t % 2 + 1) * D]
                st = first and t % 2 == 0
                if first and brow_ap is not None:
                    pe.matmul(o, ones[:, :], brow_ap, start=st, stop=False, skip_group_check=True)
                    st = False
                i_ = mm3(pe, o, sub(hp, slice(None), slice(t * P, (t + 1) * P)), wd, st, True, skip=True)
            return i_

        b_g = event("b_g", credit=1); b_a = event("b_a", credit=1); b_l = event("b_l", credit=1); b_d = event("b_d", credit=1)
        b_z = event("b_z", credit=1); b_v3 = event("b_v3", credit=1); b_r3 = event("b_r3", credit=1); b_n3 = event("b_n3", credit=1); b_m3 = event("b_m3", credit=1)
        b_x = event("b_x", credit=1); b_v4 = event("b_v4", credit=1); b_r4 = event("b_r4", credit=1); b_n4 = event("b_n4", credit=1)
        b_t4 = event("b_t4", credit=1); b_h4 = event("b_h4", credit=1); b_l4 = event("b_l4", credit=1)
        b_lg = event("b_lg", credit=1); b_lc = event("b_lc", credit=1); b_lt = event("b_lt", credit=1); b_ex = event("b_ex", credit=1); b_cm = event("b_cm", credit=1)
        s_xr = sem("s_xr"); s_moe = [sem(f"s_moe{k}") for k in range(2)]; g_hi = event("g_hi"); g_moe = event("g_moe")
        s_rw = sem("s_rw"); g_rw = event("g_rw")
        GB, DB, TB, LB, RB = 0, 2, 4, 6, 7

        def b_tail(pe, act, dve, pool, p, f):
            def x_t(t):
                return X[:, p * TPC + t, :]

            ch = bass.ds(p * CH, CH)
            if f == 0:
                if dve:
                    b_d.wait(dve, NF * p + NF - 1)
                    for t in range(TPC):
                        i_ = dve.tensor_tensor(ztile[:, t, :], PS[:, DB + t // 2, (t % 2) * D:(t % 2 + 1) * D],
                                               x_t(t), ALU.add)
                    i_.then_inc(b_z.sem, 1)
                    dve.drain()
                    stats(dve, [ztile[:, t, :] for t in range(TPC)], 0, TPC).then_inc(b_v3.sem, 1)
                if pool:
                    pool.wait_ge(s_xr, 16 * (p + 1))
                    pool.tensor_tensor(xr4[:, :, :], xr4[:, :, :],
                                       bc[:, R_B3:R_B3 + 1, :].to_broadcast([P, TPC, D]), ALU.add)
                    b_v3.wait(pool, p)
                    rsqrt(pool, 0, TPC).then_inc(b_r3.sem, 1)
            if f == 1:
                if dve:
                    b_r3.wait(dve, p)
                    norm4(dve, ztile, lambda t: ztile[:, t, :]).then_inc(b_n3.sem, 1)
                if pool:
                    b_n3.wait(pool, p)
                    pool.tensor_tensor(ztile[:, :, :], ztile[:, :, :],
                                       bc[:, R_G3:R_G3 + 1, :].to_broadcast([P, TPC, D]), ALU.mult)\
                        .then_inc(b_m3.sem, 1)
            if f == 2:
                if dve:
                    b_m3.wait(dve, p)
                    dve.tensor_tensor(tiles4(X, p), ztile[:, :, :], xr4[:, :, :], ALU.add).then_inc(b_x.sem, 1)
                    dve.drain()
                    stats(dve, [x_t(t) for t in range(TPC)], 0, TPC).then_inc(b_v4.sem, 1)
                if pool:
                    b_v4.wait(pool, p)
                    rsqrt(pool, 0, TPC).then_inc(b_r4.sem, 1)
            if f == 3 and dve:
                b_r4.wait(dve, p)
                b_t4.wait(dve, p - 1)
                norm4(dve, ntile, x_t).then_inc(b_n4.sem, 1)
            if f == 4:
                if pe:
                    b_n4.wait(pe, p)
                    b_l4.wait(pe, p - 1)
                    for k in range(KC):
                        for t in range(TPC):
                            i_ = pe.transpose(PS[:, TB + k, t * P:(t + 1) * P], ntile[:, t, k * P:(k + 1) * P],
                                              ident[:, :])
                    i_.then_inc(b_t4.sem, 1)
                if act:
                    b_t4.wait(act, p)
                    for k in range(KC):
                        i_ = act.activation(XT[0][:, k, ch], PS[:, TB + k, :], ACT.Copy)
                    i_.then_inc(b_h4.sem, 1)
                if dve:
                    b_h4.wait(dve, p)
                    for k in range(KC):
                        i_ = dve.tensor_tensor(XT[1][:, k, ch], PS[:, TB + k, :], f32(XT[0][:, k, ch]), ALU.subtract)
                    i_.then_inc(b_l4.sem, 1)
            if f == 5:
                if pe:
                    b_l4.wait(pe, p)
                    b_lc.wait(pe, p - 1)
                    for k in range(KC):
                        i_ = mm3(pe, PS[:, LB, :], sub(gT, slice(None), k), sub(XT, slice(None), k, ch),
                                 k == 0, k == KC - 1)
                    i_.then_inc(b_lg.sem, 1)
                if act:
                    b_lg.wait(act, p)
                    b_lt.wait(act, p - 1)
                    act.activation(lgT[:, :], PS[:, LB, :], ACT.Copy).then_inc(b_lc.sem, 1)
            if f == 6:
                if pe:
                    b_lc.wait(pe, p)
                    b_ex.wait(pe, p - 1)
                    for t in range(TPC):
                        i_ = pe.transpose(PS[:, RB, t * P:(t + 1) * P], lgT[:, t * P:(t + 1) * P], ident[:, :])
                    i_.then_inc(b_lt.sem, 1)
                if act:
                    b_lt.wait(act, p)
                    b_cm.wait(act, p - 1)
                    act.activation(ex[:, :, :], PS[:, RB, :].rearrange("p (t e) -> p t e", t=TPC)[:, :, 0:E], ACT.Exp,
                                   scale=-1.0).then_inc(b_ex.sem, 1)
            if f == 7 and dve:
                b_ex.wait(dve, p)
                dve.tensor_scalar(sc[:, :, :], ex[:, :, :], 1.0, None, ALU.add)
                dve.drain()
                dve.reciprocal(sc[:, :, :], sc[:, :, :])
                dve.drain()
                for t in range(TPC):
                    dve.max(top8[:, t, :], sc[:, t, :])
                dve.drain()
                for t in range(TPC):
                    dve.max_index(idx8[:, t, :], top8[:, t, :], sc[:, t, :])
                dve.tensor_tensor(tsum[:, :], top8[:, :, 0], top8[:, :, 1], ALU.add)
                dve.drain()
                dve.tensor_copy(idxf[:, :, 0:2], idx8[:, :, 0:2])
                dve.tensor_scalar(tsum[:, :], tsum[:, :], 1e-20, None, ALU.add)
                dve.drain()
                dve.reciprocal(tsum[:, :], tsum[:, :])
                dve.drain()
                for n in range(2):
                    dve.scalar_tensor_tensor(tw[:, :, n], top8[:, :, n], ROUTE_SCALE, tsum[:, :], ALU.mult, ALU.mult)
                dve.drain()
                for t in range(TPC):
                    dve.tensor_scalar(oh[:, t, :], iota[:, :], idxf[:, t, 1:2], tw[:, t, 1:2], ALU.is_equal, ALU.mult)
                    dve.tensor_scalar(ex[:, t, :], iota[:, :], idxf[:, t, 0:1], tw[:, t, 0:1], ALU.is_equal, ALU.mult)
                dve.drain()
                dve.tensor_tensor(tiles4(cmb, p), oh[:, :, :], ex[:, :, :], ALU.add).then_inc(b_cm.sem, 1)

        guv = gu.rearrange("(k p) (n c) -> p k n c", p=P, n=NU)
        dnv = dn.rearrange("(n p) d -> p n d", p=P)

        def split_unit(act, pool, sp, n, q):
            raw_, hi, lo = moe_raw[q], GU[0], GU[1]
            cols_ = bass.ds(n * 2 * I, 2 * I)
            if act:
                act.wait_ge(s_moe[q], 48 * (n // 2) + 48)
                act.activation(hi[:, :, cols_], raw_[:, 0:KC, :], ACT.Copy)
                act.activation(DN[0][:, bass.ds(n, 1), :], raw_[:, KC:KC + 1, :], ACT.Copy).then_inc(g_hi.sem, 1)
            if pool:
                g_hi.wait(pool, n)
                pool.tensor_tensor(lo[:, :, cols_], raw_[:, 0:KC, :], f32(hi[:, :, cols_]), ALU.subtract)
                pool.tensor_tensor(DN[1][:, bass.ds(n, 1), :], raw_[:, KC:KC + 1, :],
                                   f32(DN[0][:, bass.ds(n, 1), :]), ALU.subtract).then_inc(g_moe.sem, 1)
            if sp:
                g_moe.wait(sp, n - 2)
                for k in range(KC):
                    sp.dma_start(raw_[:, k, :], guv[:, k, bass.ds(n, 1), :]).then_inc(s_moe[q], 16)
                sp.dma_start(raw_[:, KC, :], dnv[:, bass.ds(n, 1), :]).then_inc(s_moe[q], 16)

        def b_chunk(pe, act, dve, pool, sp, c, tail):
            for f in range(NF):
                u = NF * c + f
                if pe:
                    b_a.wait(pe, u - 2)
                    for k in range(KC):
                        i_ = mm3(pe, PS[:, GB + f % 2, :], sub(W1, slice(None), k, slice(f * P, (f + 1) * P)),
                                 sub(XT, slice(None), k, bass.ds(c * CH, CH)), k == 0, k == KC - 1)
                    i_.then_inc(b_g.sem, 1)
                if act:
                    b_g.wait(act, u)
                    b_l.wait(act, u - 2)
                    act.activation(work[f % 2][:, :], PS[:, GB + f % 2, :], ACT.Relu, bias=b1col[:, f:f + 1])\
                        .then_inc(b_a.sem, 1)
                if dve:
                    b_a.wait(dve, u)
                    b_d.wait(dve, u - 2)
                    dve.tensor_copy(hid[f % 2][0][:, :], work[f % 2][:, :])
                    dve.drain()
                    dve.tensor_tensor(hid[f % 2][1][:, :], work[f % 2][:, :], f32(hid[f % 2][0][:, :]), ALU.subtract)\
                        .then_inc(b_l.sem, 1)
                if pe and (tail or f):
                    b_down(pe, c, f)
                if tail:
                    b_tail(pe, act, dve, pool, c - 1, f)
                if sp and tail and f == NF // 2:
                    b_x.wait(sp, c - 1)
                    sp.dma_start(xr4[:, :, :], xv[:, bass.ds(c * TPC, TPC), :]).then_inc(s_xr, 16)
                if tail and f in (3, 6):
                    n = 2 * c + 2 + f // 6
                    split_unit(act, pool, sp, n, f // 6)
                elif not tail and f % 2:
                    split_unit(act, pool, sp, f // 2, (f // 2) % 2)

        def b_down(pe, c, f):
            g = (f - 1) % NF
            b_l.wait(pe, NF * c + f - 1)
            if g == 0:
                b_z.wait(pe, c - 1)
            down(pe, 0, hid[g % 2], sub(W2, slice(None), g), DB, NF, g == 0, b2row[:, :]).then_inc(b_d.sem, 1)

        def stage_b(pe, act, dve, pool, sp):
            if sp:
                a_g2.wait(sp, NT - 1); a_c.wait(sp, NT - 1); a_l2.wait(sp, NT - 1)
                sp.dma_start(xr4[:, :, :], xv[:, 0:TPC, :]).then_inc(s_xr, 16)
            if pool:
                a_c.wait(pool, NT - 1); a_l2.wait(pool, NT - 1); a_t2.wait(pool, NT - 1)
                pool.memset(selraw[:, :, :], 0.0)
                pool.drain()
                pool.affine_select(out=selraw[:, :, :], in_=selraw[:, :, :], compare_op=ALU.not_equal, fill=1.0,
                                   base=0, pattern=[[-1, E], [0, P]], channel_multiplier=1)
                pool.drain()
                pool.tensor_copy(sel[:, :, :], selraw[:, :, :])
            if act:
                a_c.wait(act, NT - 1)
            if pe:
                a_l2.wait(pe, NT - 1)
            if dve:
                a_g2.wait(dve, NT - 1); a_t2.wait(dve, NT - 1)
            eng = pe or act or dve or pool or sp
            b_chunk(pe, act, dve, pool, sp, 0, False)
            with eng.Fori(1, NCH) as c:
                b_chunk(pe, act, dve, pool, sp, c, True)
            if pe:
                b_down(pe, NCH, 0)
            for f in range(NF):
                b_tail(pe, act, dve, pool, NCH - 1, f)

        c_g = event("c_g", credit=1); c_s = event("c_s", credit=1); c_uo = event("c_uo", credit=1); c_m = event("c_m", credit=1); c_l = event("c_l", credit=1)
        c_d = event("c_d", credit=1); c_bc = event("c_bc", credit=1)
        c_cs = event("c_cs", credit=1); c_ct = event("c_ct", credit=1); c_ch = event("c_ch", credit=1); c_cl = event("c_cl", credit=1)
        c_x = event("c_x", credit=1); c_v = event("c_v", credit=1); c_r = event("c_r", credit=1); c_n = event("c_n", credit=1)
        c_t = event("c_t", credit=1); c_h = event("c_h", credit=1); c_lo = event("c_lo", credit=1)
        CG, CU, CD, CB, CT = 0, 2, 4, 6, 7
        NR = E

        def c_tail(pe, act, dve, pool, p, j):
            def x_t(t):
                return X[:, p * TPC + t, :]

            ch = bass.ds(p * CH, CH)
            if j == 0:
                if dve:
                    c_d.wait(dve, NU * p + NU - 1)
                    for t in range(TPC):
                        i_ = dve.scalar_tensor_tensor(x_t(t), PS[:, CD + t // 2, (t % 2) * D:(t % 2 + 1) * D],
                                                      tg[:, 2:3], x_t(t), ALU.mult, ALU.add)
                    i_.then_inc(c_x.sem, 1)
                    dve.drain()
                    stats(dve, [x_t(t) for t in range(TPC)], 0, TPC).then_inc(c_v.sem, 1)
                if pool:
                    c_v.wait(pool, p)
                    rsqrt(pool, 0, TPC).then_inc(c_r.sem, 1)
            if j == 1 and dve:
                c_r.wait(dve, p)
                c_t.wait(dve, 2 * p - 1)
                norm4(dve, ntile, x_t).then_inc(c_n.sem, 1)
            if j in (2, 3):
                k = j - 2
                if pe:
                    if k == 0:
                        c_n.wait(pe, p)
                        c_cl.wait(pe, NCH - 1 if isinstance(p, int) else p + 1)
                    else:
                        c_lo.wait(pe, 2 * p)
                    for t in range(TPC):
                        i_ = pe.transpose(PS[:, CT, t * P:(t + 1) * P], ntile[:, t, k * P:(k + 1) * P], ident[:, :])
                    i_.then_inc(c_t.sem, 1)
                if act:
                    c_t.wait(act, 2 * p + k)
                    act.activation(XT[0][:, k, ch], PS[:, CT, :], ACT.Copy).then_inc(c_h.sem, 1)
                if dve:
                    c_h.wait(dve, 2 * p + k)
                    dve.tensor_tensor(XT[1][:, k, ch], PS[:, CT, :], f32(XT[0][:, k, ch]), ALU.subtract)\
                        .then_inc(c_lo.sem, 1)

        def c_down(pe, c, j):
            g = (j - 1) % NU
            c_l.wait(pe, NU * c + j - 1)
            if g == 0:
                c_x.wait(pe, c - 1)
            down(pe, 0, hid[g % 2], sub(DN, slice(None), g), CD, NU, g == 0).then_inc(c_d.sem, 1)

        def c_chunk(pe, act, dve, pool, c, tail):
            if dve:
                c_ct.wait(dve, c - 1)
                dve.tensor_copy(cst[:, :, :], tiles4(cmb, c)).then_inc(c_cs.sem, 1)
            if pe:
                c_cs.wait(pe, c)
                c_lo.wait(pe, 2 * c - 3)
                for t in range(TPC):
                    i_ = pe.transpose(PS[0:E, CT, t * P:(t + 1) * P], cst[:, t, :], ident[:, :])
                i_.then_inc(c_ct.sem, 1)
            if act:
                c_ct.wait(act, c)
                c_bc.wait(act, NR * c - 1)
                act.activation(cT[0][:, :], PS[0:E, CT, :], ACT.Copy).then_inc(c_ch.sem, 1)
            if dve:
                c_ch.wait(dve, c)
                dve.tensor_tensor(cT[1][:, :], PS[0:E, CT, :], f32(cT[0][:, :]), ALU.subtract).then_inc(c_cl.sem, 1)
            ch = bass.ds(c * CH, CH)
            for j in range(NU):
                u = NU * c + j
                e = j - 2
                v = NR * c + e
                q = j % 2
                if pe:
                    c_s.wait(pe, u - 2)
                    c_l.wait(pe, u - 2)
                    for half_, bank in ((0, CG), (1, CU)):
                        w0 = (2 * j + half_) * I
                        for k in range(KC):
                            i_ = mm3(pe, PS[:, bank + q, :], sub(GU, slice(None), k, slice(w0, w0 + I)),
                                     sub(XT, slice(None), k, ch), k == 0, k == KC - 1)
                        i_.then_inc((c_g if half_ == 0 else c_uo).sem, 1)
                    if e >= 0:
                        c_cl.wait(pe, c)
                        c_m.wait(pe, v - 1)
                        pe.matmul(PS[:, CB, :], sel[:, e, :], cT[0][:, :], start=True, stop=False)
                        pe.matmul(PS[:, CB, :], sel[:, e, :], cT[1][:, :], start=False, stop=True)\
                            .then_inc(c_bc.sem, 1)
                if act:
                    c_g.wait(act, u)
                    c_l.wait(act, u - 2)
                    act.activation(work[q][:, :], PS[:, CG + q, :], ACT.Silu).then_inc(c_s.sem, 1)
                if dve:
                    c_s.wait(dve, u)
                    c_uo.wait(dve, u)
                    hv = work[2 + q]
                    dve.tensor_tensor(hv[:, :], PS[:, CU + q, :], work[q][:, :], ALU.mult)
                    dve.drain()
                    if e >= 0:
                        c_bc.wait(dve, v)
                        dve.tensor_tensor(hv[:, :], PS[:, CB, :], hv[:, :], ALU.mult).then_inc(c_m.sem, 1)
                        dve.drain()
                    c_d.wait(dve, u - 2)
                    dve.tensor_copy(hid[q][0][:, :], hv[:, :])
                    dve.drain()
                    dve.tensor_tensor(hid[q][1][:, :], hv[:, :], f32(hid[q][0][:, :]), ALU.subtract)\
                        .then_inc(c_l.sem, 1)
                if pe and (tail or j):
                    c_down(pe, c, j)
                if tail:
                    c_tail(pe, act, dve, pool, c - 1, j)

        def stage_c(pe, act, dve, pool, sp):
            if sp:
                for k in range(KC):
                    g_moe.wait(sp, NU - 1)
                    if k:
                        g_rw.wait(sp, k - 1)
                    sp.dma_start(moe_raw[0][:, :, :], rw[k * P:(k + 1) * P, :].rearrange("p (a d) -> p a d", a=3))\
                        .then_inc(s_rw, 16)
            if pool:
                b_g.wait(pool, NF * NCH - 1)
                for k in range(KC):
                    pool.wait_ge(s_rw, 16 * (k + 1))
                    hi, lo = (W1[n][:, k, 0:3 * D].rearrange("p (a d) -> p a d", a=3) for n in range(2))
                    pool.tensor_copy(hi, moe_raw[0][:, :, :])
                    pool.drain()
                    pool.tensor_tensor(lo, moe_raw[0][:, :, :], f32(hi), ALU.subtract)
                    pool.drain()
                    pool.sem_inc(g_rw.sem, 1)
            if pe:
                g_moe.wait(pe, NU - 1)
                b_l4.wait(pe, NCH - 1)
                b_cm.wait(pe, NCH - 1)
            if act:
                act.activation(warm[:, :], tg[:, 0:1], ACT.Silu)
            eng = pe or act or dve or pool
            if not eng:
                return
            c_chunk(pe, act, dve, pool, 0, False)
            with eng.Fori(1, NCH) as c:
                c_chunk(pe, act, dve, pool, c, True)
            if pe:
                c_down(pe, NCH, 0)
            for j in range(4):
                c_tail_last(pe, act, dve, pool, NCH - 1, j)

        def c_tail_last(pe, act, dve, pool, p, j):
            c_tail(pe, act, dve, pool, p, j)

        d_b = event("d_b", credit=1); d_s = event("d_s", credit=1); d_mx = event("d_mx", credit=1); d_ex = event("d_ex", credit=1); d_at = event("d_at", credit=1)
        d_o = event("d_o", credit=1); d_z = event("d_z", credit=2); d_v = event("d_v", credit=1); d_r = event("d_r", credit=1); d_n = event("d_n", credit=1)
        d_t = event("d_t", credit=2); d_xd = event("d_xd", credit=1)
        s_zero = event("s_zero")

        def d_batch(pe, act, dve, pool, b):
            if dve:
                d_s.wait(dve, b - 1)
                for n in range(2):
                    dve.tensor_copy(Bst[n][:, :, :], f32(Bctx[n][:, :, bass.ds(b * M, M)]))
                dve.drain()
                dve.sem_inc(d_b.sem, 1)
            if pe:
                d_b.wait(pe, b)
                d_ex.wait(pe, b - 1)
                for j in range(2):
                    for k in range(KC):
                        i_ = mm3(pe, PS[0:M, j, :], sub(Bst, slice(None), k),
                                 sub(XT, slice(None), k, bass.ds(b * S + j * CH, CH)), k == 0, k == KC - 1)
                i_.then_inc(d_s.sem, 1)
            if dve:
                d_s.wait(dve, b)
                d_ex.wait(dve, b - 1)
                dve.tensor_reduce(nmax[:, :], PS[0:M, 0:2, :], AX.XY, ALU.max, negate=True).then_inc(d_mx.sem, 1)
            if act:
                d_mx.wait(act, b)
                d_at.wait(act, b - 1)
                act.activation(att[:, :].rearrange("m (j t) -> m j t", j=2), PS[0:M, 0:2, :], ACT.Exp,
                               bias=nmax[:, 0:1], accum_out=asum[:, 0:1])
                act.drain()
                act.sem_inc(d_ex.sem, 1)
            if dve:
                d_ex.wait(dve, b)
                d_o.wait(dve, 2 * b - 1)
                dve.reciprocal(ascl[:, :], asum[:, :])
                dve.tensor_copy(attp[0][:, :], att[:, :])
                dve.drain()
                dve.tensor_tensor(ascl[:, :], ascl[:, :], tg[0:M, 1:2], ALU.mult)
                dve.tensor_tensor(attp[1][:, :], att[:, :], f32(attp[0][:, :]), ALU.subtract)
                dve.drain()
                dve.tensor_scalar(c2f[:, :], C2[:, b, :], ascl[:, 0:1], None, ALU.mult)
                dve.drain()
                dve.tensor_copy(c2s[0][:, :], c2f[:, :])
                dve.drain()
                dve.tensor_tensor(c2s[1][:, :], c2f[:, :], f32(c2s[0][:, :]), ALU.subtract)
                dve.drain()
                dve.sem_inc(d_at.sem, 1)
            for g in range(2):
                c = 2 * b + g
                bank = 2 if g == 0 else 6
                if pe:
                    d_at.wait(pe, b)
                    d_z.wait(pe, c - 2)
                    for t in range(TPC):
                        tok = slice((g * TPC + t) * P, (g * TPC + t + 1) * P)
                        i_ = mm3(pe, PS[:, bank + t // 2, (t % 2) * D:(t % 2 + 1) * D],
                                 sub(attp, slice(None), tok), sub(c2s, slice(None), slice(None)), True, True)
                    i_.then_inc(d_o.sem, 1)
            for g in range(2):
                c = 2 * b + g
                bank = 2 if g == 0 else 6
                if dve:
                    d_o.wait(dve, c)
                    for t in range(TPC):
                        xt_ = X[:, c * TPC + t, :]
                        i_ = dve.tensor_tensor(xt_, PS[:, bank + t // 2, (t % 2) * D:(t % 2 + 1) * D], xt_, ALU.add)
                    i_.then_inc(d_z.sem, 1)
                    dve.drain()
                    stats(dve, [X[:, c * TPC + t, :] for t in range(TPC)], TPC * g, TPC).then_inc(d_v.sem, 1)
                if pool:
                    d_v.wait(pool, c)
                    rsqrt2(pool, TPC * g).then_inc(d_r.sem, 1)
            for g in range(2):
                c = 2 * b + g
                nt_ = ntile if g == 0 else ztile
                if dve:
                    d_r.wait(dve, c)
                    d_t.wait(dve, c - 2)
                    norm4(dve, nt_, lambda t: X[:, c * TPC + t, :], TPC * g).then_inc(d_n.sem, 1)
                if pe:
                    d_n.wait(pe, c)
                    d_xd.wait(pe, c - 1)
                    for k in range(KC):
                        for t in range(TPC):
                            i_ = pe.transpose(PS[:, 4 + k, t * P:(t + 1) * P], nt_[:, t, k * P:(k + 1) * P],
                                              ident[:, :])
                    i_.then_inc(d_t.sem, 1)
                if act:
                    d_t.wait(act, c)
                    for k in range(KC):
                        i_ = act.activation(XD[:, k, bass.ds(b * (S + 1) + 1 + g * CH, CH)], PS[:, 4 + k, :], ACT.Copy)
                    i_.then_inc(d_xd.sem, 1)

        def rsqrt2(pool, k):
            return pool.tensor_tensor(rstd[:, k:k + TPC], var[:, k:k + TPC], half[:, 0:TPC], ALU.pow)

        def stage_d(pe, act, dve, pool, sp):
            if pe:
                c_lo.wait(pe, 2 * NCH - 1)
            if dve:
                c_d.wait(dve, NU * NCH - 1)
                for b in range(B):
                    i_ = dve.memset(XD[:, :, b * (S + 1):b * (S + 1) + 1], 0.0)
                i_.then_inc(s_zero.sem, 1)
            if act:
                c_d.wait(act, NU * NCH - 1)
                act.activation(warm[:, :], tg[:, 0:1], ACT.Exp)
            eng = pe or act or dve or pool
            if not eng:
                return
            with eng.Fori(0, B) as b:
                d_batch(pe, act, dve, pool, b)

        e_df = event("e_df", credit=1); e_mx = event("e_mx", credit=1); e_xh = event("e_xh", credit=1); e_xl = event("e_xl", credit=1)
        e_k = event("e_k", credit=1); e_s = event("e_s", credit=1); e_kl = event("e_kl", credit=1); e_r = event("e_r", credit=1); e_sg = event("e_sg", credit=1)
        e_vo = event("e_vo", credit=1); e_o = event("e_o", credit=1); e_st = [sem(f"e_st{g}") for g in range(2)]
        EK, ER, EV = 0, 2, 4

        def e_chunk(pe, act, dve, pool, sp, b, g):
            c = 2 * b + g
            off = b * (S + 1) + g * CH
            rs = work[2:4]
            if pool:
                e_mx.wait(pool, 2 * c - 1)
                pool.tensor_tensor(dif[:, :, :], XD[:, :, bass.ds(off + 1, CH)], XD[:, :, bass.ds(off, CH)],
                                   ALU.subtract).then_inc(e_df.sem, 1)
            for n, cc in ((1, C_MUK), (0, C_MUR)):
                m = 2 * c + 1 - n
                if dve:
                    e_df.wait(dve, c)
                    for k in range(KC):
                        i_ = dve.scalar_tensor_tensor(xmix[n][:, k, :], dif[:, k, :], col[:, k, cc:cc + 1],
                                                      XD[:, k, bass.ds(off, CH)], ALU.mult, ALU.add)
                    i_.then_inc(e_mx.sem, 1)
                if act:
                    e_mx.wait(act, m)
                    (e_k if n else e_r).wait(act, c - 1)
                    act.activation(xm[n][0][:, :, :], xmix[n][:, :, :], ACT.Copy).then_inc(e_xh.sem, 1)
                if dve:
                    e_xh.wait(dve, m)
                    dve.tensor_tensor(xm[n][1][:, :, :], xmix[n][:, :, :], f32(xm[n][0][:, :, :]), ALU.subtract)\
                        .then_inc(e_xl.sem, 1)
            if pe:
                e_xl.wait(pe, 2 * c)
                e_s.wait(pe, c - 1)
                for f in range(KC):
                    for k in range(KC):
                        i_ = mm3(pe, PS[:, EK + f, :], sub(W1, slice(None), k, slice(D + f * P, D + (f + 1) * P)),
                                 sub(xm[1], slice(None), k), k == 0, k == KC - 1)
                i_.then_inc(e_k.sem, 1)
                e_xl.wait(pe, 2 * c + 1)
                e_sg.wait(pe, c - 1)
                for t in range(TPC):
                    for k in range(KC):
                        i_ = mm3(pe, PS[:, ER + t // 2, (t % 2) * D:(t % 2 + 1) * D],
                                 sub(xm[0], slice(None), k, slice(t * P, (t + 1) * P)),
                                 sub(W1, slice(None), k, slice(0, D)), k == 0, k == KC - 1)
                i_.then_inc(e_r.sem, 1)
            if act:
                e_k.wait(act, c)
                e_kl.wait(act, c - 1)
                for f in range(KC):
                    i_ = act.activation(work[f][:, :], PS[:, EK + f, :], ACT.Relu)
                i_.then_inc(e_s.sem, 1)
                e_r.wait(act, c)
                e_o.wait(act, c - 1)
                for q in range(2):
                    i_ = act.activation(rs[q][:, :], PS[:, ER + q, :], ACT.Sigmoid)
                i_.then_inc(e_sg.sem, 1)
            if dve:
                e_s.wait(dve, c)
                e_vo.wait(dve, c - 1)
                for f in range(KC):
                    dve.tensor_tensor(work[f][:, :], work[f][:, :], work[f][:, :], ALU.mult)
                dve.drain()
                for f in range(KC):
                    dve.tensor_copy(ka[0][:, f, :], work[f][:, :])
                dve.drain()
                for f in range(KC):
                    i_ = dve.tensor_tensor(ka[1][:, f, :], work[f][:, :], f32(ka[0][:, f, :]), ALU.subtract)
                i_.then_inc(e_kl.sem, 1)
            if pe:
                e_kl.wait(pe, c)
                e_o.wait(pe, c - 1)
                for t in range(TPC):
                    for f in range(KC):
                        i_ = mm3(pe, PS[:, EV + t // 2, (t % 2) * D:(t % 2 + 1) * D],
                                 sub(ka, slice(None), f, slice(t * P, (t + 1) * P)),
                                 sub(W1, slice(None), f, slice(2 * D, 3 * D)), f == 0, f == KC - 1)
                i_.then_inc(e_vo.sem, 1)
            ot = ztile if g == 0 else ntile
            if dve:
                e_vo.wait(dve, c)
                e_sg.wait(dve, c)
                dve.wait_ge(e_st[g], 16 * b + 16)
                for q in range(2):
                    dve.tensor_tensor(rs[q][:, :], PS[:, EV + q, :], rs[q][:, :], ALU.mult)
                dve.drain()
                for q in range(2):
                    i_ = dve.scalar_tensor_tensor(ot[:, 2 * q:2 * q + 2, :],
                                                  rs[q][:, :].rearrange("p (a d) -> p a d", a=2), tg[:, 3:4],
                                                  X[:, bass.ds(c * TPC + 2 * q, 2), :], ALU.mult, ALU.add)
                i_.then_inc(e_o.sem, 1)
            if sp:
                e_o.wait(sp, c)
                sp.dma_start(ov[:, bass.ds(c * TPC, TPC), :], ot[:, :, :]).then_inc(e_st[g], 16)

        def stage_e(pe, act, dve, pool, sp):
            if pool:
                s_zero.wait(pool, 0)
                d_xd.wait(pool, NCH - 1)
            if pe:
                g_rw.wait(pe, KC - 1)
            if act:
                act.activation(warm[:, :], tg[:, 0:1], ACT.Sigmoid)
            if dve:
                d_t.wait(dve, NCH - 1)
                d_xd.wait(dve, NCH - 1)
            eng = pe or act or dve or pool or sp
            with eng.Fori(0, B) as b:
                for g in range(2):
                    e_chunk(pe, act, dve, pool, sp, b, g)
            if sp:
                for g in range(2):
                    sp.wait_ge(e_st[g], 16 * B + 16)


        def program(pe, act, dve, pool, sp):
            if sp:
                for ev in events:
                    if ev.credit:
                        sp.sem_inc(ev.sem, ev.credit)
                for g in range(2):
                    sp.sem_inc(e_st[g], 16)
                rawv = raw.rearrange("(k p) n -> p k n", p=P)
                load(sp, "kv", ctx_sb[:, :, :], ctxT.rearrange("(k p) n -> p k n", p=P))
                load(sp, "kv", rawA[:, :, 0:2 * D], rawv[:, :, 0:2 * D])
                load(sp, "m", rawA[:, :, 2 * D:4 * D], rawv[:, :, 2 * D:4 * D])
                load(sp, "m", ntile[0:1, :, :], brow[0:4, :].rearrange("(a n) d -> a n d", a=1))
                load(sp, "m", ztile[0:1, 3, :], brow[4:5, :])
                load(sp, "q", rawA[:, :, 4 * D:6 * D], rawv[:, :, 4 * D:6 * D])
                load(sp, "x", X[:, :, :], xv)
                load(sp, "e", rawA[:, :, 6 * D:8 * D], rawv[:, :, 6 * D:8 * D])
                load(sp, "e", gT_raw[:, :, :], gateT.rearrange("(k p) n -> p k n", p=P))
                load(sp, "w1", w1raw[:, :, :], w1.rearrange("(k p) n -> p k n", p=P))
                load(sp, "w1", b1col[:, :], l1b)
                load(sp, "w2", w2raw[:, :, :], w2.rearrange("p (f d) -> p f d", f=NF))
            if act:
                load(act, "col", col[:, :, :], cols.rearrange("(k p) n -> p k n", p=P))
                load(act, "bc", gate_raw[:, :], gates.rearrange("(a n) -> a n", a=1).to_broadcast([P, 4]))
                load(act, "bc", bc[:, :, :], bcast.rearrange("(a n) d -> a n d", a=1).to_broadcast([P, NBC, D]))
            if pool:
                pool.memset(ident[:, :], 0.0)
                pool.memset(f32(ones[:, :]), 0.0)
                pool.memset(half[:, :], -0.5)
                for n in range(2):
                    pool.memset(Pm[n][:, :, :], 0.0)
                    pool.memset(work[2 + n][:, :], 0.0)
                pool.memset(lay_v1[:, :, :], 0.0)
                pool.memset(f32(bias[:, :]), 0.0)
                pool.memset(f32(sbias[:, :, :, :]), 0.0)
                pool.memset(f32(b2row[:, :]), 0.0)
                pool.memset(rstd0[:, :], -0.5)
                for n in range(2):
                    pool.memset(f32(gT[n][:, :, E:P]), 0.0)
                pool.iota(iota[:, :], [[1, E]], base=0, channel_multiplier=0, allow_small_or_imprecise_dtypes=True)
                pool.drain()
                pool.memset(f32(ones[0:1, :]), 1.0)
                pool.memset(f32(ones[32:33, :]), 1.0)
                pool.drain()
                pool.affine_select(out=ident[:, :], in_=ident[:, :], compare_op=ALU.not_equal, fill=1.0,
                                   base=0, pattern=[[-1, P]], channel_multiplier=1)
                done(pool, "const")

            def w(k, which, j):
                return rawA[:, k, which * D + j * P: which * D + (j + 1) * P]

            def wrow(k, which):
                return rawA[:, k, which * D:(which + 1) * D]

            brow_raw = [ntile[0:1, n, :] for n in range(4)] + [ztile[0:1, 3, :]]
            brow_sum = [brow_raw[BR_SO], brow_raw[BR_O], brow_raw[BR_F2]]
            kv = work
            scale = float(DH) ** -0.5
            A0B, VWB, MB, C2B = 4, 0, 2, 3

            def row_banks(p, b):
                return [(PS[p, A0B + 2 * j + k, HM:HM + 2 * M], (b, k, slice(j * 2 * M, (j + 1) * 2 * M)))
                        for k in range(2) for j in range(KC)]

            if pe:
                need(pe, "const")
                loaded(pe, "kv")
                for j in range(KC):
                    for which, c0 in ((W_K, 0), (W_VM, B * M)):
                        for k in range(KC):
                            pe.matmul(PS[:, j, c0:c0 + B * M], w(k, which, j), ctx_sb[:, k, :],
                                      start=(k == 0), stop=(k == KC - 1))
                done(pe, "kv_ps")
                loaded(pe, "m")
                loaded(pe, "col")
                for j in range(KC):
                    for k in range(KC):
                        pe.matmul(PS[:, MB, j * D:(j + 1) * D], w(k, W_V, j), wrow(k, W_SO),
                                  start=(k == 0), stop=(k == KC - 1))
                for k in range(KC):
                    pe.matmul(PS[0:1, MB + 1, 0:D], col[:, k, C_BV:C_BV + 1], wrow(k, W_SO),
                              start=(k == 0), stop=(k == KC - 1))
                done(pe, "m_ps")
                loaded(pe, "q")
                for b in range(B):
                    need(pe, f"layk{b}")
                    if b:
                        need(pe, "a0_sb")
                    for j in range(KC):
                        for k in range(2):
                            pe.matmul(PS[:, A0B + 2 * j + k, 0:HM], w(k, W_Q, j), lay_k[b][k][:, 0:HM],
                                      start=True, stop=True)
                    need(pe, "u")
                    for k in range(2):
                        for j in range(KC):
                            pe.matmul(PS[0:1, A0B + 2 * j + k, HM:HM + 2 * M], ucol[:, k:k + 1],
                                      lay_k[b][k][:, j * 2 * M:(j + 1) * 2 * M], start=True, stop=True)
                    done(pe, f"a{b}_ps")
                    need(pe, f"layv{b}")
                    need(pe, "vw0_sb" if b else "m_sb")
                    for r in range(2 * NQ):
                        j, q = r // NQ, r % NQ
                        pe.matmul(PS[:, VWB + r // 2, (r % 2) * D:(r % 2 + 1) * D],
                                  lay_v[b][j][:, q * P:(q + 1) * P], wrow(j, W_O), start=True, stop=True)
                    done(pe, f"vw{b}_ps")
                    if b == 0:
                        loaded(pe, "e")
                        for b_ in range(B):
                            for k in range(KC):
                                pe.matmul(PS[0:M, C2B, b_ * D:(b_ + 1) * D], ctx_sb[:, k, b_ * M:(b_ + 1) * M],
                                          wrow(k, W_2), start=(k == 0), stop=(k == KC - 1))
                        done(pe, "c2_ps")
                need(pe, "c2_sb")
                for j in range(KC):
                    for k in range(KC):
                        pe.matmul(PS[:, C2B, j * B * M:(j + 1) * B * M], w(k, W_E, j), ctx_sb[:, k, :],
                                  start=(k == 0), stop=(k == KC - 1))
                loaded(pe, "w1")
                for f in range(NF):
                    for k in range(KC):
                        pe.matmul(PS[:, C2B, KC * B * M + f:KC * B * M + f + 1], w1raw[:, k, f * P:(f + 1) * P],
                                  col[:, k, C_B2:C_B2 + 1], start=(k == 0), stop=(k == KC - 1))
                done(pe, "l1_ps")

            def lay_out(eng, lay, n, b, name):
                for k in range(KC):
                    for h in range(HH):
                        r = slice(h * DH, (h + 1) * DH)
                        eng.tensor_copy(lay[b][k][r, h * M:(h + 1) * M], kv[k][r, (n * B + b) * M:(n * B + b + 1) * M])
                done(eng, name)

            if dve:
                need(dve, "const")
                loaded(dve, "col")
                need(dve, "kv_ps")
                for k in range(KC):
                    dve.tensor_scalar(kv[k][:, 0:B * M], PS[:, k, 0:B * M], col[:, k, C_BK:C_BK + 1],
                                      scale, ALU.add, ALU.mult)
                for k in range(KC):
                    dve.tensor_scalar(kv[k][:, B * M:2 * B * M], PS[:, k, B * M:2 * B * M],
                                      col[:, k, C_BVM:C_BVM + 1], None, ALU.add)
                done(dve, "kv_sb")
                lay_out(dve, lay_k, 0, 0, "layk0")
                loaded(dve, "q")
                loaded(dve, "bc")
                for k in range(KC):
                    dve.tensor_tensor(utmp[:, k, :], wrow(k, W_Q), bc[:, R_B1, :], ALU.mult)
                dve.drain()
                dve.tensor_reduce(ucol[:, :], utmp[:, :, :], AX.X, ALU.add)
                dve.drain()
                dve.tensor_tensor(ucol[:, :], ucol[:, :], col[:, :, C_BQ], ALU.add)
                done(dve, "u")
                need(dve, "m_ps")
                loaded(dve, "m")
                for j in range(KC):
                    for k in range(KC):
                        dst = ztile[:, j, k * P:(k + 1) * P]
                        src = PS[:, MB, j * D + k * P:j * D + (k + 1) * P]
                        if j == k:
                            dve.tensor_tensor(dst, src, ident[:, :], ALU.add)
                        else:
                            dve.tensor_copy(dst, src)
                dve.tensor_tensor(brow_sum[0], PS[0:1, MB + 1, 0:D], brow_raw[BR_SO], ALU.add)
                done(dve, "m_sb")
                lay_out(dve, lay_k, 0, 1, "layk1")
                dve.tensor_tensor(brow_sum[1], brow_raw[BR_O], brow_raw[BR_B1], ALU.add)
                dve.tensor_tensor(brow_sum[2], brow_raw[BR_F2], brow_raw[BR_B2], ALU.add)
                dve.tensor_copy(Mt[0][:, :, :], ztile[:, 0:KC, :])
                dve.drain()
                rows = ((bias[:, 0:D], 0), (bias[:, D:2 * D], 1), (b2row[:, :], 2))
                for t_, n in rows:
                    dve.tensor_copy(t_[0:1, :], brow_sum[n])
                dve.drain()
                dve.tensor_tensor(Mt[1][:, :, :], ztile[:, 0:KC, :], f32(Mt[0][:, :, :]), ALU.subtract)
                for t_, n in rows:
                    dve.tensor_tensor(t_[32:33, :], brow_sum[n], f32(t_[0:1, :]), ALU.subtract)

                def low_parts(b):
                    need(dve, f"ahi{b}")
                    for j in range(KC):
                        for k in range(2):
                            dve.scalar_tensor_tensor(A[1][:, b, j, k, :], PS[:, A0B + 2 * j + k, 0:HM],
                                                     col[:, j, C_G1:C_G1 + 1], f32(A[0][:, b, j, k, :]),
                                                     ALU.mult, ALU.subtract)
                    for src, (b_, k, c_) in row_banks(slice(0, 1), b):
                        dve.tensor_tensor(sbias[32:33, b_, k, c_], src, f32(sbias[0:1, b_, k, c_]), ALU.subtract)
                    done(dve, f"a{b}_sb")

                def low_vw(b):
                    need(dve, f"vwhi{b}")
                    for r in range(NQ):
                        dve.tensor_tensor(VW[1][:, b, 2 * r:2 * r + 2, :],
                                          PS[:, VWB + r, :].rearrange("p (a d) -> p a d", a=2),
                                          f32(VW[0][:, b, 2 * r:2 * r + 2, :]), ALU.subtract)
                    done(dve, f"vw{b}_sb")

                low_parts(0)
                loaded(dve, "x")
                for t in range(NT):
                    dve.bn_stats(stat0[:, t, :], X[:, t, :])
                dve.drain()
                for t in range(NT):
                    dve.bn_aggr(mv0[:, t, :], stat0[:, t, :])
                dve.drain()
                dve.tensor_scalar(var0[:, :], mv0[:, :, 1], EPS, None, ALU.add)
                done(dve, "stat0")
                low_vw(0)
                low_parts(1)
                low_vw(1)
                need(dve, "l1_ps")
                bk = PS[:, C2B, 0:KC * B * M].rearrange("p (j c) -> p j c", j=KC)
                dve.tensor_copy(Bctx[0][:, :, :], bk)
                dve.tensor_tensor(b1col[:, :], PS[:, C2B, KC * B * M:KC * B * M + NF], b1col[:, :], ALU.add)
                dve.drain()
                dve.tensor_tensor(Bctx[1][:, :, :], bk, f32(Bctx[0][:, :, :]), ALU.subtract)
                done(dve, "setup")
            if act:
                loaded(act, "bc")
                act.activation(tg[:, :], gate_raw[:, :], ACT.Tanh)
                done(act, "tanh")
                loaded(act, "col")
                for b in range(B):
                    need(act, f"a{b}_ps")
                    for j in range(KC):
                        for k in range(2):
                            act.activation(A[0][:, b, j, k, :], PS[:, A0B + 2 * j + k, 0:HM], ACT.Identity,
                                           scale=col[:, j, C_G1:C_G1 + 1])
                    for src, (b_, k, c_) in row_banks(slice(0, 1), b):
                        act.activation(sbias[0:1, b_, k, c_], src, ACT.Copy)
                    done(act, f"ahi{b}")
                    need(act, f"vw{b}_ps")
                    for r in range(NQ):
                        act.activation(VW[0][:, b, 2 * r:2 * r + 2, :],
                                       PS[:, VWB + r, :].rearrange("p (a d) -> p a d", a=2), ACT.Copy)
                    done(act, f"vwhi{b}")
                    if b == 0:
                        need(act, "c2_ps")
                        act.activation(C2[:, :, :], PS[0:M, C2B, :].rearrange("m (b d) -> m b d", b=B), ACT.Copy)
                        done(act, "c2_sb")
            if pool:
                need(pool, "kv_sb")
                for b in range(B):
                    lay_out(pool, lay_v, 1, b, f"layv{b}")
                loaded(pool, "bc")
                need(pool, "tanh")
                for r_ in (R_G3, R_B3):
                    pool.tensor_scalar(bc[:, r_, :], bc[:, r_, :], tg[:, 0:1], 0.0, ALU.mult, ALU.add)
                loaded(pool, "e")
                pool.tensor_copy(gT[0][:, :, 0:E], gT_raw[:, :, :])
                pool.drain()
                pool.tensor_tensor(gT[1][:, :, 0:E], gT_raw[:, :, :], f32(gT[0][:, :, 0:E]), ALU.subtract)
                need(pool, "stat0")
                pool.tensor_tensor(rstd0[:, :], var0[:, :], rstd0[:, :], ALU.pow)
                pool.drain()
                pool.tensor_tensor(nmr0[:, :], mv0[:, :, 0], rstd0[:, :], ALU.mult)
                pool.drain()
                pool.tensor_scalar(nmr0[:, :], nmr0[:, :], -1.0, 0.0, ALU.mult, ALU.add)
                done(pool, "ln0")

            stage_a_tiles(pe, act, dve, pool, sp)
            stage_b(pe, act, dve, pool, sp)
            stage_c(pe, act, dve, pool, sp)
            stage_d(pe, act, dve, pool, sp)
            stage_e(pe, act, dve, pool, sp)

        @block.sync
        def _(eng):
            program(None, None, None, None, eng)

        @block.tensor
        def _(eng):
            program(eng, None, None, None, None)

        @block.scalar
        def _(eng):
            program(None, eng, None, None, None)

        @block.vector
        def _(eng):
            program(None, None, eng, None, None)

        @block.gpsimd
        def _(eng):
            program(None, None, None, eng, None)




def kernel(**inputs):
    import numpy as np
    import concourse.bacc as bacc
    from concourse.bass_utils import run_bass_kernel_spmd

    f = {k: np.asarray(v) for k, v in inputs.items()}
    a = {k[9:]: v for k, v in f.items() if k.startswith("L0_xattn_")}
    m = {k[7:]: v for k, v in f.items() if k.startswith("L0_ffn_")}
    r = {k[7:]: v for k, v in f.items() if k.startswith("L1_ffn_")}
    c = np.concatenate
    raw = c([a["in_proj_w"][D:2 * D].T, a["in_proj_w"][2 * D:].T, a["qkv_w"][2 * D:], a["sa_out_w"].T,
             a["in_proj_w"][:D], a["mha_out_w"].T, f["L1_xattn_We"].T, f["L1_xattn_W2"].T], axis=1)
    cols = np.stack([a["qkv_b"][2 * D:], a["in_proj_b"][D:2 * D], a["in_proj_b"][2 * D:], a["in_proj_b"][:D],
                     a["ln1_g"], a["ln1_b"], a["ln2_g"], a["ln2_b"], r["mu_r"], r["mu_k"]], axis=1)
    bcast = np.stack([a["ln1_g"], a["ln2_g"], a["ln3_g"], a["ln3_b"], a["ln1_b"]])
    brow = np.stack([a["sa_out_b"], a["mha_out_b"], a["lin2_b"], a["ln1_b"], a["ln2_b"]])
    wg = c([m["ws_gate"].reshape(2, I, D), m["w_gate"]])
    wu = c([m["ws_up"].reshape(2, I, D), m["w_up"]])
    gu = np.stack([wg, wu], axis=1).reshape(NU * 2 * I, D).T
    dn = c([m["ws_down"].T.reshape(2, I, D), m["w_down"].transpose(0, 2, 1)]).reshape(NU * I, D)
    arrays = {
        "x": f["x"].reshape(B * S, D), "ctxT": f["ctx_1024"].reshape(B * M, D).T,
        "gates": c([f["g_xattn"], f["g_ffn"]]), "raw": raw, "cols": cols, "l1b": a["lin1_b"].reshape(NF, P).T, "bcast": bcast,
        "brow": brow, "w1": a["lin1_w"].T, "w2": a["lin2_w"].T.reshape(NF, P, D).transpose(1, 0, 2).reshape(P, NF * D),
        "gateT": m["gate_weight"].T, "gu": gu, "dn": dn,
        "rw": c([r["W_r"].T, r["W_k"].T, r["W_v"].T], axis=1),
    }
    arrays = {k: np.ascontiguousarray(v) for k, v in arrays.items()}
    nc = bacc.Bacc("TRN2", target_bir_lowering=False, num_devices=1)
    aps = [nc.dram_tensor(k, v.shape, mybir.dt.from_np(v.dtype), kind="ExternalInput").ap() for k, v in arrays.items()]
    out = nc.dram_tensor("out", (B * S, D), F32, kind="ExternalOutput").ap()
    build(nc, *aps, out)
    res = run_bass_kernel_spmd(nc, [arrays], core_ids=[0])
    return res.results[0]["out"].reshape(B, S, D)
```

```python
from contextlib import ExitStack

import concourse.bass as bass
from concourse import mybir

F32 = mybir.dt.float32
F32R = mybir.dt.float32r
U32 = mybir.dt.uint32
ALU = mybir.AluOpType
ACT = mybir.ActivationFunctionType
AX = mybir.AxisListType

P = 128
B, S, D = 2, 1024, 256
KC = D // P
NT = B * S // P
CH = 512
TPC = CH // P
NCH = B * S // CH
TPB = S // P
M = 77
H, DH = 8, 32
HH = H // 2
HM = HH * M
NV = -(-H * M // P)
NW = -(-HM // P)
V_OFF = HM - (NV - NW) * P
FF, NF = 1024, 8
E, I = 8, 128
NU = E + 2
LO_ROW = 32
EPS = 1e-5
ROUTE_SCALE = 2.5

(W_K, W_VM, W_V, W_SO, W_Q, W_O, W_E, W_2) = range(8)
(C_BV, C_BK, C_BVM, C_BQ, C_G1, C_G2, C_B2, C_MUR, C_MUK) = range(9)
NCOL = 9
(R_G1, R_G2, R_G3, R_B3, R_B1) = range(5)
NBC = 5
(BR_SO, BR_O, BR_F2, BR_B1, BR_B2) = range(5)


class Event:

    def __init__(self, sem, per=1, credit=0):
        self.sem, self.per, self.credit = sem, per, credit

    def wait(self, eng, t, k=0):
        value = self.per * t + k + 1 + self.credit
        if isinstance(value, int) and value <= self.credit:
            return
        eng.wait_ge(self.sem, value)


def build(nc, x, ctxT, gates, raw, cols, l1b, bcast, brow, w1, w2, gateT, gu, dn, rw, out):
    with ExitStack() as top:
        def sem(name):
            return top.enter_context(nc.semaphore(name))

        events = []

        def event(name, per=1, credit=0):
            events.append(Event(sem(name), per, credit))
            return events[-1]

        def sb(ctx, name, shape, dt=F32):
            return ctx.enter_context(nc.sbuf_tensor(name, shape, dt))

        def pair(ctx, name, shape):
            return sb(ctx, name + "_hi", shape, F32R), sb(ctx, name + "_lo", shape, F32R)

        with ExitStack() as setup:
            rawA = sb(setup, "rawA", [P, KC, 8 * D])
            w1raw = sb(setup, "w1raw", [P, KC, FF])
            w2raw = sb(setup, "w2raw", [P, NF, D])
        XT = pair(top, "XT", [P, KC, B * S])
        X = sb(top, "X", [P, NT, D])
        W1 = pair(top, "W1", [P, KC, FF])
        W2 = pair(top, "W2", [P, NF, D])
        hid = [pair(top, f"hid{k}", [P, CH]) for k in range(2)]
        work = [sb(top, f"work{k}", [P, CH]) for k in range(4)]
        ntile = sb(top, "ntile", [P, TPC, D])
        ztile = sb(top, "ztile", [P, TPC, D])
        bc = sb(top, "bc", [P, NBC, D])
        gate_raw = sb(top, "gate_raw", [P, 4])
        tg = sb(top, "tg", [P, 4])
        col = sb(top, "col", [P, KC, NCOL])
        b1col = sb(top, "b1col", [P, NF])
        warm = sb(top, "warm", [P, 1])
        b2row = sb(top, "b2row", [33, D], F32R)
        ident = sb(top, "ident", [P, P])
        ones = sb(top, "ones", [33, P], F32R)
        ctx_sb = sb(top, "ctx_sb", [P, KC, B * M])
        Bctx = pair(top, "Bctx", [P, KC, B * M])
        C2 = sb(top, "C2", [M, B, D])
        gT_raw = sb(top, "gT_raw", [P, KC, E])
        gT = pair(top, "gT", [P, KC, P])
        cmb = sb(top, "cmb", [P, NT, E])
        moe_raw = [sb(top, f"moe_raw{k}", [P, 3, D]) for k in range(2)]
        stat = sb(top, "stat", [P, 8, 6])
        mv = sb(top, "mv", [P, 8, 2])
        var = sb(top, "var", [P, 8])
        rstd = sb(top, "rstd", [P, 8])
        half = sb(top, "half", [P, 8])
        iota = sb(top, "iota", [P, E])
        with ExitStack() as stage_a:
            Mt = pair(stage_a, "Mt", [P, KC, D])
            A = pair(stage_a, "A", [P, B, KC, 2, HM])
            VW = pair(stage_a, "VW", [P, B, NV, D])
            bias = sb(stage_a, "bias", [33, 2 * D], F32R)
            sbias = sb(stage_a, "sbias", [33, B, 2, HM], F32R)
            xt01 = pair(stage_a, "xt01", [P, 2, KC, P])
            Pm = [sb(stage_a, f"Pm{k}", [P, KC * NW * P]) for k in range(2)]
            PT = pair(stage_a, "PT", [P, NV, P])
            n0, n1, n2 = ntile[:, 0, :], (ntile[:, 1, :], ntile[:, 2, :]), (ntile[:, 3, :], ztile[:, 3, :])
            nmr = sb(stage_a, "nmr", [P, 1])
            ucol = sb(stage_a, "ucol", [P, KC])
            lay_v1 = sb(stage_a, "lay_v1", [P, KC, NW * P])
            stat0 = sb(stage_a, "stat0", [P, NT, 6])
            mv0 = sb(stage_a, "mv0", [P, NT, 2])
            var0 = sb(stage_a, "var0", [P, NT])
            rstd0 = sb(stage_a, "rstd0", [P, NT])
            nmr0 = sb(stage_a, "nmr0", [P, NT])
            mx = sb(stage_a, "mx", [P, H])
            sm = sb(stage_a, "sm", [P, H])
            rc = sb(stage_a, "rc", [P, H])
        with ExitStack() as stage_c:
            GU = pair(stage_c, "GU", [P, KC, 2 * NU * I])
            DN = pair(stage_c, "DN", [P, NU, D])
            cT = sb(stage_c, "cT", [LO_ROW + E, CH], F32R)
            cst = sb(stage_c, "cst", [P, TPC, E])
            lgT = sb(stage_c, "lgT", [P, CH])
            sel = sb(stage_c, "sel", [LO_ROW + E, E, P], F32R)
            selraw = sb(stage_c, "selraw", [LO_ROW + E, E, P])
            xr4 = sb(stage_c, "xr4", [P, TPC, D])
            ex = sb(stage_c, "ex", [P, TPC, E])
            sc = sb(stage_c, "sc", [P, TPC, E])
            top8 = sb(stage_c, "top8", [P, TPC, 8])
            idx8 = sb(stage_c, "idx8", [P, TPC, 8], U32)
            idxf = sb(stage_c, "idxf", [P, TPC, 8])
            tsum = sb(stage_c, "tsum", [P, TPC])
            tw = sb(stage_c, "tw", [P, TPC, 2])
            oh = sb(stage_c, "oh", [P, TPC, E])
        with ExitStack() as stage_e:
            XD = sb(stage_e, "XD", [P, KC, B * (S + 1)])
            att = sb(stage_e, "att", [M, S])
            attp = pair(stage_e, "attp", [M, S])
            c2s = pair(stage_e, "c2s", [M, D])
            c2f = sb(stage_e, "c2f", [M, D])
            nmax = sb(stage_e, "nmax", [M, B])
            asum = sb(stage_e, "asum", [M, B])
            ascl = sb(stage_e, "ascl", [M, 1])
            nm4 = sb(stage_e, "nm4", [P, 2 * TPC])
            dif = sb(stage_e, "dif", [P, KC, CH])
            xmix = [sb(stage_e, f"xmix{k}", [P, KC, CH]) for k in range(2)]
            xm = [pair(stage_e, f"xm{k}", [P, KC, CH]) for k in range(2)]
            sq = sb(stage_e, "sq", [P, KC, CH])
            ka = pair(stage_e, "ka", [P, KC, CH])
            rs = [sb(stage_e, f"rs{k}", [P, 2, CH]) for k in range(2)]
        PS = top.enter_context(nc.psum_tensor("PS", [P, 8, 512], F32))

        xv = x.rearrange("(i p) d -> p i d", p=P)
        ov = out.rearrange("(i p) d -> p i d", p=P)

        N_LOADS = {"kv": 2, "m": 3, "q": 1, "x0": 1, "x": 1, "e": 2, "w1": 2, "w2": 1, "col": 1, "bc": 2}
        s_ld = {name: sem("ld_" + name) for name in N_LOADS}

        def load(eng, name, dst, src):
            eng.dma_start(dst, src).then_inc(s_ld[name], 16)

        def loaded(eng, name):
            eng.wait_ge(s_ld[name], 16 * N_LOADS[name])

        flags = {}

        def flag(name):
            if name not in flags:
                flags[name] = sem("f_" + name)
            return flags[name]

        def done(eng, name):
            eng.drain()
            eng.sem_inc(flag(name), 1)

        def need(eng, name):
            eng.wait_ge(flag(name), 1)

        block = top.enter_context(nc.Block())

        lay_k = [[Pm[0][:, k * HM:(k + 1) * HM] for k in range(KC)], [work[2 + k][:, 0:HM] for k in range(KC)]]
        lay_v = [[Pm[1][:, k * NW * P:(k + 1) * NW * P] for k in range(KC)], [lay_v1[:, k, :] for k in range(KC)]]
        utmp = ztile[:, 0:KC, :]

        def mm3(pe, o, a, b, first, last, skip=False):
            pe.matmul(o, a[0], b[0], start=first, stop=False, skip_group_check=skip)
            pe.matmul(o, a[0], b[1], start=False, stop=False, skip_group_check=skip)
            return pe.matmul(o, a[1], b[0], start=False, stop=last, skip_group_check=skip)

        def sub(p2, *ix):
            return p2[0][ix], p2[1][ix]

        def f32(ap):
            return ap.bitcast(F32)

        a_n0 = event("a_n0"); a_t = event("a_t"); a_h = event("a_h"); a_l = event("a_l")
        a_y = event("a_y"); a_v = event("a_v"); a_r1 = event("a_r1"); a_n1 = event("a_n1")
        a_g1 = event("a_g1")
        a_s = event("a_s", per=2); a_mx = event("a_mx", per=2); a_ex = event("a_ex", per=2)
        a_rc = event("a_rc"); a_p = event("a_p"); a_tp = event("a_tp"); a_hp = event("a_hp")
        a_lp = event("a_lp")
        a_c = event("a_c"); a_z = event("a_z"); a_r = event("a_r"); a_n2 = event("a_n2")
        a_g2 = event("a_g2"); a_t2 = event("a_t2"); a_h2 = event("a_h2"); a_l2 = event("a_l2")

        def rsqrt(pool, k, n=1):
            return pool.tensor_tensor(rstd[:, k:k + n], var[:, k:k + n], half[:, 0:n], ALU.pow)

        def stats(dve, src, k, n=1):
            for j in range(n):
                dve.bn_stats(stat[:, k + j, :], src[j])
            dve.drain()
            for j in range(n):
                dve.bn_aggr(mv[:, k + j, :], stat[:, k + j, :])
            dve.drain()
            return dve.tensor_scalar(var[:, k:k + n], mv[:, k:k + n, 1], EPS, None, ALU.add)

        N_EXP = 2
        LAG = 5
        FFN_AT = {NT + 2: 0, NT + 3: 1, NT + 4: 2}
        N_EARLY = len(FFN_AT)

        def a_step(pe, act, dve, pool, s, par, mid=None):
            def on(off):
                return not isinstance(s, int) or 0 <= s + off < NT

            def q(off):
                return (par + off) % 2

            TB, YB, SB, PB, CB, T2B = 0, 1, 2, 4, 6, 7

            def x_tile(off):
                return X[:, s + off, :]

            def xt_tile(n, off):
                return XT[n][:, :, bass.ds((s + off) * P, P)]

            t01 = slice(0 if on(0) else 1, 2 if on(1) else 1)
            t01_ps = PS[:, TB, :].rearrange("p (a k t) -> p a k t", a=2, k=KC)[:, t01]
            pt_ps = PS[:, PB:PB + 2, :].rearrange("p b c -> p (b c)")[:, 0:NV * P]
            pt = [PT[n][:, :, :].rearrange("p r t -> p (r t)") for n in range(2)]
            t2_ps = PS[:, T2B, 0:D].rearrange("p (k t) -> p k t", k=KC)
            ln12 = (1 if on(0) else 2, 3 if on(-4) else 2)
            b1 = (s - 1) // TPB
            b3 = (s - 3) // TPB

            if pe:
                if on(-3):
                    a_p.wait(pe, s - 3)
                    a_lp.wait(pe, s - 4)
                    for r in range(NV):
                        i_ = pe.transpose(PS[:, PB + r // 4, (r % 4) * P:(r % 4 + 1) * P],
                                          Pm[q(-3)][:, r * P:(r + 1) * P], ident[:, :])
                    i_.then_inc(a_tp.sem, 1)
                if on(-5):
                    a_n2.wait(pe, s - 5)
                    a_l2.wait(pe, s - 6)
                    for k in range(KC):
                        i_ = pe.transpose(PS[:, T2B, k * P:(k + 1) * P], n2[q(-5)][:, k * P:(k + 1) * P], ident[:, :])
                    i_.then_inc(a_t2.sem, 1)
                if on(0):
                    a_l.wait(pe, s)
                    a_n1.wait(pe, s - 1)
                    for k in range(KC):
                        mm3(pe, PS[:, YB, 0:D], sub(xt01, slice(None), 1, k), sub(Mt, slice(None), k), k == 0, False)
                    pe.matmul(PS[:, YB, 0:D], ones[:, :], bias[:, 0:D], start=False, stop=True).then_inc(a_y.sem, 1)
                if on(-1):
                    a_l.wait(pe, s)
                    for j in range(2):
                        a_ex.wait(pe, s - 2, j)
                        for k in range(KC):
                            mm3(pe, PS[:, SB + j, 0:HM], sub(xt01, slice(None), 0, k),
                                sub(A, slice(None), b1, k, j), k == 0, False)
                        pe.matmul(PS[:, SB + j, 0:HM], ones[:, :], sbias[:, b1, j, :], start=False, stop=True)\
                          .then_inc(a_s.sem, 1)
                def pv(blocks):
                    for r in blocks:
                        mm3(pe, PS[:, CB, 0:D], sub(PT, slice(None), r), sub(VW, slice(None), b3, r), r == 0, False)

                if on(-3):
                    a_lp.wait(pe, s - 3)
                    a_z.wait(pe, s - 4)
                    pv(range(NV // 2))
                if mid and s >= 0:
                    mid(pe, None, s)
                if on(1) or on(0):
                    if on(0):
                        a_n1.wait(pe, s)
                    if on(1):
                        a_n0.wait(pe, s + 1)
                    a_l.wait(pe, s)
                    for a, src in enumerate((n1[q(0)], n0)):
                        if on(a):
                            for k in range(KC):
                                c0 = (a * KC + k) * P
                                i_ = pe.transpose(PS[:, TB, c0:c0 + P], src[:, k * P:(k + 1) * P], ident[:, :])
                    i_.then_inc(a_t.sem, 1)
                if on(-3):
                    pv(range(NV // 2, NV))
                    pe.matmul(PS[:, CB, 0:D], ones[:, :], bias[:, D:2 * D], start=False, stop=True)\
                      .then_inc(a_c.sem, 1)
            if act:
                def exps(off, j, g0=0, g1=HH):
                    a_mx.wait(act, s + off, j)
                    if j == 0:
                        a_tp.wait(act, s + off - 2)
                        a_rc.wait(act, s + off - 1)
                    for g in range(g0, g1):
                        h = j * HH + g
                        act.activation(Pm[q(off)][:, h * M:(h + 1) * M], PS[:, SB + j, g * M:(g + 1) * M],
                                       ACT.Exp, bias=mx[:, h:h + 1], accum_out=sm[:, h:h + 1])
                    if g1 == HH:
                        act.drain()
                        act.sem_inc(a_ex.sem, 1)

                if on(-2):
                    exps(-2, 1)
                if on(-3):
                    a_tp.wait(act, s - 3)
                    a_c.wait(act, s - 4)
                    act.activation(pt[0], pt_ps, ACT.Copy).then_inc(a_hp.sem, 1)
                if on(-5):
                    a_t2.wait(act, s - 5)
                    act.activation(xt_tile(0, -5), t2_ps, ACT.Copy).then_inc(a_h2.sem, 1)
                if on(0):
                    a_r1.wait(act, s)
                    a_t.wait(act, s - 1)
                    a_g1.wait(act, s - 2)
                    act.activation(n1[q(0)], PS[:, YB, 0:D], ACT.Identity, bias=nmr[:, 0:1],
                                   scale=rstd[:, 1:2]).then_inc(a_n1.sem, 1)
                if on(-1):
                    exps(-1, 0, 0, N_EXP)
                if on(1) or on(0):
                    a_t.wait(act, s + 1)
                    a_y.wait(act, s)
                    a_s.wait(act, s - 1, 1)
                    act.activation(xt01[0][:, t01], t01_ps, ACT.Copy).then_inc(a_h.sem, 1)
                if on(2):
                    a_t.wait(act, s + 1)
                    act.activation(n0, x_tile(2), ACT.Identity, bias=nmr0[:, bass.ds(s + 2, 1)],
                                   scale=rstd0[:, bass.ds(s + 2, 1)]).then_inc(a_n0.sem, 1)
                if on(-1):
                    exps(-1, 0, N_EXP, HH)
            if dve:
                if on(-4):
                    a_c.wait(dve, s - 4)
                    a_g1.wait(dve, s - 4)
                    dve.tensor_tensor(x_tile(-4), PS[:, CB, 0:D], x_tile(-4), ALU.add).then_inc(a_z.sem, 1)
                    dve.drain()
                    dve.bn_stats(stat[:, 2, :], x_tile(-4))
                if on(0):
                    a_y.wait(dve, s)
                    a_n1.wait(dve, s - 1)
                    dve.bn_stats(stat[:, 1, :], PS[:, YB, 0:D])
                if on(0) or on(-4):
                    dve.drain()
                    for k in range(*ln12):
                        dve.bn_aggr(mv[:, k, :], stat[:, k, :])
                    dve.drain()
                    dve.tensor_scalar(var[:, ln12[0]:ln12[1]], mv[:, ln12[0]:ln12[1], 1], EPS, None, ALU.add)\
                       .then_inc(a_v.sem, 1)
                if on(-3):
                    a_hp.wait(dve, s - 3)
                    dve.tensor_tensor(pt[1], pt_ps, f32(pt[0]), ALU.subtract).then_inc(a_lp.sem, 1)
                if on(-2):
                    a_ex.wait(dve, s - 2, 1)
                    a_p.wait(dve, s - 3)
                    dve.reciprocal(rc[:, :], sm[:, :]).then_inc(a_rc.sem, 1)
                if on(-1):
                    for j in range(2):
                        a_s.wait(dve, s - 1, j)
                        a_ex.wait(dve, s - 2, j)
                        dve.tensor_reduce(mx[:, j * HH:(j + 1) * HH],
                                          PS[:, SB + j, 0:HM].rearrange("p (g m) -> p g m", g=HH),
                                          AX.X, ALU.max, negate=True).then_inc(a_mx.sem, 1)
                if on(-4):
                    a_r.wait(dve, s)
                    a_t2.wait(dve, s - 6)
                    a_g2.wait(dve, s - 6)
                    dve.tensor_scalar(n2[q(-4)], x_tile(-4), mv[:, 2, 0:1], rstd[:, 2:3],
                                      ALU.subtract, ALU.mult).then_inc(a_n2.sem, 1)
                if on(-5):
                    a_h2.wait(dve, s - 5)
                    dve.tensor_tensor(xt_tile(1, -5), t2_ps, f32(xt_tile(0, -5)), ALU.subtract)\
                       .then_inc(a_l2.sem, 1)
                if mid and s >= 0:
                    mid(None, dve, s)
                if on(1) or on(0):
                    a_h.wait(dve, s + 1)
                    dve.tensor_tensor(xt01[1][:, t01], t01_ps, f32(xt01[0][:, t01]), ALU.subtract).then_inc(a_l.sem, 1)
            if pool:
                if on(-1):
                    a_n1.wait(pool, s - 1)
                    a_n0.wait(pool, s - 1)
                    pool.tensor_tensor(x_tile(-1), n1[q(-1)], bc[:, R_G1, :], ALU.mult).then_inc(a_g1.sem, 1)
                if on(0) or on(-4):
                    a_v.wait(pool, s)
                    if on(0):
                        a_n1.wait(pool, s - 1)
                    if on(-4):
                        a_n2.wait(pool, s - 5)
                    rsqrt(pool, ln12[0], ln12[1] - ln12[0]).then_inc(a_r.sem, 1)
                if on(0):
                    pool.drain()
                    pool.tensor_scalar(nmr[:, :], mv[:, 1, 0:1], rstd[:, 1:2], -1.0, ALU.mult, ALU.mult)\
                        .then_inc(a_r1.sem, 1)
                if on(-2):
                    a_rc.wait(pool, s - 2)
                    pn = Pm[q(-2)][:, 0:H * M].rearrange("p (h m) -> p h m", h=H)
                    pool.tensor_tensor(pn, pn, rc[:, :].unsqueeze(2).to_broadcast([P, H, M]), ALU.mult)\
                        .then_inc(a_p.sem, 1)
                if on(-5):
                    a_n2.wait(pool, s - 5)
                    pool.tensor_tensor(x_tile(-5), n2[q(-5)], bc[:, R_G2, :], ALU.mult)\
                        .then_inc(a_g2.sem, 1)

        w_hi = event("w_hi"); w2_lo = event("w2_lo")
        FFN_ACT, FFN_DVE = {0: 0, 2: 1, 3: 2, 4: 3}, {1: 0, 3: 1, 4: 2, 5: 3}
        NPART = 4

        def ffn_weights(act, dve, pool, n):
            k, c1 = n // 2, slice((n % 2) * FF // 2, (n % 2 + 1) * FF // 2)
            f2 = slice(n * NF // NPART, (n + 1) * NF // NPART)
            g2 = col[:, k, C_G2:C_G2 + 1]
            if act:
                loaded(act, "w1")
                loaded(act, "w2")
                act.activation(W1[0][:, k, c1], w1raw[:, k, c1], ACT.Identity, scale=g2)
                act.activation(W2[0][:, f2, :], w2raw[:, f2, :], ACT.Copy)
                act.drain()
                act.sem_inc(w_hi.sem, 1)
            if dve:
                w_hi.wait(dve, n)
                dve.scalar_tensor_tensor(W1[1][:, k, c1], w1raw[:, k, c1], g2, f32(W1[0][:, k, c1]),
                                         ALU.mult, ALU.subtract)
            if pool:
                w_hi.wait(pool, n)
                pool.tensor_tensor(W2[1][:, f2, :], w2raw[:, f2, :], f32(W2[0][:, f2, :]), ALU.subtract)\
                    .then_inc(w2_lo.sem, 1)

        def stage_a_tiles(pe, act, dve, pool, sp, late_setup, late_work):
            if pe:
                need(pe, "setup")
            if act:
                need(act, "setup")
                need(act, "ln0_0")
            if pool:
                need(pool, "setup")
                for n in range(2):
                    pool.memset(Pm[n][:, H * M:NV * P], 0.0)
                pool.drain()
            eng = pe or act or dve or pool
            if not eng:
                return
            if act:
                act.activation(n0, X[:, 0, :], ACT.Identity, bias=nmr0[:, 0:1], scale=rstd0[:, 0:1])\
                   .then_inc(a_n0.sem, 1)
            for s in range(-1, LAG + 1):
                if pe and s == 3:
                    need(pe, "vw1_sb")
                if act and s == TPC - 2:
                    need(act, "ln0_1")
                if s == LAG:
                    if dve:
                        w2_lo.wait(dve, NPART - 1)
                    if act:
                        for g in range(2, NT // TPC):
                            need(act, f"ln0_{g}")
                    if pe:
                        need(pe, "l1_sb")
                a_step(pe, act, dve, pool, s, s % 2, late_work)
                late_setup(act, dve, pool, s)
            with eng.Fori(LAG + 1, NT - 3, 2) as s:
                a_step(pe, act, dve, pool, s, (LAG + 1) % 2)
                a_step(pe, act, dve, pool, s + 1, LAG % 2)
            for s in range(NT - 2, NT + LAG):
                a_step(pe, act, dve, pool, s, s % 2)
                if s in FFN_AT:
                    if pe:
                        a_l2.wait(pe, TPC - 1)
                    b_unit(pe, act, dve, pool, sp, 0, FFN_AT[s], False)

        def tiles4(buf, c):
            return buf[:, bass.ds(c * TPC, TPC), :]

        def norm4(dve, dst, src, k=0):
            for t in range(TPC):
                i_ = dve.tensor_scalar(dst[:, t, :], src(t), mv[:, k + t, 0:1], rstd[:, k + t:k + t + 1],
                                       ALU.subtract, ALU.mult)
            return i_

        def down(pe, hp, wd, bank0, first, brow_ap=None):
            for t in range(TPC):
                o = PS[:, bank0 + t // 2, (t % 2) * D:(t % 2 + 1) * D]
                st = first and t % 2 == 0
                if first and brow_ap is not None:
                    pe.matmul(o, ones[:, :], brow_ap, start=st, stop=False, skip_group_check=True)
                    st = False
                i_ = mm3(pe, o, sub(hp, slice(None), slice(t * P, (t + 1) * P)), wd, st, True, skip=True)
            return i_

        b_g = event("b_g", credit=1); b_a = event("b_a", credit=1); b_l = event("b_l", credit=1)
        b_d = event("b_d", credit=1)
        b_z = event("b_z", credit=1); b_v3 = event("b_v3", credit=1); b_r3 = event("b_r3", credit=1)
        b_m3 = event("b_m3", credit=1)
        b_x = event("b_x", credit=1); b_v4 = event("b_v4", credit=1); b_r4 = event("b_r4", credit=1)
        b_n4 = event("b_n4", credit=1)
        b_t4 = event("b_t4", credit=1); b_h4 = event("b_h4", credit=1); b_l4 = event("b_l4", credit=1)
        b_lg = event("b_lg", credit=1); b_lc = event("b_lc", credit=1); b_lt = event("b_lt", credit=1)
        b_ex = event("b_ex", credit=1); b_cm = event("b_cm", credit=1); b_tw = event("b_tw", credit=1)
        s_xr = sem("s_xr"); s_moe = [sem(f"s_moe{k}") for k in range(2)]; g_hi = event("g_hi")
        g_moe = event("g_moe")
        s_rw = sem("s_rw"); g_rw = event("g_rw")
        GB, DB, TB, LB, RB = 0, 2, 4, 6, 7

        def route(dve, p, part):
            if part == 0:
                dve.tensor_scalar(sc[:, :, :], ex[:, :, :], 1.0, None, ALU.add)
                dve.drain()
                dve.reciprocal(sc[:, :, :], sc[:, :, :])
                dve.drain()
                for t in range(TPC):
                    dve.max(top8[:, t, :], sc[:, t, :])
                dve.drain()
                for t in range(TPC):
                    dve.max_index(idx8[:, t, :], top8[:, t, :], sc[:, t, :])
                dve.tensor_tensor(tsum[:, :], top8[:, :, 0], top8[:, :, 1], ALU.add)
                dve.drain()
                return
            dve.tensor_copy(idxf[:, :, 0:2], idx8[:, :, 0:2])
            dve.tensor_scalar(tsum[:, :], tsum[:, :], 1e-20, None, ALU.add)
            dve.drain()
            dve.reciprocal(tsum[:, :], tsum[:, :])
            dve.drain()
            dve.tensor_scalar(tsum[:, :], tsum[:, :], ROUTE_SCALE, None, ALU.mult)
            dve.drain()
            dve.sem_inc(b_tw.sem, 1)

        def combine(pool, p):
            b_tw.wait(pool, p)
            pool.tensor_tensor(tw[:, :, :], top8[:, :, 0:2], tsum[:, :].unsqueeze(2).to_broadcast([P, TPC, 2]),
                               ALU.mult)
            pool.drain()
            for t in range(TPC):
                pool.tensor_scalar(oh[:, t, :], iota[:, :], idxf[:, t, 1:2], tw[:, t, 1:2], ALU.is_equal, ALU.mult)
                pool.tensor_scalar(ex[:, t, :], iota[:, :], idxf[:, t, 0:1], tw[:, t, 0:1], ALU.is_equal, ALU.mult)
            pool.drain()
            pool.tensor_tensor(tiles4(cmb, p), oh[:, :, :], ex[:, :, :], ALU.add).then_inc(b_cm.sem, 1)

        def b_residual(pool, c):
            pool.wait_ge(s_xr, 16 * (c + 1))
            pool.tensor_tensor(xr4[:, :, :], xr4[:, :, :],
                               bc[:, R_B3:R_B3 + 1, :].to_broadcast([P, TPC, D]), ALU.add).then_inc(b_m3.sem, 1)

        def b_tail(pe, act, dve, pool, p, f):
            def x_t(t):
                return X[:, p * TPC + t, :]

            ch = bass.ds(p * CH, CH)
            if f == 0:
                if dve:
                    b_d.wait(dve, NF * p + NF - 1)
                    for q in range(2):
                        i_ = dve.tensor_tensor(ztile[:, 2 * q:2 * q + 2, :],
                                               PS[:, DB + q, :].rearrange("p (a d) -> p a d", a=2),
                                               X[:, bass.ds(p * TPC + 2 * q, 2), :], ALU.add)
                    i_.then_inc(b_z.sem, 1)
                    dve.drain()
                    stats(dve, [ztile[:, t, :] for t in range(TPC)], 0, TPC).then_inc(b_v3.sem, 1)
                if pool:
                    b_v3.wait(pool, p)
                    rsqrt(pool, 0, TPC).then_inc(b_r3.sem, 1)
            if f == 1 and dve:
                for t in range(TPC):
                    dve.scalar_tensor_tensor(ztile[:, t, :], ztile[:, t, :], mv[:, t, 0:1], bc[:, R_G3, :],
                                             ALU.subtract, ALU.mult)
                dve.drain()
                b_m3.wait(dve, p)
                b_r3.wait(dve, p)
                for t in range(TPC):
                    i_ = dve.scalar_tensor_tensor(x_t(t), ztile[:, t, :], rstd[:, t:t + 1], xr4[:, t, :],
                                                  ALU.mult, ALU.add)
                i_.then_inc(b_x.sem, 1)
            if f == 2:
                if dve:
                    dve.drain()
                    stats(dve, [x_t(t) for t in range(TPC)], 0, TPC).then_inc(b_v4.sem, 1)
                if pool:
                    b_v4.wait(pool, p)
                    rsqrt(pool, 0, TPC).then_inc(b_r4.sem, 1)
            if f == 3 and dve:
                b_r4.wait(dve, p)
                b_t4.wait(dve, p - 1)
                norm4(dve, ntile, x_t).then_inc(b_n4.sem, 1)
            if f == 4:
                if pe:
                    b_n4.wait(pe, p)
                    b_l4.wait(pe, p - 1)
                    for k in range(KC):
                        for t in range(TPC):
                            i_ = pe.transpose(PS[:, TB + k, t * P:(t + 1) * P], ntile[:, t, k * P:(k + 1) * P],
                                              ident[:, :])
                    i_.then_inc(b_t4.sem, 1)
                if act:
                    b_t4.wait(act, p)
                    for k in range(KC):
                        i_ = act.activation(XT[0][:, k, ch], PS[:, TB + k, :], ACT.Copy)
                    i_.then_inc(b_h4.sem, 1)
                if dve:
                    b_h4.wait(dve, p)
                    for k in range(KC):
                        i_ = dve.tensor_tensor(XT[1][:, k, ch], PS[:, TB + k, :], f32(XT[0][:, k, ch]), ALU.subtract)
                    i_.then_inc(b_l4.sem, 1)
            if f == 5:
                if pe:
                    b_l4.wait(pe, p)
                    b_lc.wait(pe, p - 1)
                    for k in range(KC):
                        i_ = mm3(pe, PS[:, LB, :], sub(gT, slice(None), k), sub(XT, slice(None), k, ch),
                                 k == 0, k == KC - 1)
                    i_.then_inc(b_lg.sem, 1)
                if act:
                    b_lg.wait(act, p)
                    b_lt.wait(act, p - 1)
                    act.activation(lgT[:, :], PS[:, LB, :], ACT.Copy).then_inc(b_lc.sem, 1)
            if f == 6:
                if pe:
                    b_lc.wait(pe, p)
                    b_ex.wait(pe, p - 1)
                    for t in range(TPC):
                        i_ = pe.transpose(PS[:, RB, t * P:(t + 1) * P], lgT[:, t * P:(t + 1) * P], ident[:, :])
                    i_.then_inc(b_lt.sem, 1)
                if act:
                    b_lt.wait(act, p)
                    b_cm.wait(act, p - 1)
                    act.activation(ex[:, :, :], PS[:, RB, :].rearrange("p (t e) -> p t e", t=TPC)[:, :, 0:E], ACT.Exp,
                                   scale=-1.0).then_inc(b_ex.sem, 1)
            if f == 6 and dve:
                b_ex.wait(dve, p)
                b_cm.wait(dve, p - 1)
                route(dve, p, 0)
            if f == 7:
                if dve:
                    route(dve, p, 1)
                if pool:
                    combine(pool, p)

        guv = gu.rearrange("(k p) (n c) -> p k n c", p=P, n=NU)
        dnv = dn.rearrange("(n p) d -> p n d", p=P)

        def split_unit(act, pool, sp, n, q):
            raw_, hi, lo = moe_raw[q], GU[0], GU[1]
            cols_ = bass.ds(n * 2 * I, 2 * I)
            if act:
                act.wait_ge(s_moe[q], 48 * (n // 2) + 48)
                act.activation(hi[:, :, cols_], raw_[:, 0:KC, :], ACT.Copy)
                act.activation(DN[0][:, bass.ds(n, 1), :], raw_[:, KC:KC + 1, :], ACT.Copy).then_inc(g_hi.sem, 1)
            if pool:
                g_hi.wait(pool, n)
                pool.tensor_tensor(lo[:, :, cols_], raw_[:, 0:KC, :], f32(hi[:, :, cols_]), ALU.subtract)
                pool.tensor_tensor(DN[1][:, bass.ds(n, 1), :], raw_[:, KC:KC + 1, :],
                                   f32(DN[0][:, bass.ds(n, 1), :]), ALU.subtract).then_inc(g_moe.sem, 1)
            if sp:
                g_moe.wait(sp, n - 2)
                for k in range(KC):
                    sp.dma_start(raw_[:, k, :], guv[:, k, bass.ds(n, 1), :]).then_inc(s_moe[q], 16)
                sp.dma_start(raw_[:, KC, :], dnv[:, bass.ds(n, 1), :]).then_inc(s_moe[q], 16)

        def b_unit(pe, act, dve, pool, sp, c, f, tail):
            u = NF * c + f
            if pe:
                b_a.wait(pe, u - 2)
                for k in range(KC):
                    i_ = mm3(pe, PS[:, GB + f % 2, :], sub(W1, slice(None), k, slice(f * P, (f + 1) * P)),
                             sub(XT, slice(None), k, bass.ds(c * CH, CH)), k == 0, k == KC - 1)
                i_.then_inc(b_g.sem, 1)
            if act:
                b_g.wait(act, u)
                b_l.wait(act, u - 2)
                b_d.wait(act, u - 2)
                for dst in (work[f % 2], hid[f % 2][0]):
                    i_ = act.activation(dst[:, :], PS[:, GB + f % 2, :], ACT.Relu, bias=b1col[:, f:f + 1])
                i_.then_inc(b_a.sem, 1)
            if dve:
                b_a.wait(dve, u)
                dve.tensor_tensor(hid[f % 2][1][:, :], work[f % 2][:, :], f32(hid[f % 2][0][:, :]), ALU.subtract)\
                    .then_inc(b_l.sem, 1)
            if pe and (tail or f):
                b_down(pe, c, f)
            if tail:
                b_tail(pe, act, dve, pool, c - 1, f)
            if tail and f == NF // 2:
                if sp:
                    b_x.wait(sp, c - 1)
                    sp.dma_start(xr4[:, :, :], xv[:, bass.ds(c * TPC, TPC), :]).then_inc(s_xr, 16)
                if pool:
                    b_residual(pool, c)

        def b_chunk(pe, act, dve, pool, sp, c):
            for f in range(NF):
                b_unit(pe, act, dve, pool, sp, c, f, True)
                if f in (3, 6):
                    split_unit(act, pool, sp, 2 * c + 2 + f // 6, f // 6)

        def b_down(pe, c, f):
            g = (f - 1) % NF
            b_l.wait(pe, NF * c + f - 1)
            if g == 0:
                b_z.wait(pe, c - 1)
                if isinstance(c, int):
                    a_ex.wait(pe, NT - 1, 1)
            down(pe, hid[g % 2], sub(W2, slice(None), g), DB, g == 0, b2row[:, :]).then_inc(b_d.sem, 1)

        def stage_b(pe, act, dve, pool, sp):
            if sp:
                for n in range(2):
                    split_unit(None, None, sp, n, n)
                a_g2.wait(sp, NT - 1); a_c.wait(sp, NT - 1); a_l2.wait(sp, NT - 1)
                sp.dma_start(xr4[:, :, :], xv[:, 0:TPC, :]).then_inc(s_xr, 16)
            if pool:
                a_c.wait(pool, NT - 1); a_l2.wait(pool, NT - 1); a_t2.wait(pool, NT - 1)
                pool.memset(selraw[:, :, :], 0.0)
                pool.drain()
                pool.memset(f32(cT[:, :]), 0.0)
                for r0 in (0, LO_ROW):
                    pool.affine_select(out=selraw[:, :, :], in_=selraw[:, :, :], compare_op=ALU.not_equal, fill=1.0,
                                       base=-r0, pattern=[[-1, E], [0, P]], channel_multiplier=1)
                    pool.drain()
                pool.tensor_copy(sel[:, :, :], selraw[:, :, :])
            if act:
                a_c.wait(act, NT - 1)
            if pe:
                a_l2.wait(pe, NT - 1)
            if dve:
                a_g2.wait(dve, NT - 1); a_t2.wait(dve, NT - 1)
            if pool:
                b_residual(pool, 0)
            for f in range(N_EARLY, NF):
                b_unit(pe, act, dve, pool, sp, 0, f, False)
                n = f - (NF - 4)
                if n >= 0:
                    split_unit(act, pool, sp if n > 1 else None, n, n % 2)
            eng = pe or act or dve or pool or sp
            with eng.Fori(1, NCH) as c:
                b_chunk(pe, act, dve, pool, sp, c)
            if pe:
                b_down(pe, NCH, 0)

        c_g = event("c_g", credit=1); c_s = event("c_s", credit=1); c_uo = event("c_uo", credit=1)
        c_m = event("c_m", credit=1); c_l = event("c_l", credit=1)
        c_d = event("c_d", credit=1); c_bc = event("c_bc", credit=1)
        c_cs = event("c_cs", credit=1); c_ct = event("c_ct", credit=1); c_ch = event("c_ch", credit=1)
        c_cl = event("c_cl", credit=1)
        c_x = event("c_x", credit=1); c_v = event("c_v", credit=1); c_r = event("c_r", credit=1)
        c_n = event("c_n", credit=1)
        c_t = event("c_t", credit=1); c_h = event("c_h", credit=1); c_lo = event("c_lo", credit=1)
        CG, CD, CU, CB, CT = 0, 2, 4, 6, 7
        NR = E

        def c_tail(pe, act, dve, pool, p, j):
            def x_t(t):
                return X[:, p * TPC + t, :]

            ch = bass.ds(p * CH, CH)
            if j == 0:
                if dve:
                    c_d.wait(dve, NU * p + NU - 1)
                    for t in range(TPC):
                        i_ = dve.scalar_tensor_tensor(x_t(t), PS[:, CD + t // 2, (t % 2) * D:(t % 2 + 1) * D],
                                                      tg[:, 2:3], x_t(t), ALU.mult, ALU.add)
                    i_.then_inc(c_x.sem, 1)
            if j == 1:
                if dve:
                    dve.drain()
                    stats(dve, [x_t(t) for t in range(TPC)], 0, TPC).then_inc(c_v.sem, 1)
                if pool:
                    c_v.wait(pool, p)
                    rsqrt(pool, 0, TPC).then_inc(c_r.sem, 1)
            if j == 2 and dve:
                c_r.wait(dve, p)
                c_t.wait(dve, 2 * p - 1)
                norm4(dve, ntile, x_t).then_inc(c_n.sem, 1)
            if j in (3, 4):
                k = j - 3
                if pe:
                    if k == 0:
                        c_n.wait(pe, p)
                        c_cl.wait(pe, NCH - 1 if isinstance(p, int) else p + 1)
                    else:
                        c_lo.wait(pe, 2 * p)
                    for t in range(TPC):
                        i_ = pe.transpose(PS[:, CT, t * P:(t + 1) * P], ntile[:, t, k * P:(k + 1) * P], ident[:, :])
                    i_.then_inc(c_t.sem, 1)
                if act:
                    c_t.wait(act, 2 * p + k)
                    act.activation(XT[0][:, k, ch], PS[:, CT, :], ACT.Copy).then_inc(c_h.sem, 1)
                if dve:
                    c_h.wait(dve, 2 * p + k)
                    dve.tensor_tensor(XT[1][:, k, ch], PS[:, CT, :], f32(XT[0][:, k, ch]), ALU.subtract)\
                        .then_inc(c_lo.sem, 1)

        def c_down(pe, c, j):
            g = (j - 1) % NU
            c_l.wait(pe, NU * c + j - 1)
            if g == 0:
                c_x.wait(pe, c - 1)
                if isinstance(c, int) and c == 0:
                    b_z.wait(pe, NCH - 1)
            down(pe, hid[g % 2], sub(DN, slice(None), g), CD, g == 0).then_inc(c_d.sem, 1)

        l_pe = event("l_pe"); l_act = event("l_act"); l_dve = event("l_dve")

        def rwkv_weights(pool, k):
            b_g.wait(pool, NF * NCH - 1)
            pool.wait_ge(s_rw, 16 * (k + 1))
            hi, lo = (W1[n][:, k, 0:3 * D].rearrange("p (a d) -> p a d", a=3) for n in range(2))
            pool.tensor_copy(hi, moe_raw[0][:, :, :])
            pool.drain()
            pool.tensor_tensor(lo, moe_raw[0][:, :, :], f32(hi), ALU.subtract).then_inc(g_rw.sem, 1)

        def b_last_tail(pe, act, dve, pool, j):
            p = NCH - 1
            ch = slice(p * CH, (p + 1) * CH)
            if j in (1, 2, 3):
                b_tail(pe, act, dve, pool, p, j)
            if j in (4, 6) and pool:
                rwkv_weights(pool, (j - 4) // 2)
            if j in (4, 5):
                k = j - 4
                if pe:
                    b_n4.wait(pe, p)
                    if k == 0:
                        c_cl.wait(pe, 0)
                    l_dve.wait(pe, k - 1)
                    for t in range(TPC):
                        i_ = pe.transpose(PS[:, CT, t * P:(t + 1) * P], ntile[:, t, k * P:(k + 1) * P], ident[:, :])
                    i_.then_inc(l_pe.sem, 1)
                if act:
                    l_pe.wait(act, k)
                    act.activation(XT[0][:, k, ch], PS[:, CT, :], ACT.Copy).then_inc(l_act.sem, 1)
                if dve:
                    l_act.wait(dve, k)
                    dve.tensor_tensor(XT[1][:, k, ch], PS[:, CT, :], f32(XT[0][:, k, ch]), ALU.subtract)\
                        .then_inc(l_dve.sem, 1)
            if j == 6:
                if pe:
                    l_dve.wait(pe, KC - 1)
                    for k in range(KC):
                        i_ = mm3(pe, PS[:, CT, :], sub(gT, slice(None), k), sub(XT, slice(None), k, ch),
                                 k == 0, k == KC - 1)
                    i_.then_inc(l_pe.sem, 1)
                if act:
                    l_pe.wait(act, 2)
                    act.activation(lgT[:, :], PS[:, CT, :], ACT.Copy).then_inc(l_act.sem, 1)
            if j == 7:
                if pe:
                    l_act.wait(pe, 2)
                    for t in range(TPC):
                        i_ = pe.transpose(PS[:, CT, t * P:(t + 1) * P], lgT[:, t * P:(t + 1) * P], ident[:, :])
                    i_.then_inc(l_pe.sem, 1)
                if act:
                    l_pe.wait(act, 3)
                    act.activation(ex[:, :, :], PS[:, CT, :].rearrange("p (t e) -> p t e", t=TPC)[:, :, 0:E], ACT.Exp,
                                   scale=-1.0).then_inc(l_act.sem, 1)
            if j == 8:
                if dve:
                    l_act.wait(dve, 3)
                    b_cm.wait(dve, p - 1)
                    route(dve, p, 0)
                if pe:
                    l_act.wait(pe, 3)
            if j == 9:
                if dve:
                    route(dve, p, 1)
                if pool:
                    combine(pool, p)

        def combine_rows(pe, act, dve, c):
            if pe:
                c_cs.wait(pe, c)
                c_lo.wait(pe, 2 * c - 3)
                for t in range(TPC):
                    i_ = pe.transpose(PS[0:E, CT, t * P:(t + 1) * P], cst[:, t, :], ident[:, :])
                i_.then_inc(c_ct.sem, 1)
            if act:
                c_ct.wait(act, c)
                c_bc.wait(act, NR * c - 1)
                act.activation(cT[0:E, :], PS[0:E, CT, :], ACT.Copy).then_inc(c_ch.sem, 1)
            if dve:
                c_ch.wait(dve, c)
                dve.tensor_tensor(cT[LO_ROW:LO_ROW + E, :], PS[0:E, CT, :], f32(cT[0:E, :]), ALU.subtract)\
                   .then_inc(c_cl.sem, 1)

        def c_chunk(pe, act, dve, pool, c, tail):
            ch = bass.ds(c * CH, CH)
            if dve:
                b_cm.wait(dve, c)
                c_ct.wait(dve, c - 1)
                dve.tensor_copy(cst[:, :, :], tiles4(cmb, c)).then_inc(c_cs.sem, 1)
            for j in range(NU):
                u = NU * c + j
                e = j - 2
                v = NR * c + e
                q = j % 2
                if pe:
                    c_s.wait(pe, u - 2)
                    c_l.wait(pe, u - 2)
                    for half_, bank in ((0, CG), (1, CU)):
                        w0 = (2 * j + half_) * I
                        for k in range(KC):
                            i_ = mm3(pe, PS[:, bank + q, :], sub(GU, slice(None), k, slice(w0, w0 + I)),
                                     sub(XT, slice(None), k, ch), k == 0, k == KC - 1)
                        i_.then_inc((c_g if half_ == 0 else c_uo).sem, 1)
                    if e >= 0:
                        c_cl.wait(pe, c)
                        c_m.wait(pe, v - 1)
                        pe.matmul(PS[:, CB, :], sel[:, e, :], cT[:, :], start=True, stop=True).then_inc(c_bc.sem, 1)
                if act:
                    c_g.wait(act, u)
                    c_l.wait(act, u - 2)
                    act.activation(work[q][:, :], PS[:, CG + q, :], ACT.Silu).then_inc(c_s.sem, 1)
                if dve:
                    c_s.wait(dve, u)
                    c_uo.wait(dve, u)
                    hv = work[2 + q]
                    dve.tensor_tensor(hv[:, :], PS[:, CU + q, :], work[q][:, :], ALU.mult)
                    dve.drain()
                    if e >= 0:
                        c_bc.wait(dve, v)
                        dve.tensor_tensor(hv[:, :], PS[:, CB, :], hv[:, :], ALU.mult).then_inc(c_m.sem, 1)
                        dve.drain()
                    c_d.wait(dve, u - 2)
                    dve.tensor_copy(hid[q][0][:, :], hv[:, :])
                    dve.drain()
                    dve.tensor_tensor(hid[q][1][:, :], hv[:, :], f32(hid[q][0][:, :]), ALU.subtract)\
                        .then_inc(c_l.sem, 1)
                if j == 0 and not tail:
                    b_tail(pe, act, dve, pool, NCH - 1, 0)
                if pe and (tail or j):
                    c_down(pe, c, j)
                if j == 0:
                    combine_rows(pe, act, dve, c)
                if tail:
                    c_tail(pe, act, dve, pool, c - 1, j)
                else:
                    b_last_tail(pe, act, dve, pool, j)

        def stage_c(pe, act, dve, pool, sp):
            if sp:
                for k in range(KC):
                    g_moe.wait(sp, NU - 1)
                    if k:
                        g_rw.wait(sp, k - 1)
                    sp.dma_start(moe_raw[0][:, :, :], rw[k * P:(k + 1) * P, :].rearrange("p (a d) -> p a d", a=3))\
                        .then_inc(s_rw, 16)
            if pe:
                g_moe.wait(pe, NU - 1)
            if act:
                b_l.wait(act, NF * NCH - 1)
                act.activation(warm[:, :], tg[:, 0:1], ACT.Silu)
            eng = pe or act or dve or pool
            if not eng:
                return
            c_chunk(pe, act, dve, pool, 0, False)
            with eng.Fori(1, NCH) as c:
                c_chunk(pe, act, dve, pool, c, True)
            if pe:
                c_down(pe, NCH, 0)

        d_s = event("d_s"); d_mx = event("d_mx"); d_ex = event("d_ex"); d_at = event("d_at")
        d_o = event("d_o"); d_z = event("d_z"); d_v = event("d_v"); d_r = event("d_r"); d_n = event("d_n")
        d_na = event("d_na"); d_t = event("d_t"); d_xd = event("d_xd")
        O_BANK = (4, 6, 2, 4)

        def d_scores(pe, act, dve, pool, sp, b):
            sc_ps = PS[0:M, 2 * b:2 * b + 2, :]
            if pe:
                c_lo.wait(pe, 2 * (TPB // TPC) * (b + 1) - 1)
                if b:
                    c_x.wait(pe, NCH - 1)
                else:
                    c_s.wait(pe, NU * NCH - 1)
                for j in range(2):
                    for k in range(KC):
                        i_ = mm3(pe, PS[0:M, 2 * b + j, :], sub(Bctx, slice(None), k, slice(b * M, (b + 1) * M)),
                                 sub(XT, slice(None), k, slice(b * S + j * CH, b * S + (j + 1) * CH)),
                                 k == 0, k == KC - 1)
                i_.then_inc(d_s.sem, 1)
            if dve:
                d_s.wait(dve, b)
                dve.tensor_reduce(nmax[:, b:b + 1], sc_ps, AX.XY, ALU.max, negate=True).then_inc(d_mx.sem, 1)
            if act:
                d_mx.wait(act, b)
                d_at.wait(act, b - 1)
                act.activation(att[:, :].rearrange("m (j t) -> m j t", j=2), sc_ps, ACT.Exp,
                               bias=nmax[:, b:b + 1], accum_out=asum[:, b:b + 1])
                act.drain()
                act.sem_inc(d_ex.sem, 1)

        def d_weights(pe, act, dve, pool, sp, b):
            if dve:
                d_ex.wait(dve, b)
                d_o.wait(dve, 2 * b - 1)
                dve.reciprocal(ascl[:, :], asum[:, b:b + 1])
                dve.tensor_copy(attp[0][:, :], att[:, :])
                dve.drain()
                dve.scalar_tensor_tensor(c2f[:, :], C2[:, b, :], tg[0:M, 1:2], ascl[:, 0:1].to_broadcast([M, D]),
                                         ALU.mult, ALU.mult)
                dve.tensor_tensor(attp[1][:, :], att[:, :], f32(attp[0][:, :]), ALU.subtract)
                dve.drain()
                dve.tensor_copy(c2s[0][:, :], c2f[:, :])
                dve.drain()
                dve.tensor_tensor(c2s[1][:, :], c2f[:, :], f32(c2s[0][:, :]), ALU.subtract)
                dve.drain()
                dve.sem_inc(d_at.sem, 1)

        def x_rows(i, t):
            return X[:, i * TPC + t, :]

        def stat_cols(i):
            return TPC * ((i + 1) % 2)

        def d_out(pe, act, dve, pool, sp, i):
            bank = O_BANK[i]
            if pe:
                d_at.wait(pe, i // 2)
                for ev, n in (((c_l, NU * NCH - 1),), ((c_m, NR * NCH - 1), (c_lo, 2 * NCH - 1)), ((d_ex, 1),),
                              ((d_z, 0),))[i]:
                    ev.wait(pe, n)
                for t in range(TPC):
                    tok = slice(((i % 2) * TPC + t) * P, ((i % 2) * TPC + t + 1) * P)
                    i_ = mm3(pe, PS[:, bank + t // 2, (t % 2) * D:(t % 2 + 1) * D],
                             sub(attp, slice(None), tok), sub(c2s, slice(None), slice(None)), True, True)
                i_.then_inc(d_o.sem, 1)
            if dve:
                d_o.wait(dve, i)
                for q in range(2):
                    xr_ = X[:, i * TPC + 2 * q:i * TPC + 2 * q + 2, :]
                    i_ = dve.tensor_tensor(xr_, PS[:, bank + q, :].rearrange("p (a d) -> p a d", a=2), xr_, ALU.add)
                i_.then_inc(d_z.sem, 1)

        def d_stats(pe, act, dve, pool, sp, i):
            k0 = stat_cols(i)
            if dve:
                d_n.wait(dve, i - 2)
                d_na.wait(dve, i - 2)
                dve.drain()
                stats(dve, [x_rows(i, t) for t in range(TPC)], k0, TPC).then_inc(d_v.sem, 1)
            if pool:
                d_v.wait(pool, i)
                rsqrt(pool, k0, TPC)
                pool.drain()
                pool.tensor_tensor(nm4[:, k0:k0 + TPC], mv[:, k0:k0 + TPC, 0], rstd[:, k0:k0 + TPC], ALU.mult)
                pool.drain()
                pool.tensor_scalar(nm4[:, k0:k0 + TPC], nm4[:, k0:k0 + TPC], -1.0, 0.0, ALU.mult, ALU.add)\
                    .then_inc(d_r.sem, 1)

        def d_norm(pe, act, dve, pool, sp, i):
            nb, k0 = (ztile, ntile)[i % 2], stat_cols(i)
            for eng, ts, ev in ((act, range(0, N_ACT), d_na), (dve, range(N_ACT, TPC), d_n)):
                if eng:
                    d_r.wait(eng, i)
                    d_t.wait(eng, i - 2)
                    if i == 1:
                        c_t.wait(eng, 2 * NCH - 1)
                    for t in ts:
                        if eng is act:
                            i_ = act.activation(nb[:, t, :], x_rows(i, t), ACT.Identity,
                                                bias=nm4[:, k0 + t:k0 + t + 1], scale=rstd[:, k0 + t:k0 + t + 1])
                        else:
                            i_ = dve.tensor_scalar(nb[:, t, :], x_rows(i, t), mv[:, k0 + t, 0:1],
                                                   rstd[:, k0 + t:k0 + t + 1], ALU.subtract, ALU.mult)
                    i_.then_inc(ev.sem, 1)

        def d_transposes(pe, act, dve, pool, sp, i):
            nb = (ztile, ntile)[i % 2]
            if pe:
                d_n.wait(pe, i)
                d_na.wait(pe, i)
                d_ex.wait(pe, 0)
                d_xd.wait(pe, i - 1)
                for k in range(KC):
                    for t in range(TPC):
                        i_ = pe.transpose(PS[:, k, t * P:(t + 1) * P], nb[:, t, k * P:(k + 1) * P], ident[:, :])
                i_.then_inc(d_t.sem, 1)
            if act:
                d_t.wait(act, i)
                o = (i // 2) * (S + 1) + 1 + (i % 2) * CH
                for k in range(KC):
                    i_ = act.activation(XD[:, k, o:o + CH], PS[:, k, :], ACT.Copy)
                i_.then_inc(d_xd.sem, 1)

        e_df = event("e_df"); e_mx = event("e_mx"); e_xh = event("e_xh"); e_lk = event("e_lk")
        e_lr = event("e_lr")
        e_k = event("e_k"); e_s = event("e_s"); e_ah = event("e_ah"); e_kl = event("e_kl"); e_r = event("e_r")
        e_sg = event("e_sg"); e_sq = event("e_sq"); e_vo = event("e_vo"); e_m = event("e_m", per=2)
        e_o = event("e_o", per=2)
        e_ol = event("e_ol", per=2)
        e_st = sem("e_st")

        def odd(c, n):
            return tuple(XT[h][:, :, n * CH:(n + 1) * CH] for h in range(2))

        def xm_of(n, c):
            return odd(c, n) if c % 2 else tuple(h[:, :, :] for h in xm[n])

        def ka_of(c):
            return odd(c, 2) if c % 2 else tuple(h[:, :, :] for h in ka)

        def e_mix(pe, act, dve, pool, sp, c, n=0):
            off = (c // 2) * (S + 1) + (c % 2) * CH
            if pool and n == 0:
                d_xd.wait(pool, c)
                e_mx.wait(pool, 2 * c - 1)
                pool.tensor_tensor(dif[:, :, :], XD[:, :, off + 1:off + 1 + CH], XD[:, :, off:off + CH],
                                   ALU.subtract).then_inc(e_df.sem, 1)
            cc = (C_MUK, C_MUR)[n]
            m = 2 * c + n
            if dve:
                e_df.wait(dve, c)
                e_xh.wait(dve, m - 2)
                e_lr.wait(dve, c - 1)
                for k in range(KC):
                    i_ = dve.scalar_tensor_tensor(xmix[n][:, k, :], dif[:, k, :], col[:, k, cc:cc + 1],
                                                  XD[:, k, off:off + CH], ALU.mult, ALU.add)
                i_.then_inc(e_mx.sem, 1)
            if act:
                e_mx.wait(act, m)
                (e_r if n else e_k).wait(act, c - 2)
                d_s.wait(act, 1)
                act.activation(xm_of(n, c)[0], xmix[n][:, :, :], ACT.Copy).then_inc(e_xh.sem, 1)
            eng, ev = (pool, e_lr) if n else (dve, e_lk)
            if eng:
                e_xh.wait(eng, m)
                eng.tensor_tensor(xm_of(n, c)[1], xmix[n][:, :, :], f32(xm_of(n, c)[0]), ALU.subtract)\
                   .then_inc(ev.sem, 1)

        def e_key(pe, act, dve, pool, sp, c):
            bank = 0 if c % 2 else 6
            if pe:
                e_lk.wait(pe, c)
                if c == 0:
                    g_rw.wait(pe, KC - 1)
                    d_z.wait(pe, 1)
                elif c == 1:
                    d_xd.wait(pe, NCH - 1)
                e_s.wait(pe, c - 2)
                for f in range(KC):
                    for k in range(KC):
                        i_ = mm3(pe, PS[:, bank + f, :], sub(W1, slice(None), k, slice(D + f * P, D + (f + 1) * P)),
                                 sub(xm_of(0, c), slice(None), k), k == 0, k == KC - 1)
                i_.then_inc(e_k.sem, 1)
            k_ps = PS[:, bank:bank + KC, :]
            if act:
                e_k.wait(act, c)
                e_kl.wait(act, c - 1)
                act.activation(sq[:, :, :], k_ps, ACT.Relu).then_inc(e_s.sem, 1)
            if dve:
                e_s.wait(dve, c)
                dve.tensor_tensor(sq[:, :, :], sq[:, :, :], sq[:, :, :], ALU.mult).then_inc(e_sq.sem, 1)

        def e_key_pair(pe, act, dve, pool, sp, c):
            if act:
                e_sq.wait(act, c)
                e_vo.wait(act, c - 2)
                act.activation(ka_of(c)[0], sq[:, :, :], ACT.Copy).then_inc(e_ah.sem, 1)
            if dve:
                e_ah.wait(dve, c)
                dve.tensor_tensor(ka_of(c)[1], sq[:, :, :], f32(ka_of(c)[0]), ALU.subtract)\
                   .then_inc(e_kl.sem, 1)

        def e_gate(pe, act, dve, pool, sp, c):
            if pe:
                e_lr.wait(pe, c)
                d_z.wait(pe, NCH - 1)
                e_sg.wait(pe, c - 1)
                for t in range(TPC):
                    for k in range(KC):
                        i_ = mm3(pe, PS[:, 4 + t // 2, (t % 2) * D:(t % 2 + 1) * D],
                                 sub(xm_of(1, c), slice(None), k, slice(t * P, (t + 1) * P)),
                                 sub(W1, slice(None), k, slice(0, D)), k == 0, k == KC - 1)
                i_.then_inc(e_r.sem, 1)
            if act:
                e_r.wait(act, c)
                e_o.wait(act, c - 2, 1)
                act.activation(rs[c % 2][:, :, :], PS[:, 4:6, :], ACT.Sigmoid).then_inc(e_sg.sem, 1)

        def e_value(pe, act, dve, pool, sp, c):
            r_ = rs[c % 2]
            if pe:
                e_kl.wait(pe, c)
                d_z.wait(pe, NCH - 2)
                e_m.wait(pe, c - 1, 1)
                for t in range(TPC):
                    for f in range(KC):
                        i_ = mm3(pe, PS[:, 2 + t // 2, (t % 2) * D:(t % 2 + 1) * D],
                                 sub(ka_of(c), slice(None), f, slice(t * P, (t + 1) * P)),
                                 sub(W1, slice(None), f, slice(2 * D, 3 * D)), f == 0, f == KC - 1)
                i_.then_inc(e_vo.sem, 1)
            if dve:
                e_vo.wait(dve, c)
                e_sg.wait(dve, c)
            for q in range(2):
                if dve:
                    dve.scalar_tensor_tensor(r_[:, q, :], PS[:, 2 + q, :], tg[:, 3:4], r_[:, q, :],
                                             ALU.mult, ALU.mult).then_inc(e_m.sem, 1)
                last = c == NCH - 1
                eng, ev, n = (dve, e_ol, 0) if last else (pool, e_o, c)
                x2 = X[:, c * TPC + 2 * q:c * TPC + 2 * q + 2, :]
                if eng:
                    e_m.wait(eng, c, q)
                    eng.tensor_tensor(x2, r_[:, q, :].rearrange("p (a d) -> p a d", a=2), x2, ALU.add)\
                       .then_inc(ev.sem, 1)
                if sp:
                    ev.wait(sp, n, q)
                    sp.dma_start(ov[:, c * TPC + 2 * q:c * TPC + 2 * q + 2, :], x2).then_inc(e_st, 16)

        def c_tail_phase(pe, act, dve, pool, sp, j):
            c_tail(pe, act, dve, pool, NCH - 1, j)

        def e_mix_r(pe, act, dve, pool, sp, c):
            e_mix(pe, act, dve, pool, sp, c, 1)

        PHASES = {"t": c_tail_phase, "S": d_scores, "W": d_weights, "O": d_out, "Q": d_stats, "N": d_norm,
                  "T": d_transposes, "x": e_mix, "y": e_mix_r, "k": e_key, "l": e_key_pair, "r": e_gate, "v": e_value}
        SCHEDULE = ("t0 t1 S0 t2 t3 t4 W0 S1 O0 Q0 O1 N0 T0 Q1 W1 N1 x0 O2 Q2 y0 T1 O3 N2 Q3 "
                    "k0 l0 T2 N3 r0 T3 x1 v0 y1 k1 l1 x2 y2 r1 v1 k2 l2 x3 r2 y3 v2 k3 l3 r3 v3")
        N_ACT = 2

        def layer1(pe, act, dve, pool, sp):
            if act:
                act.activation(warm[:, :], tg[:, 0:1], ACT.Exp)
            if pool:
                c_d.wait(pool, NU * NCH - 1)
                for b in range(B):
                    pool.memset(XD[:, :, b * (S + 1):b * (S + 1) + 1], 0.0)
                pool.drain()
            for ph in SCHEDULE.split():
                PHASES[ph[0]](pe, act, dve, pool, sp, int(ph[1:]))
                if ph == "S1" and act:
                    act.activation(warm[:, :], tg[:, 0:1], ACT.Sigmoid)
            if sp:
                sp.wait_ge(e_st, 16 * 2 * NCH)

        def program(pe, act, dve, pool, sp):
            if sp:
                for ev in events:
                    if ev.credit:
                        sp.sem_inc(ev.sem, ev.credit)
                rawv = raw.rearrange("(k p) n -> p k n", p=P)
                load(sp, "kv", ctx_sb[:, :, :], ctxT.rearrange("(k p) n -> p k n", p=P))
                load(sp, "kv", rawA[:, :, 0:2 * D], rawv[:, :, 0:2 * D])
                load(sp, "x0", X[:, 0:TPC, :], xv[:, 0:TPC, :])
                load(sp, "m", rawA[:, :, 2 * D:4 * D], rawv[:, :, 2 * D:4 * D])
                load(sp, "m", ntile[0:1, :, :], brow[0:4, :].rearrange("(a n) d -> a n d", a=1))
                load(sp, "m", ztile[0:1, 3, :], brow[4:5, :])
                load(sp, "q", rawA[:, :, 4 * D:6 * D], rawv[:, :, 4 * D:6 * D])
                load(sp, "x", X[:, TPC:, :], xv[:, TPC:, :])
                load(sp, "e", rawA[:, :, 6 * D:8 * D], rawv[:, :, 6 * D:8 * D])
                load(sp, "e", gT_raw[:, :, :], gateT.rearrange("(k p) n -> p k n", p=P))
                load(sp, "w1", w1raw[:, :, :], w1.rearrange("(k p) n -> p k n", p=P))
                load(sp, "w1", b1col[:, :], l1b)
                load(sp, "w2", w2raw[:, :, :], w2.rearrange("p (f d) -> p f d", f=NF))
            if act:
                load(act, "col", col[:, :, :], cols.rearrange("(k p) n -> p k n", p=P))
                load(act, "bc", gate_raw[:, :], gates.rearrange("(a n) -> a n", a=1).to_broadcast([P, 4]))
                load(act, "bc", bc[:, :, :], bcast.rearrange("(a n) d -> a n d", a=1).to_broadcast([P, NBC, D]))
            if pool:
                pool.memset(ident[:, :], 0.0)
                pool.memset(f32(ones[:, :]), 0.0)
                pool.memset(half[:, :], -0.5)
                for n in range(2):
                    pool.memset(Pm[n][:, :], 0.0)
                    pool.memset(work[2 + n][:, :], 0.0)
                pool.memset(lay_v1[:, :, :], 0.0)
                pool.memset(f32(bias[:, :]), 0.0)
                pool.memset(f32(sbias[:, :, :, :]), 0.0)
                pool.memset(f32(b2row[:, :]), 0.0)
                pool.memset(rstd0[:, :], -0.5)
                for n in range(2):
                    pool.memset(f32(gT[n][:, :, E:P]), 0.0)
                pool.iota(iota[:, :], [[1, E]], base=0, channel_multiplier=0, allow_small_or_imprecise_dtypes=True)
                pool.drain()
                pool.memset(f32(ones[0:1, :]), 1.0)
                pool.memset(f32(ones[32:33, :]), 1.0)
                pool.drain()
                pool.affine_select(out=ident[:, :], in_=ident[:, :], compare_op=ALU.not_equal, fill=1.0,
                                   base=0, pattern=[[-1, P]], channel_multiplier=1)
                done(pool, "const")

            def w(k, which, j):
                return rawA[:, k, which * D + j * P: which * D + (j + 1) * P]

            def wrow(k, which):
                return rawA[:, k, which * D:(which + 1) * D]

            brow_raw = [ntile[0:1, n, :] for n in range(4)] + [ztile[0:1, 3, :]]
            brow_sum = [brow_raw[BR_SO], brow_raw[BR_O], brow_raw[BR_F2]]
            kv = work
            scale = float(DH) ** -0.5
            A0B, VWB, MB, VW1B, C2B, L1B = 4, 0, 2, 4, 3, 7

            def row_banks(p, b):
                return [(PS[p, A0B + 2 * j + k, HM:HM + 2 * M], (b, k, slice(j * 2 * M, (j + 1) * 2 * M)))
                        for k in range(2) for j in range(KC)]

            def scores_matrix(pe, b):
                need(pe, f"layk{b}")
                for j in range(KC):
                    for k in range(2):
                        pe.matmul(PS[:, A0B + 2 * j + k, 0:HM], w(k, W_Q, j), lay_k[b][k][:, 0:HM],
                                  start=True, stop=True)
                need(pe, "u")
                for k in range(2):
                    for j in range(KC):
                        pe.matmul(PS[0:1, A0B + 2 * j + k, HM:HM + 2 * M], ucol[:, k:k + 1],
                                  lay_k[b][k][:, j * 2 * M:(j + 1) * 2 * M], start=True, stop=True)
                done(pe, f"a{b}_ps")

            def value_matrix(pe, b, bank):
                need(pe, f"layv{b}")
                need(pe, "a1_sb" if b else "m_sb")
                for r in range(NV):
                    parts = [(j, r - j * (NV - NW)) for j in range(KC) if 0 <= r - j * (NV - NW) < NW]
                    for j, q in parts:
                        pe.matmul(PS[:, bank + r // 2, (r % 2) * D:(r % 2 + 1) * D],
                                  lay_v[b][j][:, q * P:(q + 1) * P], wrow(j, W_O),
                                  start=(j, q) == parts[0], stop=(j, q) == parts[-1])
                done(pe, f"vw{b}_ps")

            if pe:
                need(pe, "const")
                loaded(pe, "kv")
                for j in range(KC):
                    for which, c0 in ((W_K, 0), (W_VM, B * M)):
                        for k in range(KC):
                            pe.matmul(PS[:, j, c0:c0 + B * M], w(k, which, j), ctx_sb[:, k, :],
                                      start=(k == 0), stop=(k == KC - 1))
                done(pe, "kv_ps")
                loaded(pe, "m")
                loaded(pe, "col")
                for j in range(KC):
                    for k in range(KC):
                        pe.matmul(PS[:, MB, j * D:(j + 1) * D], w(k, W_V, j), wrow(k, W_SO),
                                  start=(k == 0), stop=(k == KC - 1))
                for k in range(KC):
                    pe.matmul(PS[0:1, MB + 1, 0:D], col[:, k, C_BV:C_BV + 1], wrow(k, W_SO),
                              start=(k == 0), stop=(k == KC - 1))
                done(pe, "m_ps")
                loaded(pe, "q")
                scores_matrix(pe, 0)
                value_matrix(pe, 0, VWB)
                loaded(pe, "e")
                for b in range(B):
                    for k in range(KC):
                        pe.matmul(PS[0:M, C2B, b * D:(b + 1) * D], ctx_sb[:, k, b * M:(b + 1) * M],
                                  wrow(k, W_2), start=(k == 0), stop=(k == KC - 1))
                done(pe, "c2_ps")
                need(pe, "a0_sb")
                scores_matrix(pe, 1)

            def lay_out(eng, lay, n, b, name, on_act=False):
                for k in range(KC):
                    for h in range(HH):
                        r = slice(h * DH, (h + 1) * DH)
                        src = kv[k][r, (n * B + b) * M:(n * B + b + 1) * M]
                        dst = lay[b][k][r, n * k * V_OFF + h * M:n * k * V_OFF + (h + 1) * M]
                        if on_act:
                            eng.activation(dst, src, ACT.Copy)
                        else:
                            eng.tensor_copy(dst, src)
                done(eng, name)

            def high_parts(act, b):
                need(act, f"a{b}_ps")
                for j in range(KC):
                    for k in range(2):
                        act.activation(A[0][:, b, j, k, :], PS[:, A0B + 2 * j + k, 0:HM], ACT.Identity,
                                       scale=col[:, j, C_G1:C_G1 + 1])
                for src, (b_, k, c_) in row_banks(slice(0, 1), b):
                    act.activation(sbias[0:1, b_, k, c_], src, ACT.Copy)
                done(act, f"ahi{b}")

            def vw_blocks(bank, r):
                n = min(2, NV - r)
                return PS[:, bank + r // 2, 0:n * D].rearrange("p (a d) -> p a d", a=n)

            def high_vw(act, b, bank):
                need(act, f"vw{b}_ps")
                for r in range(0, NV, 2):
                    act.activation(VW[0][:, b, r:min(r + 2, NV), :], vw_blocks(bank, r), ACT.Copy)
                done(act, f"vwhi{b}")

            def low_parts(dve, b):
                need(dve, f"ahi{b}")
                for j in range(KC):
                    for k in range(2):
                        dve.scalar_tensor_tensor(A[1][:, b, j, k, :], PS[:, A0B + 2 * j + k, 0:HM],
                                                 col[:, j, C_G1:C_G1 + 1], f32(A[0][:, b, j, k, :]),
                                                 ALU.mult, ALU.subtract)
                for src, (b_, k, c_) in row_banks(slice(0, 1), b):
                    dve.tensor_tensor(sbias[32:33, b_, k, c_], src, f32(sbias[0:1, b_, k, c_]), ALU.subtract)
                done(dve, f"a{b}_sb")

            def low_vw(dve, b, bank):
                need(dve, f"vwhi{b}")
                for r in range(0, NV, 2):
                    blk = slice(r, min(r + 2, NV))
                    dve.tensor_tensor(VW[1][:, b, blk, :], vw_blocks(bank, r), f32(VW[0][:, b, blk, :]), ALU.subtract)
                done(dve, f"vw{b}_sb")

            def ln0_stats(dve, g):
                ts = range(g * TPC, (g + 1) * TPC)
                loaded(dve, "x" if g else "x0")
                for t in ts:
                    dve.bn_stats(stat0[:, t, :], X[:, t, :])
                dve.drain()
                for t in ts:
                    dve.bn_aggr(mv0[:, t, :], stat0[:, t, :])
                dve.drain()
                dve.tensor_scalar(var0[:, ts[0]:ts[-1] + 1], mv0[:, ts[0]:ts[-1] + 1, 1], EPS, None, ALU.add)
                done(dve, f"stat0_{g}")

            def ln0_scale(pool, g):
                c4 = slice(g * TPC, (g + 1) * TPC)
                need(pool, f"stat0_{g}")
                pool.tensor_tensor(rstd0[:, c4], var0[:, c4], rstd0[:, c4], ALU.pow)
                pool.drain()
                pool.tensor_tensor(nmr0[:, c4], mv0[:, c4, 0], rstd0[:, c4], ALU.mult)
                pool.drain()
                pool.tensor_scalar(nmr0[:, c4], nmr0[:, c4], -1.0, 0.0, ALU.mult, ALU.add)
                done(pool, f"ln0_{g}")

            bk = PS[:, L1B, 0:KC * B * M].rearrange("p (j c) -> p j c", j=KC)

            def late_products(pe, s):
                if s == 0:
                    need(pe, "c2_sb")
                if s == 1:
                    value_matrix(pe, 1, VW1B)
                if s == 2:
                    need(pe, "a1_sb")
                    for j in range(KC):
                        for k in range(KC):
                            pe.matmul(PS[:, L1B, j * B * M:(j + 1) * B * M], w(k, W_E, j), ctx_sb[:, k, :],
                                      start=(k == 0), stop=(k == KC - 1))
                    loaded(pe, "w1")
                if s in (2, 3):
                    for f in {2: (0, 1, 2), 3: (3, 4, 5, 6, 7)}[s]:
                        for k in range(KC):
                            pe.matmul(PS[:, L1B, KC * B * M + f:KC * B * M + f + 1],
                                      w1raw[:, k, f * P:(f + 1) * P], col[:, k, C_B2:C_B2 + 1],
                                      start=(k == 0), stop=(k == KC - 1))
                if s == 3:
                    done(pe, "l1_ps")

            def late_dve(dve, s):
                if s == 0:
                    low_parts(dve, 1)
                if s == 2:
                    low_vw(dve, 1, VW1B)
                if s == LAG - 1:
                    need(dve, "l1_ps")
                    dve.tensor_copy(Bctx[0][:, :, :], bk)
                    dve.tensor_tensor(b1col[:, :], PS[:, L1B, KC * B * M:KC * B * M + NF], b1col[:, :], ALU.add)
                    dve.drain()
                    dve.tensor_tensor(Bctx[1][:, :, :], bk, f32(Bctx[0][:, :, :]), ALU.subtract)
                    done(dve, "l1_sb")
                if s + 1 in range(1, NT // TPC):
                    ln0_stats(dve, s + 1)
                if s in FFN_DVE:
                    ffn_weights(None, dve, None, FFN_DVE[s])

            def late_setup(act, dve, pool, s):
                if s == -1 and act:
                    high_parts(act, 1)
                if s == 1 and act:
                    high_vw(act, 1, VW1B)
                if pool and s + 1 in range(1, NT // TPC):
                    ln0_scale(pool, s + 1)
                if s in FFN_ACT:
                    ffn_weights(act, None, pool, FFN_ACT[s])

            def late_work(pe, dve, s):
                if pe:
                    late_products(pe, s)
                if dve:
                    late_dve(dve, s)

            if dve:
                need(dve, "const")
                loaded(dve, "col")
                ln0_stats(dve, 0)
                need(dve, "kv_ps")
                for k in range(KC):
                    dve.tensor_scalar(kv[k][:, 0:B * M], PS[:, k, 0:B * M], col[:, k, C_BK:C_BK + 1],
                                      scale, ALU.add, ALU.mult)
                done(dve, "k_sb")
                lay_out(dve, lay_k, 0, 0, "layk0")
                loaded(dve, "q")
                loaded(dve, "bc")
                for k in range(KC):
                    dve.tensor_tensor(utmp[:, k, :], wrow(k, W_Q), bc[:, R_B1, :], ALU.mult)
                dve.drain()
                dve.tensor_reduce(ucol[:, :], utmp[:, :, :], AX.X, ALU.add)
                dve.drain()
                dve.tensor_tensor(ucol[:, :], ucol[:, :], col[:, :, C_BQ], ALU.add)
                done(dve, "u")
                need(dve, "m_ps")
                loaded(dve, "m")
                for j in range(KC):
                    for k in range(KC):
                        dst = ztile[:, j, k * P:(k + 1) * P]
                        src = PS[:, MB, j * D + k * P:j * D + (k + 1) * P]
                        if j == k:
                            dve.tensor_tensor(dst, src, ident[:, :], ALU.add)
                        else:
                            dve.tensor_copy(dst, src)
                dve.tensor_tensor(brow_sum[0], PS[0:1, MB + 1, 0:D], brow_raw[BR_SO], ALU.add)
                done(dve, "m_sb")
                dve.tensor_tensor(brow_sum[1], brow_raw[BR_O], brow_raw[BR_B1], ALU.add)
                dve.tensor_tensor(brow_sum[2], brow_raw[BR_F2], brow_raw[BR_B2], ALU.add)
                dve.tensor_copy(Mt[0][:, :, :], ztile[:, 0:KC, :])
                dve.drain()
                rows = ((bias[:, 0:D], 0), (bias[:, D:2 * D], 1), (b2row[:, :], 2))
                for t_, n in rows:
                    dve.tensor_copy(t_[0:1, :], brow_sum[n])
                dve.drain()
                dve.tensor_tensor(Mt[1][:, :, :], ztile[:, 0:KC, :], f32(Mt[0][:, :, :]), ALU.subtract)
                for t_, n in rows:
                    dve.tensor_tensor(t_[32:33, :], brow_sum[n], f32(t_[0:1, :]), ALU.subtract)

                low_parts(dve, 0)
                low_vw(dve, 0, VWB)
                done(dve, "setup")
            if act:
                loaded(act, "bc")
                act.activation(tg[:, :], gate_raw[:, :], ACT.Tanh)
                done(act, "tanh")
                loaded(act, "col")
                need(act, "k_sb")
                for k in range(KC):
                    act.activation(kv[k][:, B * M:2 * B * M], PS[:, k, B * M:2 * B * M], ACT.Identity,
                                   bias=col[:, k, C_BVM:C_BVM + 1])
                done(act, "kv_sb")
                lay_out(act, lay_k, 0, 1, "layk1", True)
                high_parts(act, 0)
                high_vw(act, 0, VWB)
                need(act, "c2_ps")
                act.activation(C2[:, :, :], PS[0:M, C2B, :].rearrange("m (b d) -> m b d", b=B), ACT.Copy)
                done(act, "c2_sb")
            if pool:
                ln0_scale(pool, 0)
                need(pool, "kv_sb")
                for b in range(B):
                    lay_out(pool, lay_v, 1, b, f"layv{b}")
                loaded(pool, "bc")
                need(pool, "tanh")
                for r_ in (R_G3, R_B3):
                    pool.tensor_scalar(bc[:, r_, :], bc[:, r_, :], tg[:, 0:1], 0.0, ALU.mult, ALU.add)
                loaded(pool, "e")
                pool.tensor_copy(gT[0][:, :, 0:E], gT_raw[:, :, :])
                pool.drain()
                pool.tensor_tensor(gT[1][:, :, 0:E], gT_raw[:, :, :], f32(gT[0][:, :, 0:E]), ALU.subtract)

            stage_a_tiles(pe, act, dve, pool, sp, late_setup, late_work)
            stage_b(pe, act, dve, pool, sp)
            stage_c(pe, act, dve, pool, sp)
            layer1(pe, act, dve, pool, sp)

        @block.sync
        def _(eng):
            program(None, None, None, None, eng)

        @block.tensor
        def _(eng):
            program(eng, None, None, None, None)

        @block.scalar
        def _(eng):
            program(None, eng, None, None, None)

        @block.vector
        def _(eng):
            program(None, None, eng, None, None)

        @block.gpsimd
        def _(eng):
            program(None, None, None, eng, None)



def kernel(**inputs):
    import numpy as np
    import concourse.bacc as bacc
    from concourse.bass_utils import run_bass_kernel_spmd

    f = {k: np.asarray(v) for k, v in inputs.items()}
    a = {k[9:]: v for k, v in f.items() if k.startswith("L0_xattn_")}
    m = {k[7:]: v for k, v in f.items() if k.startswith("L0_ffn_")}
    r = {k[7:]: v for k, v in f.items() if k.startswith("L1_ffn_")}
    c = np.concatenate
    raw = c([a["in_proj_w"][D:2 * D].T, a["in_proj_w"][2 * D:].T, a["qkv_w"][2 * D:], a["sa_out_w"].T,
             a["in_proj_w"][:D], a["mha_out_w"].T, f["L1_xattn_We"].T, f["L1_xattn_W2"].T], axis=1)
    cols = np.stack([a["qkv_b"][2 * D:], a["in_proj_b"][D:2 * D], a["in_proj_b"][2 * D:], a["in_proj_b"][:D],
                     a["ln1_g"], a["ln2_g"], a["ln2_b"], r["mu_r"], r["mu_k"]], axis=1)
    bcast = np.stack([a["ln1_g"], a["ln2_g"], a["ln3_g"], a["ln3_b"], a["ln1_b"]])
    brow = np.stack([a["sa_out_b"], a["mha_out_b"], a["lin2_b"], a["ln1_b"], a["ln2_b"]])
    wg = c([m["ws_gate"].reshape(2, I, D), m["w_gate"]])
    wu = c([m["ws_up"].reshape(2, I, D), m["w_up"]])
    gu = np.stack([wg, wu], axis=1).reshape(NU * 2 * I, D).T
    dn = c([m["ws_down"].T.reshape(2, I, D), m["w_down"].transpose(0, 2, 1)]).reshape(NU * I, D)
    arrays = {
        "x": f["x"].reshape(B * S, D), "ctxT": f["ctx_1024"].reshape(B * M, D).T,
        "gates": c([f["g_xattn"], f["g_ffn"]]), "raw": raw, "cols": cols, "l1b": a["lin1_b"].reshape(NF, P).T,
        "bcast": bcast, "brow": brow, "w1": a["lin1_w"].T,
        "w2": a["lin2_w"].T.reshape(NF, P, D).transpose(1, 0, 2).reshape(P, NF * D),
        "gateT": m["gate_weight"].T, "gu": gu, "dn": dn,
        "rw": c([r["W_r"].T, r["W_k"].T, r["W_v"].T], axis=1),
    }
    arrays = {k: np.ascontiguousarray(v) for k, v in arrays.items()}
    nc = bacc.Bacc("TRN2", target_bir_lowering=False, num_devices=1)
    aps = [nc.dram_tensor(k, v.shape, mybir.dt.from_np(v.dtype), kind="ExternalInput").ap()
           for k, v in arrays.items()]
    out = nc.dram_tensor("out", (B * S, D), F32, kind="ExternalOutput").ap()
    build(nc, *aps, out)
    res = run_bass_kernel_spmd(nc, [arrays], core_ids=[0])
    return res.results[0]["out"].reshape(B, S, D)
```
